# Optimizing a Trainium2 kernel written in Bass

```python
import numpy as np
import jax
import jax.numpy as jnp

def _softmax(x, axis=-1):
    return jax.nn.softmax(x, axis=axis)

def _gelu(x):
    return jax.nn.gelu(x, approximate=True)

def _silu(x):
    return jax.nn.silu(x)

def _sigmoid(x):
    return jax.nn.sigmoid(x)

def _layernorm(x, axis=-1, eps=1e-05):
    m = jnp.mean(x, axis=axis, keepdims=True)
    v = jnp.var(x, axis=axis, keepdims=True)
    return (x - m) / jnp.sqrt(v + eps)

def _scatter_add(tgt, idx, src, axis=0):
    return tgt.at[idx].add(src)

def _segment_sum(src, seg, n):
    return jax.ops.segment_sum(src, seg, n)
kernel_name = 'mk_early_fusion_d2_tok_img768_r4_116a20'

def setup_inputs(seed: int=0):
    np.random.seed(seed)
    _w = jnp.asarray

    def _rec_inputs():
        import jax
        import jax.numpy as jnp
        _rk = jax.random.key(seed)
        x = -0.000356955 + 1 * jax.random.normal(jax.random.fold_in(_rk, 1), (8, 3, 96, 96), jnp.float32)
        txt = 0.000273629 + 0.577477 * jax.random.normal(jax.random.fold_in(_rk, 2), (8, 128, 192), jnp.float32)
        return (x, txt)
    x, txt = _rec_inputs()

    def _L0_tok_setup():
        import jax, jax.numpy as jnp
        import numpy as np
        IMAGE_SIZE = 224
        PATCH = 16
        HIDDEN = 192
        C = 3
        key = jax.random.key(seed)
        k1, k2, k3 = jax.random.split(key, 3)
        img = jax.random.normal(k1, (128, C, IMAGE_SIZE, IMAGE_SIZE), dtype=jnp.float32)
        d_in = C * PATCH * PATCH
        bound = 1.0 / np.sqrt(d_in)
        W = jax.random.uniform(k2, (HIDDEN, d_in), jnp.float32, -bound, bound)
        b = jax.random.uniform(k3, (HIDDEN,), jnp.float32, -bound, bound)
        return {'img': img, 'W': W, 'b': b}
    _L0_tok_all = _L0_tok_setup()
    _L0_tok_in = {k: v for k, v in _L0_tok_all.items() if k in ('W', 'b')}
    del _L0_tok_all

    def _L0_attn_setup():
        import jax, jax.numpy as jnp
        import numpy as np
        B, N, DIM, H = (8, 256, 192, 12)
        DH = DIM // H
        LATENT = 32
        EPS = 1e-05

        def _heads(t):
            b, n, _ = t.shape
            return t.reshape(b, n, H, DH).transpose(0, 2, 1, 3).reshape(b * H, n, DH)

        def _merge(t, b):
            _, n, dh = t.shape
            return t.reshape(b, H, n, dh).transpose(0, 2, 1, 3).reshape(b, n, H * dh)

        def _ln(v, g, bta):
            mu = v.mean(-1, keepdims=True)
            var = ((v - mu) ** 2).mean(-1, keepdims=True)
            return (v - mu) * jax.lax.rsqrt(var + EPS) * g + bta

        def _rope(t):
            n, dh = (t.shape[-2], t.shape[-1])
            inv = 1.0 / 10000.0 ** (jnp.arange(0, dh, 2, dtype=jnp.float32) / dh)
            f = jnp.arange(n, dtype=jnp.float32)[:, None] * inv[None, :]
            f = jnp.concatenate([f, f], -1)[None]
            x1, x2 = jnp.split(t, 2, -1)
            rot = jnp.concatenate([-x2, x1], -1)
            return t * jnp.cos(f) + rot * jnp.sin(f)
        key = jax.random.key(seed)
        ks = jax.random.split(key, 6)
        s = 0.02
        return {'x': jax.random.normal(ks[0], (B, N, DIM), jnp.float32), 'Wq': jax.random.normal(ks[1], (DIM, DIM), jnp.float32) * s, 'Wkv': jax.random.normal(ks[2], (DIM, DIM), jnp.float32) * s, 'Wo_ctx': jax.random.normal(ks[3], (DIM, DIM), jnp.float32) * s, 'bo_ctx': jnp.zeros((DIM,), jnp.float32), 'Wo_lat': jax.random.normal(ks[4], (DIM, DIM), jnp.float32) * s, 'bo_lat': jnp.zeros((DIM,), jnp.float32), 'ln_g': jnp.ones((DH,), jnp.float32), 'ln_b': jnp.zeros((DH,), jnp.float32)}
    _L0_attn_all = _L0_attn_setup()
    _L0_attn_in = {k: v for k, v in _L0_attn_all.items() if k in ('Wq', 'Wkv', 'Wo_ctx', 'bo_ctx', 'Wo_lat', 'bo_lat', 'ln_g', 'ln_b')}
    del _L0_attn_all

    def _L0_ffn_setup():
        import jax, jax.numpy as jnp
        import numpy as np
        B, S, D_IN, D_HID, D_OUT = (32, 128, 192, 768, 192)
        key = jax.random.key(seed)
        k1, k2, k3, k4 = jax.random.split(key, 4)
        init_k = float(np.sqrt(1.0 / D_IN))
        init_k2 = float(np.sqrt(1.0 / D_HID))
        x = jax.random.normal(k1, (B, S, D_IN), dtype=jnp.float32)
        in_weight = jax.random.uniform(k2, (D_HID, D_IN), dtype=jnp.float32, minval=-init_k, maxval=init_k)
        in_bias = jax.random.uniform(k3, (D_HID,), dtype=jnp.float32, minval=-init_k, maxval=init_k)
        out_weight = jax.random.uniform(k4, (D_HID, D_OUT), dtype=jnp.float32, minval=-init_k2, maxval=init_k2)
        return {'x': x, 'in_weight': in_weight, 'in_bias': in_bias, 'out_weight': out_weight}
    _L0_ffn_all = _L0_ffn_setup()
    _L0_ffn_in = {k: v for k, v in _L0_ffn_all.items() if k in ('in_weight', 'in_bias', 'out_weight')}
    del _L0_ffn_all

    def _L1_attn_setup():
        import jax, jax.numpy as jnp
        import numpy as np
        D_MODEL = 192
        N_LAYER = 4
        D_INNER = 2 * D_MODEL
        D_STATE = 16
        D_CONV = 4
        DT_RANK = (D_MODEL + 15) // 16
        EPS = 1e-05

        def _ln(x, w, b):
            mu = jnp.mean(x, axis=-1, keepdims=True)
            var = jnp.mean(jnp.square(x - mu), axis=-1, keepdims=True)
            return (x - mu) * jax.lax.rsqrt(var + EPS) * w + b

        def _mixer(u, p):
            B, L, _ = u.shape
            xz = jnp.einsum('bld,ed->ble', u, p['in_proj_w'])
            x, z = jnp.split(xz, 2, axis=-1)
            xp = jnp.pad(x, ((0, 0), (D_CONV - 1, 0), (0, 0)))
            x = sum((p['conv_w'][:, k] * xp[:, k:k + L, :] for k in range(D_CONV))) + p['conv_b']
            x = jax.nn.silu(x)
            x_dbl = jnp.einsum('bld,ed->ble', x, p['x_proj_w'])
            dt, Bm, Cm = jnp.split(x_dbl, [DT_RANK, DT_RANK + D_STATE], axis=-1)
            dt = jax.nn.softplus(jnp.einsum('blr,dr->bld', dt, p['dt_proj_w']) + p['dt_proj_b'])
            A = -jnp.exp(p['A_log'])

            def step(h, xs):
                dt_t, B_t, C_t, x_t = xs
                dA = jnp.exp(dt_t[:, :, None] * A)
                h = dA * h + (dt_t * x_t)[:, :, None] * B_t[:, None, :]
                y = jnp.einsum('bds,bs->bd', h, C_t)
                return (h, y)
            h0 = jnp.zeros((B, D_INNER, D_STATE), x.dtype)
            xs = (dt.transpose(1, 0, 2), Bm.transpose(1, 0, 2), Cm.transpose(1, 0, 2), x.transpose(1, 0, 2))
            _, ys = jax.lax.scan(step, h0, xs)
            y = ys.transpose(1, 0, 2) + x * p['D_skip']
            y = y * jax.nn.silu(z)
            return jnp.einsum('bld,ed->ble', y, p['out_proj_w'])
        key = jax.random.key(seed)
        ks = jax.random.split(key, 8)
        s = 0.02
        n, dm, di = (N_LAYER, D_MODEL, D_INNER)
        return {'embeddings': jax.random.normal(ks[0], (2, 256, dm), jnp.float32), 'norm_w': jnp.ones((n, dm), jnp.float32), 'norm_b': jnp.zeros((n, dm), jnp.float32), 'in_proj_w': jax.random.normal(ks[1], (n, 2 * di, dm), jnp.float32) * s, 'conv_w': jax.random.normal(ks[2], (n, di, D_CONV), jnp.float32) * s, 'conv_b': jnp.zeros((n, di), jnp.float32), 'x_proj_w': jax.random.normal(ks[3], (n, DT_RANK + 2 * D_STATE, di), jnp.float32) * s, 'dt_proj_w': jax.random.normal(ks[4], (n, di, DT_RANK), jnp.float32) * s, 'dt_proj_b': jnp.full((n, di), float(np.log(np.expm1(0.01))), jnp.float32), 'A_log': jnp.broadcast_to(jnp.log(jnp.arange(1, D_STATE + 1, dtype=jnp.float32)), (n, di, D_STATE)) + jnp.zeros((n, di, D_STATE), jnp.float32), 'D_skip': jnp.ones((n, di), jnp.float32), 'out_proj_w': jax.random.normal(ks[5], (n, dm, di), jnp.float32) * s, 'norm_f_w': jnp.ones((dm,), jnp.float32), 'norm_f_b': jnp.zeros((dm,), jnp.float32)}
    _L1_attn_all = _L1_attn_setup()
    _L1_attn_in = {k: v for k, v in _L1_attn_all.items() if k in ('norm_w', 'norm_b', 'in_proj_w', 'conv_w', 'conv_b', 'x_proj_w', 'dt_proj_w', 'dt_proj_b', 'A_log', 'D_skip', 'out_proj_w', 'norm_f_w', 'norm_f_b')}
    del _L1_attn_all

    def _L1_ffn_setup():
        import math
        import jax, jax.numpy as jnp
        import numpy as np
        EMBED_CHOICES = [96, 144, 192]
        RATIO_CHOICES = [2, 3, 4]
        E_MAX = 192
        H_MAX = 768

        def new_gelu(x):
            c = math.sqrt(2.0 / math.pi)
            return 0.5 * x * (1.0 + jnp.tanh(c * (x + 0.044715 * x * x * x)))

        def _mixed_coeffs(alpha_e, alpha_r):
            h_idx = jnp.arange(H_MAX)
            d_idx = jnp.arange(E_MAX)
            C0 = jnp.zeros((H_MAX, E_MAX), jnp.float32)
            c0b = jnp.zeros((H_MAX,), jnp.float32)
            C1 = jnp.zeros((E_MAX, H_MAX), jnp.float32)
            c1b = jnp.zeros((E_MAX,), jnp.float32)
            for i, e in enumerate(EMBED_CHOICES):
                m_in = (d_idx < e).astype(jnp.float32)
                for j, r in enumerate(RATIO_CHOICES):
                    a = alpha_e[i] * alpha_r[j]
                    m_out = (h_idx < r * e).astype(jnp.float32)
                    C0 = C0 + a * (m_out[:, None] * m_in[None, :])
                    c0b = c0b + a * m_out
                    C1 = C1 + a * (m_in[:, None] * m_out[None, :])
                    c1b = c1b + a * m_in
            return (C0, c0b, C1, c1b)
        key = jax.random.key(seed)
        ks = jax.random.split(key, 6)
        x = jax.random.normal(ks[0], (8, 512, E_MAX), jnp.float32)
        w_fc = jax.random.normal(ks[1], (H_MAX, E_MAX), jnp.float32) * 0.02
        b_fc = jnp.zeros((H_MAX,), jnp.float32)
        w_proj = jax.random.normal(ks[2], (E_MAX, H_MAX), jnp.float32) * 0.02
        b_proj = jnp.zeros((E_MAX,), jnp.float32)
        alpha_e = jax.nn.softmax(jax.random.normal(ks[3], (3,), jnp.float32))
        alpha_r = jax.nn.softmax(jax.random.normal(ks[4], (3,), jnp.float32))
        return {'x': x, 'w_fc': w_fc, 'b_fc': b_fc, 'w_proj': w_proj, 'b_proj': b_proj, 'alpha_e': alpha_e, 'alpha_r': alpha_r}
    _L1_ffn_all = _L1_ffn_setup()
    _L1_ffn_in = {k: v for k, v in _L1_ffn_all.items() if k in ('w_fc', 'b_fc', 'w_proj', 'b_proj', 'alpha_e', 'alpha_r')}
    del _L1_ffn_all
    return {'x': x, 'txt': txt, 'L0_tok_W': _L0_tok_in['W'], 'L0_tok_b': _L0_tok_in['b'], 'L0_attn_Wq': _L0_attn_in['Wq'], 'L0_attn_Wkv': _L0_attn_in['Wkv'], 'L0_attn_Wo_ctx': _L0_attn_in['Wo_ctx'], 'L0_attn_bo_ctx': _L0_attn_in['bo_ctx'], 'L0_attn_Wo_lat': _L0_attn_in['Wo_lat'], 'L0_attn_bo_lat': _L0_attn_in['bo_lat'], 'L0_attn_ln_g': _L0_attn_in['ln_g'], 'L0_attn_ln_b': _L0_attn_in['ln_b'], 'L0_ffn_in_weight': _L0_ffn_in['in_weight'], 'L0_ffn_in_bias': _L0_ffn_in['in_bias'], 'L0_ffn_out_weight': _L0_ffn_in['out_weight'], 'L1_attn_norm_w': _L1_attn_in['norm_w'], 'L1_attn_norm_b': _L1_attn_in['norm_b'], 'L1_attn_in_proj_w': _L1_attn_in['in_proj_w'], 'L1_attn_conv_w': _L1_attn_in['conv_w'], 'L1_attn_conv_b': _L1_attn_in['conv_b'], 'L1_attn_x_proj_w': _L1_attn_in['x_proj_w'], 'L1_attn_dt_proj_w': _L1_attn_in['dt_proj_w'], 'L1_attn_dt_proj_b': _L1_attn_in['dt_proj_b'], 'L1_attn_A_log': _L1_attn_in['A_log'], 'L1_attn_D_skip': _L1_attn_in['D_skip'], 'L1_attn_out_proj_w': _L1_attn_in['out_proj_w'], 'L1_attn_norm_f_w': _L1_attn_in['norm_f_w'], 'L1_attn_norm_f_b': _L1_attn_in['norm_f_b'], 'L1_ffn_w_fc': _L1_ffn_in['w_fc'], 'L1_ffn_b_fc': _L1_ffn_in['b_fc'], 'L1_ffn_w_proj': _L1_ffn_in['w_proj'], 'L1_ffn_b_proj': _L1_ffn_in['b_proj'], 'L1_ffn_alpha_e': _L1_ffn_in['alpha_e'], 'L1_ffn_alpha_r': _L1_ffn_in['alpha_r']}

def reference(x, txt, L0_tok_W, L0_tok_b, L0_attn_Wq, L0_attn_Wkv, L0_attn_Wo_ctx, L0_attn_bo_ctx, L0_attn_Wo_lat, L0_attn_bo_lat, L0_attn_ln_g, L0_attn_ln_b, L0_ffn_in_weight, L0_ffn_in_bias, L0_ffn_out_weight, L1_attn_norm_w, L1_attn_norm_b, L1_attn_in_proj_w, L1_attn_conv_w, L1_attn_conv_b, L1_attn_x_proj_w, L1_attn_dt_proj_w, L1_attn_dt_proj_b, L1_attn_A_log, L1_attn_D_skip, L1_attn_out_proj_w, L1_attn_norm_f_w, L1_attn_norm_f_b, L1_ffn_w_fc, L1_ffn_b_fc, L1_ffn_w_proj, L1_ffn_b_proj, L1_ffn_alpha_e, L1_ffn_alpha_r):
    import jax
    import jax.numpy as jnp

    def _L0_tok_ref(img, W, b):
        import jax, jax.numpy as jnp
        import numpy as np
        IMAGE_SIZE = 224
        PATCH = 16
        HIDDEN = 192
        C = 3
        B, Cc, H, Wd = img.shape
        hp, wp = (H // PATCH, W // PATCH if False else Wd // PATCH)
        hp = H // PATCH
        x = img.reshape(B, Cc, hp, PATCH, wp, PATCH)
        x = x.transpose(0, 2, 4, 1, 3, 5)
        x = x.reshape(B, hp * wp, Cc * PATCH * PATCH)
        return jnp.einsum('bld,hd->blh', x, W) + b

    def _L0_attn_ref(x, Wq, Wkv, Wo_ctx, bo_ctx, Wo_lat, bo_lat, ln_g, ln_b):
        import jax, jax.numpy as jnp
        import numpy as np
        B, N, DIM, H = (8, 256, 192, 12)
        DH = DIM // H
        LATENT = 32
        EPS = 1e-05

        def _heads(t):
            b, n, _ = t.shape
            return t.reshape(b, n, H, DH).transpose(0, 2, 1, 3).reshape(b * H, n, DH)

        def _merge(t, b):
            _, n, dh = t.shape
            return t.reshape(b, H, n, dh).transpose(0, 2, 1, 3).reshape(b, n, H * dh)

        def _ln(v, g, bta):
            mu = v.mean(-1, keepdims=True)
            var = ((v - mu) ** 2).mean(-1, keepdims=True)
            return (v - mu) * jax.lax.rsqrt(var + EPS) * g + bta

        def _rope(t):
            n, dh = (t.shape[-2], t.shape[-1])
            inv = 1.0 / 10000.0 ** (jnp.arange(0, dh, 2, dtype=jnp.float32) / dh)
            f = jnp.arange(n, dtype=jnp.float32)[:, None] * inv[None, :]
            f = jnp.concatenate([f, f], -1)[None]
            x1, x2 = jnp.split(t, 2, -1)
            rot = jnp.concatenate([-x2, x1], -1)
            return t * jnp.cos(f) + rot * jnp.sin(f)
        b, n, _ = x.shape
        ctx = n - LATENT
        q = _heads(x @ Wq)
        kv = _heads(x @ Wkv)
        q = _rope(q)
        kv = _rope(kv)
        q = q * DH ** (-0.5)
        q_lat, q_ctx = (q[:, ctx:], q[:, :ctx])
        kv_ctx = kv[:, :ctx]
        lkv = _ln(kv, ln_g, ln_b)
        lkv_ctx = _ln(kv_ctx, ln_g, ln_b)
        attn_lat = jax.nn.softmax(jnp.einsum('bid,bkd->bik', q_lat, kv), axis=-1)
        attn_ctx = jax.nn.softmax(jnp.einsum('bid,bkd->bik', q_ctx, kv_ctx), axis=-1)
        out_lat = _merge(jnp.einsum('bik,bkd->bid', attn_lat, lkv), b) @ Wo_lat + bo_lat
        out_ctx = _merge(jnp.einsum('bik,bkd->bid', attn_ctx, lkv_ctx), b) @ Wo_ctx + bo_ctx
        return jnp.concatenate([out_ctx, out_lat], axis=1)

    def _L0_ffn_ref(x, in_weight, in_bias, out_weight):
        import jax, jax.numpy as jnp
        import numpy as np
        B, S, D_IN, D_HID, D_OUT = (32, 128, 192, 768, 192)
        lead = x.shape[:-1]
        xt = x.reshape(-1, in_weight.shape[1])
        h = jax.nn.gelu(jnp.einsum('td,hd->th', xt, in_weight) + in_bias, approximate=False)
        out = jnp.einsum('th,ho->to', h, out_weight)
        return out.reshape(*lead, out_weight.shape[1])

    def _L1_attn_ref(embeddings, norm_w, norm_b, in_proj_w, conv_w, conv_b, x_proj_w, dt_proj_w, dt_proj_b, A_log, D_skip, out_proj_w, norm_f_w, norm_f_b):
        import jax, jax.numpy as jnp
        import numpy as np
        D_MODEL = 192
        N_LAYER = 4
        D_INNER = 2 * D_MODEL
        D_STATE = 16
        D_CONV = 4
        DT_RANK = (D_MODEL + 15) // 16
        EPS = 1e-05

        def _ln(x, w, b):
            mu = jnp.mean(x, axis=-1, keepdims=True)
            var = jnp.mean(jnp.square(x - mu), axis=-1, keepdims=True)
            return (x - mu) * jax.lax.rsqrt(var + EPS) * w + b

        def _mixer(u, p):
            B, L, _ = u.shape
            xz = jnp.einsum('bld,ed->ble', u, p['in_proj_w'])
            x, z = jnp.split(xz, 2, axis=-1)
            xp = jnp.pad(x, ((0, 0), (D_CONV - 1, 0), (0, 0)))
            x = sum((p['conv_w'][:, k] * xp[:, k:k + L, :] for k in range(D_CONV))) + p['conv_b']
            x = jax.nn.silu(x)
            x_dbl = jnp.einsum('bld,ed->ble', x, p['x_proj_w'])
            dt, Bm, Cm = jnp.split(x_dbl, [DT_RANK, DT_RANK + D_STATE], axis=-1)
            dt = jax.nn.softplus(jnp.einsum('blr,dr->bld', dt, p['dt_proj_w']) + p['dt_proj_b'])
            A = -jnp.exp(p['A_log'])

            def step(h, xs):
                dt_t, B_t, C_t, x_t = xs
                dA = jnp.exp(dt_t[:, :, None] * A)
                h = dA * h + (dt_t * x_t)[:, :, None] * B_t[:, None, :]
                y = jnp.einsum('bds,bs->bd', h, C_t)
                return (h, y)
            h0 = jnp.zeros((B, D_INNER, D_STATE), x.dtype)
            xs = (dt.transpose(1, 0, 2), Bm.transpose(1, 0, 2), Cm.transpose(1, 0, 2), x.transpose(1, 0, 2))
            _, ys = jax.lax.scan(step, h0, xs)
            y = ys.transpose(1, 0, 2) + x * p['D_skip']
            y = y * jax.nn.silu(z)
            return jnp.einsum('bld,ed->ble', y, p['out_proj_w'])
        params = dict(norm_w=norm_w, norm_b=norm_b, in_proj_w=in_proj_w, conv_w=conv_w, conv_b=conv_b, x_proj_w=x_proj_w, dt_proj_w=dt_proj_w, dt_proj_b=dt_proj_b, A_log=A_log, D_skip=D_skip, out_proj_w=out_proj_w)

        def layer_step(carry, p):
            hidden, residual = carry
            residual = hidden + residual
            h = _ln(residual, p['norm_w'], p['norm_b'])
            h = _mixer(h, p)
            return ((h, residual), None)
        carry = (embeddings, jnp.zeros_like(embeddings))
        (hidden, residual), _ = jax.lax.scan(layer_step, carry, params)
        residual = hidden + residual
        return _ln(residual, norm_f_w, norm_f_b)

    def _L1_ffn_ref(x, w_fc, b_fc, w_proj, b_proj, alpha_e, alpha_r):
        import math
        import jax, jax.numpy as jnp
        import numpy as np
        EMBED_CHOICES = [96, 144, 192]
        RATIO_CHOICES = [2, 3, 4]
        E_MAX = 192
        H_MAX = 768

        def new_gelu(x):
            c = math.sqrt(2.0 / math.pi)
            return 0.5 * x * (1.0 + jnp.tanh(c * (x + 0.044715 * x * x * x)))

        def _mixed_coeffs(alpha_e, alpha_r):
            h_idx = jnp.arange(H_MAX)
            d_idx = jnp.arange(E_MAX)
            C0 = jnp.zeros((H_MAX, E_MAX), jnp.float32)
            c0b = jnp.zeros((H_MAX,), jnp.float32)
            C1 = jnp.zeros((E_MAX, H_MAX), jnp.float32)
            c1b = jnp.zeros((E_MAX,), jnp.float32)
            for i, e in enumerate(EMBED_CHOICES):
                m_in = (d_idx < e).astype(jnp.float32)
                for j, r in enumerate(RATIO_CHOICES):
                    a = alpha_e[i] * alpha_r[j]
                    m_out = (h_idx < r * e).astype(jnp.float32)
                    C0 = C0 + a * (m_out[:, None] * m_in[None, :])
                    c0b = c0b + a * m_out
                    C1 = C1 + a * (m_in[:, None] * m_out[None, :])
                    c1b = c1b + a * m_in
            return (C0, c0b, C1, c1b)
        C0, c0b, C1, c1b = _mixed_coeffs(alpha_e, alpha_r)
        W0 = w_fc * C0
        b0 = b_fc * c0b
        h = jnp.einsum('bte,he->bth', x, W0) + b0
        h = new_gelu(h)
        W1 = w_proj * C1
        b1 = b_proj * c1b
        out = jnp.einsum('bth,eh->bte', h, W1) + b1
        return out
    h = _L0_tok_ref(x, L0_tok_W, L0_tok_b)
    h = jnp.concatenate([h, txt], axis=1)
    h = h + _L0_attn_ref(_layernorm(h, axis=-1), L0_attn_Wq, L0_attn_Wkv, L0_attn_Wo_ctx, L0_attn_bo_ctx, L0_attn_Wo_lat, L0_attn_bo_lat, L0_attn_ln_g, L0_attn_ln_b)
    h = h + _L0_ffn_ref(_layernorm(h, axis=-1), L0_ffn_in_weight, L0_ffn_in_bias, L0_ffn_out_weight)
    h = h + _L1_attn_ref(_layernorm(h, axis=-1), L1_attn_norm_w, L1_attn_norm_b, L1_attn_in_proj_w, L1_attn_conv_w, L1_attn_conv_b, L1_attn_x_proj_w, L1_attn_dt_proj_w, L1_attn_dt_proj_b, L1_attn_A_log, L1_attn_D_skip, L1_attn_out_proj_w, L1_attn_norm_f_w, L1_attn_norm_f_b)
    h = h + _L1_ffn_ref(_layernorm(h, axis=-1), L1_ffn_w_fc, L1_ffn_b_fc, L1_ffn_w_proj, L1_ffn_b_proj, L1_ffn_alpha_e, L1_ffn_alpha_r)
    return h

_drawn_inputs = setup_inputs


def setup_inputs(seed=0):
    import zlib

    import numpy as np

    out = dict(_drawn_inputs(seed))
    spreads = {'L0_attn_bo_ctx': (0.0, 0.1),
     'L0_attn_bo_lat': (0.0, 0.1),
     'L0_attn_ln_g': (1.0, 0.6),
     'L0_attn_ln_b': (0.0, 0.1),
     'L1_attn_norm_w': (1.0, 0.6),
     'L1_attn_norm_b': (0.0, 0.8),
     'L1_attn_conv_b': (0.0, 0.8),
     'L1_attn_dt_proj_b': (-4.600165843963623, 0.6),
     'L1_attn_D_skip': (1.0, 0.6),
     'L1_attn_norm_f_w': (1.0, 0.2),
     'L1_attn_norm_f_b': (0.0, 0.27),
     'L1_ffn_b_fc': (0.0, 0.655),
     'L1_ffn_b_proj': (0.0, 0.1)}
    factors = {'L0_tok_b': 3.225,
     'L0_attn_Wq': 5.058,
     'L1_attn_in_proj_w': 8.0,
     'L1_attn_conv_w': 8.0,
     'L1_attn_x_proj_w': 8.0,
     'L1_attn_dt_proj_w': 8.0,
     'L1_attn_A_log': 8.0,
     'L1_attn_out_proj_w': 8.0,
     'L1_ffn_alpha_r': 7.514}
    for name, (base, spread) in spreads.items():
        noise = np.random.default_rng([zlib.crc32(name.encode()), seed]).standard_normal(out[name].shape)
        drawn = base * np.exp(spread * noise) if base else spread * noise
        out[name] = jnp.asarray(drawn.astype(out[name].dtype))
    for name, factor in factors.items():
        out[name] = (out[name] * factor).astype(out[name].dtype)
    return out
```

```python
from contextlib import ExitStack

import concourse.bass as bass
from concourse import mybir

F32 = mybir.dt.float32
BF16 = mybir.dt.bfloat16
ALU = mybir.AluOpType
ACT = mybir.ActivationFunctionType
AX = mybir.AxisListType

B = 8
IMG, TXT = 36, 128
L = IMG + TXT
HL = L // 2
NT = 2 * B
D = 192
DH2 = D // 2
PK = 768 // 128
H, DH = 12, 16
LAT = 32
CTX = L - LAT
HC, HR = 3, 4
HID = 768
HM = HID // 128
EPS = 1e-5
NL = 4
DI = 384
NC = DI // 128
NS = 16
TAPS = 4
RANK = 12
GB = 2
NG = B // GB
GT = 2 * GB
W = GB * L
UNITS = NL * NG
STEPS = NC * NS
P_A, P_D = 0, NC * NS
P_F = P_D + NC
P_CW, P_CB = 0, NC * TAPS
P_DTB = P_CB + NC
P_NW = P_DTB + NC
P_NB = P_NW + 2
NPF = P_NB + 2
NPACK = P_F + NPF


class Steps:

    def __init__(self, sem, names):
        self.sem = sem
        self.order = {name: k + 1 for k, name in enumerate(names)}
        assert len(self.order) == len(names)
        self.said = 0

    def next(self, name):
        assert self.order[name] == self.said % len(self.order) + 1, name
        self.said += 1
        return self.sem

    def at(self, turn, name):
        value = turn * len(self.order) + self.order[name]
        return max(value, 0) if isinstance(value, int) else value


def turns(eng, n, body):
    body(0, True, n == 1)
    if n > 2:
        with eng.Fori(1, n - 1) as turn:
            body(turn, False, False)
    if n > 1:
        body(n - 1, False, True)


def build(nc, a, out):
    with ExitStack() as ctx:
        def sb(name, shape, dt=F32, where=ctx):
            return where.enter_context(nc.sbuf_tensor(name, shape, dt))

        def sem(name):
            return ctx.enter_context(nc.semaphore(name))

        bank0 = ctx.enter_context(nc.psum_tensor("bank0", [128, 512], F32))
        two = ctx.enter_context(nc.psum_tensor("bank12", [128, 1024], F32))
        bank3 = ctx.enter_context(nc.psum_tensor("bank3", [128, 512], F32))
        pair = [ctx.enter_context(nc.psum_tensor(f"pair{k}", [128, 2, 512], F32)) for k in range(2)]
        bank = [bank0[:, :], two[:, 0:512], two[:, 512:1024], bank3[:, :]] + [pair[0][:, 0, :], pair[0][:, 1, :], pair[1][:, 0, :], pair[1][:, 1, :]]

        h = sb("h", [HL, NT, D])
        res = sb("res", [HL, NT, D])
        ident = sb("ident", [128, 128])
        ones = sb("ones", [1, HL])
        eps = sb("eps", [128, 1])
        s_base = sem("s_base")
        embed(nc, a, sb, sem, bank, h, ident, ones, eps, s_base)
        attention(nc, a, sb, sem, bank, h, ident, eps)
        mlp(nc, a, sb, sem, bank, pair, h, ident, ones, eps, 1, None)
        normalise(nc, a, sb, sem, h, res, eps, False)
        mamba(nc, a, sb, sem, bank, two, pair, res, ident, eps)
        normalise(nc, a, sb, sem, res, h, eps, True)
        mlp(nc, a, sb, sem, bank, pair, h, ident, ones, eps, 2, out)


def embed(nc, a, sb, sem, bank, h, ident, ones, eps, s_base):
    with ExitStack() as ctx, nc.Block() as block:
        patches = sb("patches", [128, PK, B * IMG], where=ctx)
        tok_w = sb("tok_w", [128, PK, D], where=ctx)
        tok_b = sb("tok_b", [1, D], where=ctx)
        s_load = sem("s_patches")
        s_txt = sem("s_txt")
        s_const = sem("s_const")
        s_img = sem("s_img")
        s_copied = sem("s_img_copied")

        @block.sync
        def _(sp):
            sp.dma_start(patches[:], a["patches"]).then_inc(s_load, 16)
            sp.dma_start(tok_w[:], a["tok_w"]).then_inc(s_load, 16)
            sp.dma_start(tok_b[:], a["tok_b"]).then_inc(s_load, 16)
            sp.dma_start(ident[:], a["ident"]).then_inc(s_base, 16)
            sp.dma_start(h[IMG:HL, 0:NT:2, :], a["txt"][:, 0:HL - IMG, :].rearrange("b t d -> t b d")).then_inc(s_txt, 16)
            sp.dma_start(h[:, 1:NT:2, :], a["txt"][:, HL - IMG:TXT, :].rearrange("b t d -> t b d")).then_inc(s_txt, 16)
            sp.wait_ge(s_txt, 32)
            sp.wait_ge(s_base, 16)

        @block.gpsimd
        def _(pool):
            pool.memset(ones[:], 1.0).then_inc(s_const, 1)
            pool.memset(eps[:], EPS).then_inc(s_const, 1)

        @block.tensor
        def _(pe):
            pe.wait_ge(s_load, 48)
            pe.wait_ge(s_const, 2)
            for b in range(B):
                o = bank[b // 2][0:IMG, (b % 2) * D:(b % 2 + 1) * D]
                for k in range(PK):
                    pe.matmul(o, patches[:, k, b * IMG:(b + 1) * IMG], tok_w[:, k, :], start=(k == 0), stop=False)
                pe.matmul(o, ones[:, 0:IMG], tok_b[:], start=False, stop=True).then_inc(s_img, 1)

        @block.vector
        def _(dve):
            for n in range(B // 2):
                dve.wait_ge(s_img, 2 * n + 2)
                for k in range(2):
                    dve.tensor_copy(h[0:IMG, 2 * (2 * n + k), :], bank[n][0:IMG, k * D:(k + 1) * D]).then_inc(s_copied, 1)


def attention(nc, a, sb, sem, bank, h, ident, eps):
    with ExitStack() as ctx, nc.Block() as block:
        w_qkv = sb("w_qkv", [DH2, 2, 2 * D], where=ctx)
        w_ctx = sb("w_ctx", [DH2, 2, D], where=ctx)
        w_lat = sb("w_lat", [DH2, 2, D], where=ctx)
        b_out = sb("b_out", [2, D], where=ctx)
        kind = sb("kind", [2, L], where=ctx)
        rope = sb("rope", [HL, 2, 2, 2 * D], where=ctx)
        gain = sb("gain", [HL, DH], where=ctx)
        shift = sb("shift", [HL, DH], where=ctx)
        stats = sb("a_stats", [HL, 2, 6], where=ctx)
        mv = sb("a_mv", [HL, 2, 2], where=ctx)
        lv = sb("a_lv", [HL, 2], where=ctx)
        spare = sb("a_spare", [HL, 1], where=ctx)
        rstd = sb("a_rstd", [HL, 2], where=ctx)
        xn = sb("a_xn", [HL, 2, D], where=ctx)
        xt = sb("a_xt", [DH2, 2, L], where=ctx)
        t_cos = sb("t_cos", [HL, 2, 2 * D], where=ctx)
        t_sin = sb("t_sin", [HL, 2, 2 * D], where=ctx)
        qk = sb("qk", [HL, 2, 2 * H, 32], where=ctx)
        qt = sb("qt", [128, HC, L], where=ctx)
        kt = sb("kt", [128, HC, L], where=ctx)
        mu = sb("k_mu", [HL, 2, H], where=ctx)
        var = sb("k_var", [HL, 2, H], where=ctx)
        klv = sb("k_lv", [HL, 2, H], where=ctx)
        krs = sb("k_rs", [HL, 2, H], where=ctx)
        kc = sb("k_c", [HL, 2, H, DH], where=ctx)
        ksq = sb("k_sq", [HL, 2, H, DH], where=ctx)
        v = sb("v", [HL, 2, H, DH + 1], where=ctx)
        pt = sb("pt", [HL, 2, HR, HC * L], where=ctx)
        rsum = sb("rsum", [HL, 2, H, 1], where=ctx)
        o = sb("o", [HL, 2, H, DH], where=ctx)
        ot_ctx = sb("ot_ctx", [DH2, 2, L], where=ctx)
        ot_lat = sb("ot_lat", [DH2, 2, L], where=ctx)

        s_load = sem("s_attn_load")
        s_zero = sem("s_attn_zero")
        dve_a = Steps(sem("dve_project"), ["aggr", "xn", "cos0", "sin0", "rope0", "cos1", "sin1", "rope1", "ksum", "kmu", "kvar"])
        act_a = Steps(sem("act_project"), ["lv", "rstd", "xt", "qt", "kt", "klv", "krs"])
        pe_a = Steps(sem("pe_project"), ["xt", "qkv0", "qkv1", "qt", "kt"])
        pool_a = Steps(sem("pool_project"), ["kc", "ksq", "kn", "kg", "v"])
        s_stats = sem("dve_attn_stats")
        dve_c = Steps(sem("dve_attend"), [f"max{n}" for n in range(8)] + ["recip", "o", "add"])
        act_c = Steps(sem("act_attend"), ["qt"] + [f"exp{n}" for n in range(8)] + ["ot"])
        pe_c = Steps(sem("pe_attend"), [f"s{n}" for n in range(8)] + ["qt"] + [f"p{n}" for n in range(8)] + ["pv", "ot", "out"])
        n_loads = 9

        @block.sync
        def _(sp):
            for dst, name in ((w_qkv, "w_qkv"), (rope, "rope"), (qk, "qk_pad"), (w_ctx, "w_ctx"), (w_lat, "w_lat"),
                              (b_out, "b_out"), (kind, "kind")):
                sp.dma_start(dst[:], a[name]).then_inc(s_load, 16)
            sp.dma_start(gain[:], a["ln_g"].partition_broadcast(HL)).then_inc(s_load, 16)
            sp.dma_start(shift[:], a["ln_b"].partition_broadcast(HL)).then_inc(s_load, 16)

        @block.vector
        def _(dve):
            def stats_of(b):
                for j in range(2):
                    last = dve.bn_stats(stats[:, j, :], h[:, 2 * b + j, :])
                last.then_inc(s_stats, 1)
                dve.wait_ge(s_stats, 1 * b + 1)
                dve.wait_ge(act_a.sem, act_a.at(b - 1, "rstd"))
                dve.memset(spare[:], 0.0)
                for j in range(2):
                    last = dve.bn_aggr(mv[:, j, :], stats[:, j, :])
                last.then_inc(dve_a.next("aggr"), 1)

            def normalised(b):
                dve.wait_ge(act_a.sem, act_a.at(b, "rstd"))
                dve.wait_ge(pe_a.sem, pe_a.at(b - 1, "xt"))
                for j in range(2):
                    last = dve.tensor_scalar(xn[:, j, :], h[:, 2 * b + j, :], mv[:, j, 0:1], rstd[:, j:j + 1], ALU.subtract, ALU.mult)
                last.then_inc(dve_a.next("xn"), 1)

            def rotate(b):
                for j in range(2):
                    src = bank[5 - j][0:HL, 0:2 * D]
                    dve.wait_ge(pe_a.sem, pe_a.at(b, f"qkv{j}"))
                    dve.tensor_tensor(t_cos[:, j, :], src, rope[:, 0, j, :], ALU.mult).then_inc(dve_a.next(f"cos{j}"), 1)
                    half = "p (h u e) -> p h u e"
                    x = src.rearrange(half, u=2, e=DH // 2)
                    s = rope[:, 1, j, :].rearrange(half, u=2, e=DH // 2)
                    y = t_sin[:, j, :].rearrange(half, u=2, e=DH // 2)
                    dve.tensor_tensor(y[:, :, 0, :], x[:, :, 1, :], s[:, :, 0, :], ALU.mult)
                    dve.tensor_tensor(y[:, :, 1, :], x[:, :, 0, :], s[:, :, 1, :], ALU.mult).then_inc(dve_a.next(f"sin{j}"), 1)
                    dve.wait_ge(dve_a.sem, dve_a.at(b, f"sin{j}"))
                    dve.wait_ge(pe_c.sem, pe_c.at(b - 1, "qt"))
                    if j == 0:
                        dve.wait_ge(pool_a.sem, pool_a.at(b - 1, "kc"))
                    dve.tensor_tensor(qk[:, j, :, 0:DH], t_cos[:, j, :].rearrange("p (h e) -> p h e", e=DH),
                                                 t_sin[:, j, :].rearrange("p (h e) -> p h e", e=DH), ALU.add).then_inc(dve_a.next(f"rope{j}"), 1)
                dve.wait_ge(dve_a.sem, dve_a.at(b, "rope1"))
                dve.wait_ge(pool_a.sem, pool_a.at(b - 1, "kc"))
                dve.tensor_reduce(mu[:], qk[:, :, H:2 * H, 0:DH], AX.X, ALU.add).then_inc(dve_a.next("ksum"), 1)
                dve.wait_ge(dve_a.sem, dve_a.at(b, "ksum"))
                dve.tensor_scalar(mu[:], mu[:], 1.0 / DH, None, ALU.mult).then_inc(dve_a.next("kmu"), 1)

            def variance(b):
                dve.wait_ge(pool_a.sem, pool_a.at(b, "ksq"))
                dve.wait_ge(act_a.sem, act_a.at(b - 1, "klv"))
                dve.tensor_reduce(var[:], ksq[:], AX.X, ALU.add).then_inc(dve_a.next("kvar"), 1)

            def maxima(b):
                for n in range(8):
                    j, r = divmod(n, HR)
                    dve.wait_ge(pe_c.sem, pe_c.at(b, f"s{n}"))
                    dve.tensor_reduce(qk[:, j, r:H:HR, DH + 1], bank[n % 4][0:HL, 0:HC * L].rearrange("p (c k) -> p c k", c=HC),
                                                 AX.X, ALU.max).then_inc(dve_c.next(f"max{n}"), 1)

            def weigh(b):
                pv = bank[6][0:HL, 0:2 * H * (DH + 1)].rearrange("p (j h e) -> p j h e", j=2, h=H)
                dve.wait_ge(pe_c.sem, pe_c.at(b, "pv"))
                dve.reciprocal(rsum[:], pv[:, :, :, DH:DH + 1]).then_inc(dve_c.next("recip"), 1)
                dve.wait_ge(dve_c.sem, dve_c.at(b, "recip"))
                dve.wait_ge(pe_c.sem, pe_c.at(b - 1, "ot"))
                dve.tensor_tensor(o[:], pv[:, :, :, 0:DH], rsum[:].to_broadcast([HL, 2, H, DH]), ALU.mult).then_inc(dve_c.next("o"), 1)

            def add(b):
                dve.wait_ge(pe_c.sem, pe_c.at(b, "out"))
                t = h[:, bass.ds(2 * b, 2), :].rearrange("p t d -> p (t d)")
                dve.tensor_tensor(t, t, bank[6][0:HL, 0:2 * D], ALU.add).then_inc(dve_c.next("add"), 1)

            dve.memset(v[:], 1.0)
            dve.memset(ot_ctx[:], 0.0)
            dve.memset(ot_lat[:], 0.0).then_inc(s_zero, 1)
            stats_of(0)
            normalised(0)
            dve.wait_ge(s_load, 16 * n_loads)
            rotate(0)
            variance(0)

            def body(b, first, last):
                maxima(b)
                if not last:
                    stats_of(b + 1)
                    normalised(b + 1)
                    rotate(b + 1)
                weigh(b)
                if not last:
                    variance(b + 1)
                add(b)

            turns(dve, B, body)

        @block.gpsimd
        def _(pool):
            def values(b):
                def each(t):
                    return t.unsqueeze(3).to_broadcast([HL, 2, H, DH])

                def all_heads(t):
                    return t.unsqueeze(1).unsqueeze(1).to_broadcast([HL, 2, H, DH])

                pool.wait_ge(dve_a.sem, dve_a.at(b, "kmu"))
                pool.wait_ge(pool_a.sem, pool_a.at(b - 1, "v"))
                pool.tensor_tensor(kc[:], qk[:, :, H:2 * H, 0:DH], each(mu[:]), ALU.subtract).then_inc(pool_a.next("kc"), 1)
                pool.wait_ge(pool_a.sem, pool_a.at(b, "kc"))
                pool.wait_ge(dve_a.sem, dve_a.at(b - 1, "kvar"))
                pool.tensor_tensor(ksq[:], kc[:], kc[:], ALU.mult).then_inc(pool_a.next("ksq"), 1)
                pool.wait_ge(act_a.sem, act_a.at(b, "krs"))
                pool.tensor_tensor(kc[:], kc[:], each(krs[:]), ALU.mult).then_inc(pool_a.next("kn"), 1)
                pool.wait_ge(pool_a.sem, pool_a.at(b, "kn"))
                pool.tensor_tensor(kc[:], kc[:], all_heads(gain[:]), ALU.mult).then_inc(pool_a.next("kg"), 1)
                pool.wait_ge(pool_a.sem, pool_a.at(b, "kg"))
                pool.wait_ge(pe_c.sem, pe_c.at(b - 1, "pv"))
                pool.tensor_tensor(v[:, :, :, 0:DH], kc[:], all_heads(shift[:]), ALU.add).then_inc(pool_a.next("v"), 1)

            pool.wait_ge(s_load, 16 * n_loads)
            pool.wait_ge(s_zero, 1)
            values(0)

            def body(b, first, last):
                if not last:
                    values(b + 1)

            turns(pool, B, body)

        @block.scalar
        def _(act):
            def rstd_of(b):
                act.wait_ge(dve_a.sem, dve_a.at(b, "aggr"))
                act.wait_ge(dve_a.sem, dve_a.at(b - 1, "xn"))
                act.activation(lv[:], mv[:, :, 1], ACT.Ln, bias=eps[0:HL, :]).then_inc(act_a.next("lv"), 1)
                act.wait_ge(act_a.sem, act_a.at(b, "lv"))
                act.activation(rstd[:], lv[:], ACT.Exp, scale=-0.5).then_inc(act_a.next("rstd"), 1)

            def copy_xt(b):
                act.wait_ge(pe_a.sem, pe_a.at(b, "xt"))
                act.activation(xt[:], bank[4][0:DH2, 0:2 * L].rearrange("p (k l) -> p k l", k=2), ACT.Copy).then_inc(act_a.next("xt"), 1)

            def copy_qkt(b):
                act.wait_ge(pe_a.sem, pe_a.at(b, "qt"))
                act.activation(qt[:], bank[4][:, 0:HC * L].rearrange("p (c l) -> p c l", c=HC), ACT.Copy).then_inc(act_a.next("qt"), 1)
                act.wait_ge(pe_a.sem, pe_a.at(b, "kt"))
                act.activation(kt[:], bank[5][:, 0:HC * L].rearrange("p (c l) -> p c l", c=HC), ACT.Copy).then_inc(act_a.next("kt"), 1)

            def k_rstd(b):
                act.wait_ge(dve_a.sem, dve_a.at(b, "kvar"))
                act.wait_ge(pool_a.sem, pool_a.at(b - 1, "kn"))
                act.activation(klv[:], var[:], ACT.Ln, bias=eps[0:HL, :], scale=1.0 / DH).then_inc(act_a.next("klv"), 1)
                act.wait_ge(act_a.sem, act_a.at(b, "klv"))
                act.activation(krs[:], klv[:], ACT.Exp, scale=-0.5).then_inc(act_a.next("krs"), 1)

            def copy_q_with_max(b):
                act.wait_ge(pe_c.sem, pe_c.at(b, "qt"))
                act.activation(qt[:], bank[7][:, 0:HC * L].rearrange("p (c l) -> p c l", c=HC), ACT.Copy).then_inc(act_c.next("qt"), 1)

            def exps(b):
                act.wait_ge(pe_c.sem, pe_c.at(b - 1, "pv"))
                for n in range(8):
                    kj, r = divmod(n, HR)
                    act.wait_ge(pe_c.sem, pe_c.at(b, f"p{n}"))
                    act.activation(pt[:, kj, r, :], bank[n % 4][0:HL, 0:HC * L], ACT.Exp).then_inc(act_c.next(f"exp{n}"), 1)

            def copy_ot(b):
                act.wait_ge(pe_c.sem, pe_c.at(b, "ot"))
                src = bank[7][0:DH2, 0:2 * L].rearrange("p (k l) -> p k l", k=2)
                act.activation(ot_ctx[:, :, 0:CTX], src[:, :, 0:CTX], ACT.Copy)
                act.activation(ot_lat[:, :, CTX:L], src[:, :, CTX:L], ACT.Copy).then_inc(act_c.next("ot"), 1)

            act.wait_ge(s_zero, 1)
            rstd_of(0)
            copy_xt(0)
            copy_qkt(0)
            k_rstd(0)

            def body(b, first, last):
                copy_q_with_max(b)
                if not last:
                    rstd_of(b + 1)
                exps(b)
                if not last:
                    copy_xt(b + 1)
                    copy_qkt(b + 1)
                copy_ot(b)
                if not last:
                    k_rstd(b + 1)

            turns(act, B, body)

        @block.tensor
        def _(pe):
            def transpose_x(b):
                pe.wait_ge(dve_a.sem, dve_a.at(b, "xn"))
                pe.wait_ge(dve_a.sem, dve_a.at(b - 1, "sin1"))
                pe.wait_ge(act_a.sem, act_a.at(b - 1, "qt"))
                for k in range(2):
                    for j in range(2):
                        last = pe.transpose(bank[4][0:DH2, k * L + j * HL:k * L + (j + 1) * HL], xn[:, j, k * DH2:(k + 1) * DH2], ident[0:HL, 0:HL])
                last.then_inc(pe_a.next("xt"), 1)

            def project(b):
                pe.wait_ge(act_a.sem, act_a.at(b, "xt"))
                pe.wait_ge(act_a.sem, act_a.at(b - 1, "kt"))
                for j in range(2):
                    for k in range(2):
                        last = pe.matmul(bank[5 - j][0:HL, 0:2 * D], xt[:, k, j * HL:(j + 1) * HL], w_qkv[:, k, :], start=(k == 0), stop=(k == 1))
                    last.then_inc(pe_a.next(f"qkv{j}"), 1)

            def transpose_heads(dst, first_head):
                for j in range(2):
                    for c in range(HC):
                        src = qk[:, j, first_head + HR * c:first_head + HR * (c + 1), :].rearrange("p h e -> p (h e)")
                        last = pe.transpose(dst[:, c * L + j * HL:c * L + (j + 1) * HL], src, ident[0:HL, 0:HL])
                return last

            def transpose_qk(b):
                pe.wait_ge(dve_a.sem, dve_a.at(b, "rope1"))
                transpose_heads(bank[4], 0).then_inc(pe_a.next("qt"), 1)
                transpose_heads(bank[5], H).then_inc(pe_a.next("kt"), 1)

            def scores(b):
                pe.wait_ge(act_a.sem, act_a.at(b, "kt"))
                for n in range(8):
                    j, r = divmod(n, HR)
                    if n < 4:
                        pe.wait_ge(act_c.sem, act_c.at(b - 1, f"exp{n + 4}"))
                    else:
                        pe.wait_ge(dve_c.sem, dve_c.at(b, f"max{n - 4}"))
                    rows = slice(32 * r, 32 * r + DH + 1)
                    for c in range(HC):
                        last = pe.matmul(bank[n % 4][0:HL, c * L:(c + 1) * L], qt[rows, c, j * HL:(j + 1) * HL], kt[rows, c, :],
                                         start=True, stop=True)
                    last.then_inc(pe_c.next(f"s{n}"), 1)

            def transpose_q_with_max(b):
                pe.wait_ge(dve_c.sem, dve_c.at(b, "max7"))
                pe.wait_ge(act_c.sem, act_c.at(b - 1, "ot"))
                transpose_heads(bank[7], 0).then_inc(pe_c.next("qt"), 1)

            def shifted_scores(b):
                pe.wait_ge(act_c.sem, act_c.at(b, "qt"))
                for n in range(8):
                    j, r = divmod(n, HR)
                    if n >= 4:
                        pe.wait_ge(act_c.sem, act_c.at(b, f"exp{n - 4}"))
                    rows = slice(32 * r, 32 * r + DH + 2)
                    for c in range(HC):
                        last = pe.matmul(bank[n % 4][0:HL, c * L:(c + 1) * L], kt[rows, c, j * HL:(j + 1) * HL], qt[rows, c, :],
                                         start=True, stop=True)
                    last.then_inc(pe_c.next(f"p{n}"), 1)

            def weigh_values(b):
                pe.wait_ge(act_c.sem, act_c.at(b, "exp7"))
                pe.wait_ge(pool_a.sem, pool_a.at(b, "v"))
                pe.wait_ge(dve_c.sem, dve_c.at(b - 1, "add"))
                for j in range(2):
                    for hd in range(H):
                        c, r = divmod(hd, HR)
                        at = (j * H + hd) * (DH + 1)
                        for kj in range(2):
                            last = pe.matmul(bank[6][0:HL, at:at + DH + 1], pt[:, kj, r, c * L + j * HL:c * L + (j + 1) * HL],
                                             v[:, kj, hd, :], start=(kj == 0), stop=(kj == 1))
                last.then_inc(pe_c.next("pv"), 1)

            def transpose_o(b):
                pe.wait_ge(dve_c.sem, dve_c.at(b, "o"))
                for k in range(2):
                    for j in range(2):
                        src = o[:, j, :, :].rearrange("p h e -> p (h e)")[:, k * DH2:(k + 1) * DH2]
                        last = pe.transpose(bank[7][0:DH2, k * L + j * HL:k * L + (j + 1) * HL], src, ident[0:HL, 0:HL])
                last.then_inc(pe_c.next("ot"), 1)

            def project_out(b):
                pe.wait_ge(act_c.sem, act_c.at(b, "ot"))
                for j in range(2):
                    dst = bank[6][0:HL, j * D:(j + 1) * D]
                    cols = slice(j * HL, (j + 1) * HL)
                    pe.matmul(dst, kind[:, cols], b_out[:], start=True, stop=False)
                    for t, w in ((ot_ctx, w_ctx), (ot_lat, w_lat)):
                        for k in range(2):
                            last = pe.matmul(dst, t[:, k, cols], w[:, k, :], start=False, stop=(t is ot_lat and k == 1))
                last.then_inc(pe_c.next("out"), 1)

            pe.wait_ge(s_load, 16 * n_loads)
            transpose_x(0)
            project(0)
            transpose_qk(0)

            def body(b, first, last):
                scores(b)
                transpose_q_with_max(b)
                shifted_scores(b)
                if not last:
                    transpose_x(b + 1)
                    project(b + 1)
                weigh_values(b)
                if not last:
                    transpose_qk(b + 1)
                transpose_o(b)
                project_out(b)

            turns(pe, B, body)


def mlp(nc, a, sb, sem, bank, pair, h, ident, ones, eps, which, out):
    mixed = which == 2
    n = f"m{which}_"
    with ExitStack() as ctx, nc.Block() as block:
        w_up = sb(n + "w_up", [DH2, 2, HID], where=ctx)
        b_up = sb(n + "b_up", [128, HM], where=ctx)
        w_down = sb(n + "w_down", [128, HM, D], where=ctx)
        stats = sb(n + "stats", [HL, GT, 6], where=ctx)
        mv = sb(n + "mv", [HL, GT, 2], where=ctx)
        lv = sb(n + "lv", [HL, GT], where=ctx)
        spare = sb(n + "spare", [HL, 1], where=ctx)
        rstd = sb(n + "rstd", [HL, GT], where=ctx)
        xn = sb(n + "xn", [HL, GT, D], where=ctx)
        xt = sb(n + "xt", [DH2, 2, W], where=ctx)
        act_out = sb(n + "hidden", [128, HM, W], where=ctx)
        s_load = sem(n + "s_load")
        s_stats = sem(n + "dve_stats")
        s_stored = sem(n + "s_stored")
        dve_s = Steps(sem(n + "dve"), ["aggr", "xn"])
        s_add = Steps(sem(n + "dve_add"), ["add"])
        act_s = Steps(sem(n + "act_norm"), ["lv", "rstd", "xt"])
        act_g = Steps(sem(n + "act_gelu"), [f"g{m}" for m in range(HM)])
        pe_x = Steps(sem(n + "pe_xt"), ["xt"])
        pe_s = Steps(sem(n + "pe"), [f"up{m}" for m in range(HM)] + ["down"])
        n_loads = 3
        if mixed:
            b_down = sb("b_down", [1, D], where=ctx)
            alpha_e = sb("alpha_e", [3, 1], where=ctx)
            alpha_r = sb("alpha_r", [3, 3], where=ctx)
            rows = sb("mix_rows", [3, 3, HID], where=ctx)
            cols = sb("mix_cols", [3, D], where=ctx)
            one3 = sb("one3", [3, 1], where=ctx)
            coef = sb("mix_coef", [3, HID], where=ctx)
            sum_r = sb("mix_sum", [3, 2], where=ctx)
            n_loads += 6
            s_mix = Steps(sem("dve_mix"), ["c0", "c1", "c2", "coef", "sum", "esum", "b_up", "b_down", "w"])
            s_mixed = Steps(sem("pe_mix"), ["b", "up0", "up1", "down0", "down1", "down2"])

        @block.sync
        def _(sp):
            for dst, name in ((w_up, "w_up"), (b_up, "b_up"), (w_down, "w_down")):
                sp.dma_start(dst[:], a[f"{name}{which}"]).then_inc(s_load, 16)
            if mixed:
                for dst, name in ((b_down, "b_down2"), (alpha_e, "alpha_e"), (rows, "mix_rows"), (cols, "mix_cols"), (one3, "one3")):
                    sp.dma_start(dst[:], a[name]).then_inc(s_load, 16)
                sp.dma_start(alpha_r[:], a["alpha_r"].partition_broadcast(3)).then_inc(s_load, 16)
                out_v = out.rearrange("b (j p) d -> p (b j) d", j=2)
                for q in range(NG):
                    sp.wait_ge(s_add.sem, s_add.at(q, "add"))
                    sp.dma_start(out_v[:, bass.ds(GT * q, GT), :], h[:, bass.ds(GT * q, GT), :]).then_inc(s_stored, 16)
                sp.wait_ge(s_stored, 16 * NG)

        @block.vector
        def _(dve):
            def norm(q):
                for t in range(GT):
                    last = dve.bn_stats(stats[:, t, :], h[:, GT * q + t, :])
                last.then_inc(s_stats, 1)
                dve.wait_ge(s_stats, 1 * q + 1)
                dve.wait_ge(act_s.sem, act_s.at(q - 1, "lv"))
                dve.memset(spare[:], 0.0)
                for t in range(GT):
                    last = dve.bn_aggr(mv[:, t, :], stats[:, t, :])
                last.then_inc(dve_s.next("aggr"), 1)
                dve.wait_ge(act_s.sem, act_s.at(q, "rstd"))
                dve.wait_ge(pe_x.sem, pe_x.at(q - 1, "xt"))
                for t in range(GT):
                    last = dve.tensor_scalar(xn[:, t, :], h[:, GT * q + t, :], mv[:, t, 0:1], rstd[:, t:t + 1], ALU.subtract, ALU.mult)
                last.then_inc(dve_s.next("xn"), 1)

            def add(q):
                dve.wait_ge(pe_s.sem, pe_s.at(q, "down"))
                t = h[:, bass.ds(GT * q, GT), :].rearrange("p (k t) d -> p k (t d)", k=2)
                dve.tensor_tensor(t, t, pair[1][0:HL, :, 0:2 * D], ALU.add).then_inc(s_add.next("add"), 1)

            if mixed:
                dve.wait_ge(s_load, 16 * n_loads)
                dve.tensor_scalar(coef[:], rows[:, 0, :], alpha_r[:, 0:1], None, ALU.mult).then_inc(s_mix.next("c0"), 1)
                for j in range(1, 3):
                    dve.wait_ge(s_mix.sem, s_mix.at(0, f"c{j - 1}"))
                    dve.scalar_tensor_tensor(coef[:], rows[:, j, :], alpha_r[:, j:j + 1], coef[:], ALU.mult, ALU.add).then_inc(s_mix.next(f"c{j}"), 1)
                dve.wait_ge(s_mix.sem, s_mix.at(0, "c2"))
                dve.tensor_scalar(coef[:], coef[:], alpha_e[:, 0:1], None, ALU.mult).then_inc(s_mix.next("coef"), 1)
                dve.tensor_reduce(sum_r[:, 0:1], alpha_r[:], AX.X, ALU.add).then_inc(s_mix.next("sum"), 1)
                dve.wait_ge(s_mix.sem, s_mix.at(0, "sum"))
                dve.tensor_scalar(sum_r[:, 1:2], sum_r[:, 0:1], alpha_e[:, 0:1], None, ALU.mult).then_inc(s_mix.next("esum"), 1)
                dve.wait_ge(s_mixed.sem, s_mixed.at(0, "b"))
                dve.tensor_tensor(b_up[:], b_up[:], bank[0][:, 0:HM], ALU.mult).then_inc(s_mix.next("b_up"), 1)
                dve.tensor_tensor(b_down[:], b_down[:], bank[0][0:1, 64:64 + D], ALU.mult).then_inc(s_mix.next("b_down"), 1)
                for k in range(2):
                    dve.wait_ge(s_mixed.sem, s_mixed.at(0, f"up{k}"))
                    for half in range(2):
                        part = w_up[:, k, half * DI:(half + 1) * DI]
                        dve.tensor_tensor(part, part, pair[k][0:DH2, half, 0:DI], ALU.mult)
                for k in range(3):
                    dve.wait_ge(s_mixed.sem, s_mixed.at(0, f"down{k}"))
                    part = w_down[:, 2 * k:2 * k + 2, :].rearrange("p m d -> p (m d)")
                    last = dve.tensor_tensor(part, part, bank[1 + k][:, 0:2 * D], ALU.mult)
                last.then_inc(s_mix.next("w"), 1)
            norm(0)

            def body(q, first, last):
                if not last:
                    norm(q + 1)
                add(q)

            turns(dve, NG, body)

        @block.scalar
        def _(act):
            def norm(q):
                act.wait_ge(dve_s.sem, dve_s.at(q, "aggr"))
                act.wait_ge(dve_s.sem, dve_s.at(q - 1, "xn"))
                act.activation(lv[:], mv[:, :, 1], ACT.Ln, bias=eps[0:HL, :]).then_inc(act_s.next("lv"), 1)
                act.wait_ge(act_s.sem, act_s.at(q, "lv"))
                act.activation(rstd[:], lv[:], ACT.Exp, scale=-0.5).then_inc(act_s.next("rstd"), 1)

            def copy_xt(q):
                act.wait_ge(pe_x.sem, pe_x.at(q, "xt"))
                act.wait_ge(pe_s.sem, pe_s.at(q - 1, f"up{HM - 1}"))
                act.activation(xt[:], pair[0][0:DH2, :, 0:W], ACT.Copy).then_inc(act_s.next("xt"), 1)

            norm(0)
            copy_xt(0)
            act.wait_ge(s_load, 16 * n_loads)
            if mixed:
                act.wait_ge(s_mix.sem, s_mix.at(0, "w"))

            def body(q, first, last):
                if not last:
                    norm(q + 1)
                act.wait_ge(pe_s.sem, pe_s.at(q - 1, "down"))
                for m in range(HM):
                    act.wait_ge(pe_s.sem, pe_s.at(q, f"up{m}"))
                    act.activation(act_out[:, m, :], bank[m % 4][:, 0:W], ACT.Gelu_apprx_tanh if mixed else ACT.Gelu,
                                              bias=b_up[:, m:m + 1]).then_inc(act_g.next(f"g{m}"), 1)
                if not last:
                    copy_xt(q + 1)

            turns(act, NG, body)

        @block.tensor
        def _(pe):
            def transpose_x(q):
                pe.wait_ge(dve_s.sem, dve_s.at(q, "xn"))
                pe.wait_ge(act_s.sem, act_s.at(q - 1, "xt"))
                for k in range(2):
                    for t in range(GT):
                        last = pe.transpose(pair[0][0:DH2, k, t * HL:(t + 1) * HL], xn[:, t, k * DH2:(k + 1) * DH2], ident[0:HL, 0:HL])
                last.then_inc(pe_x.next("xt"), 1)

            pe.wait_ge(s_load, 16 * n_loads)
            if mixed:
                pe.wait_ge(s_mix.sem, s_mix.at(0, "esum"))
                for m in range(HM):
                    pe.matmul(bank[0][:, m:m + 1], coef[:, m * 128:(m + 1) * 128], one3[:], start=True, stop=True)
                pe.matmul(bank[0][0:1, 64:64 + D], sum_r[:, 1:2], cols[:], start=True, stop=True).then_inc(s_mixed.next("b"), 1)
                for k in range(2):
                    for half in range(2):
                        last = pe.matmul(pair[k][0:DH2, half, 0:DI], cols[:, k * DH2:(k + 1) * DH2], coef[:, half * DI:(half + 1) * DI], start=True, stop=True)
                    last.then_inc(s_mixed.next(f"up{k}"), 1)
                for k in range(3):
                    for m in range(2):
                        last = pe.matmul(bank[1 + k][:, m * D:(m + 1) * D], coef[:, (2 * k + m) * 128:(2 * k + m + 1) * 128], cols[:], start=True, stop=True)
                    last.then_inc(s_mixed.next(f"down{k}"), 1)
                pe.wait_ge(s_mix.sem, s_mix.at(0, "w"))
            transpose_x(0)

            def body(q, first, last):
                pe.wait_ge(act_s.sem, act_s.at(q, "xt"))
                for m in range(HM):
                    if m < 4:
                        pe.wait_ge(act_g.sem, act_g.at(q - 1, f"g{m + 4 if m + 4 < HM else m}"))
                    else:
                        pe.wait_ge(act_g.sem, act_g.at(q, f"g{m - 4}"))
                    for k in range(2):
                        last_mm = pe.matmul(bank[m % 4][:, 0:W], w_up[:, k, m * 128:(m + 1) * 128], xt[:, k, :], start=(k == 0), stop=(k == 1))
                    last_mm.then_inc(pe_s.next(f"up{m}"), 1)
                if not last:
                    transpose_x(q + 1)
                pe.wait_ge(s_add.sem, s_add.at(q - 1, "add"))
                pe.wait_ge(act_g.sem, act_g.at(q, f"g{HM - 1}"))
                for t in range(GT):
                    dst = pair[1][0:HL, t // 2, (t % 2) * D:(t % 2 + 1) * D]
                    for m in range(HM):
                        last_mm = pe.matmul(dst, act_out[:, m, t * HL:(t + 1) * HL], w_down[:, m, :], start=(m == 0), stop=(m == HM - 1 and not mixed))
                    if mixed:
                        last_mm = pe.matmul(dst, ones[:], b_down[:], start=False, stop=True)
                last_mm.then_inc(pe_s.next("down"), 1)

            turns(pe, NG, body)


def normalise(nc, a, sb, sem, src, dst, eps, final):
    n = "nf_" if final else "n0_"
    with ExitStack() as ctx, nc.Block() as block:
        stats = sb(n + "stats", [HL, GT, 6], where=ctx)
        mv = sb(n + "mv", [HL, GT, 2], where=ctx)
        lv = sb(n + "lv", [HL, GT], where=ctx)
        spare = sb(n + "spare", [HL, 1], where=ctx)
        rstd = sb(n + "rstd", [HL, GT], where=ctx)
        s_dve = Steps(sem(n + "dve"), ["stats", "aggr", "xn"] + (["w", "b", "add"] if final else []))
        s_act = Steps(sem(n + "act"), ["lv", "rstd"])
        if final:
            s_load = sem("s_final_load")
            fw = sb("final_w", [HL, D], where=ctx)
            fb = sb("final_b", [HL, D], where=ctx)
            xn = sb("final_xn", [HL, GT, D], where=ctx)

            @block.sync
            def _(sp):
                sp.dma_start(fw[:], a["final_w"].partition_broadcast(HL)).then_inc(s_load, 16)
                sp.dma_start(fb[:], a["final_b"].partition_broadcast(HL)).then_inc(s_load, 16)

        @block.vector
        def _(dve):
            def body(q, first, last):
                for t in range(GT):
                    ins = dve.bn_stats(stats[:, t, :], src[:, GT * q + t, :])
                ins.then_inc(s_dve.next("stats"), 1)
                dve.wait_ge(s_dve.sem, s_dve.at(q, "stats"))
                dve.memset(spare[:], 0.0)
                for t in range(GT):
                    ins = dve.bn_aggr(mv[:, t, :], stats[:, t, :])
                ins.then_inc(s_dve.next("aggr"), 1)
                dve.wait_ge(s_act.sem, s_act.at(q, "rstd"))
                for t in range(GT):
                    to = xn[:, t, :] if final else dst[:, GT * q + t, :]
                    ins = dve.tensor_scalar(to, src[:, GT * q + t, :], mv[:, t, 0:1], rstd[:, t:t + 1], ALU.subtract, ALU.mult)
                ins.then_inc(s_dve.next("xn"), 1)
                if final:
                    dve.wait_ge(s_dve.sem, s_dve.at(q, "xn"))
                    dve.tensor_tensor(xn[:], xn[:], fw[:].unsqueeze(1).to_broadcast([HL, GT, D]), ALU.mult).then_inc(s_dve.next("w"), 1)
                    dve.wait_ge(s_dve.sem, s_dve.at(q, "w"))
                    dve.tensor_tensor(xn[:], xn[:], fb[:].unsqueeze(1).to_broadcast([HL, GT, D]), ALU.add).then_inc(s_dve.next("b"), 1)
                    dve.wait_ge(s_dve.sem, s_dve.at(q, "b"))
                    to = dst[:, bass.ds(GT * q, GT), :]
                    dve.tensor_tensor(to, to, xn[:], ALU.add).then_inc(s_dve.next("add"), 1)

            if final:
                dve.wait_ge(s_load, 32)
            turns(dve, NG, body)

        @block.scalar
        def _(act):
            def body(q, first, last):
                act.wait_ge(s_dve.sem, s_dve.at(q, "aggr"))
                act.activation(lv[:], mv[:, :, 1], ACT.Ln, bias=eps[0:HL, :]).then_inc(s_act.next("lv"), 1)
                act.wait_ge(s_act.sem, s_act.at(q, "lv"))
                act.activation(rstd[:], lv[:], ACT.Exp, scale=-0.5).then_inc(s_act.next("rstd"), 1)

            turns(act, NG, body)


def mamba(nc, a, sb, sem, bank, two, pair, res, ident, eps):
    with ExitStack() as ctx, nc.Block() as block:
        packs = sb("packs", [128, NL, NPACK], where=ctx)
        w_in = sb("w_in", [DH2, 2, 2 * DI], where=ctx)
        w_x = sb("w_x", [128, NC, 128], where=ctx)
        w_dt = sb("w_dt", [RANK, DI], where=ctx)
        w_out = sb("w_out", [128, NC, D], where=ctx)
        spread = sb("spread", [128, 2 * NS, 128], BF16, where=ctx)
        pf = sb("pf", [128, NPF], where=ctx)
        ps = [sb(f"ps{p}", [128, P_F], where=ctx) for p in range(2)]
        stats = sb("b_stats", [HL, GT, 6], where=ctx)
        mv = sb("b_mv", [HL, GT, 2], where=ctx)
        vare = sb("b_vare", [HL, GT], where=ctx)
        minus_half = sb("minus_half", [HL, GT], where=ctx)
        rstd = sb("b_rstd", [HL, GT], where=ctx)
        spare = sb("b_spare", [HL, 1], where=ctx)
        xn = sb("b_xn", [HL, GT, D], where=ctx)
        xt = sb("b_xt", [DH2, 2, W], where=ctx)
        xpad = sb("xpad", [128, NC, GB, L + TAPS - 1], where=ctx)
        conv = sb("conv", [128, NC, W], where=ctx)
        dtr = sb("dtr", [RANK, W], where=ctx)
        bcr = sb("bcr", [128, W], where=ctx)
        bcs = sb("bcs", [128, W], BF16, where=ctx)
        sp_abs = sb("sp_abs", [128, NC, W], where=ctx)
        x = [sb(f"x{p}", [128, NC, W], where=ctx) for p in range(2)]
        z = [sb(f"z{p}", [128, NC, W], where=ctx) for p in range(2)]
        dt = [sb(f"dt{p}", [128, NC, W], where=ctx) for p in range(2)]
        bc = [sb(f"bc{p}", [128, 2 * NS, W], where=ctx) for p in range(2)]
        NA, NH, NQ = 4, 3, 4
        da = sb("da", [128, NA, GB, L], where=ctx)
        hs = sb("hs", [128, NH, W], where=ctx)
        hc = sb("hc", [128, NQ, W], where=ctx)
        y = sb("y", [128, NC, W], where=ctx)

        s_load = sem("s_mamba_load")
        s_w = sem("s_w_in")
        s_wo = sem("s_w_out")
        s_zero = sem("s_mamba_zero")
        s_a = sem("s_a")
        s_neg = sem("s_neg")
        s_half = sem("s_half")
        dve_f = Steps(sem("dve_front"), ["stats", "aggr", "vare", "xn"] + [f"c{k}" for k in range(TAPS)] +
                      ["dtr", "rest", "mid", "lo", "sp0", "sp1", "sp2", "dt"])
        act_f = Steps(sem("act_front"), ["xt0", "xt1", "x01", "x2", "z01", "z2", "x", "hi", "abs0", "abs1", "abs2", "exp", "ln"] +
                      [f"bc{k}" for k in range(NS)])
        pe_f = Steps(sem("pe_front"), ["xt"] + [f"in{k}" for k in range(2 * NC)] + ["xp", "dt01", "dt2"] + [f"bc{k}" for k in range(NS)])
        pool_f = Steps(sem("pool_front"), ["pf", "ps", "rstd"])
        names = []
        for n in range(STEPS):
            names += [f"dtx{n // NS}"] if n % NS == 0 else []
            names += [f"m{n}"]
            names += [f"s{n - 1}"] if n else []
            names += [f"yd{n // NS - 1}", f"g{n // NS - 1}"] if n % NS == 4 and n > NS else []
        dve_s = Steps(sem("dve_scan"), names + [f"s{STEPS - 1}"])
        dve_t = Steps(sem("dve_tail"), ["yd2", "g2", "add"])
        act_s = Steps(sem("act_scan"), [f"a{n}" for n in range(STEPS)])
        pool_s = Steps(sem("pool_scan"), [f"h{n}" for n in range(STEPS)])
        pe_s = Steps(sem("pe_scan"), [f"y{n}" for n in range(STEPS)])
        pe_t = Steps(sem("pe_tail"), ["out"])

        BC_BEFORE = 10
        PE_BC = [28, 29, 31, 32, 34, 35, 37, 38, 41, 43]
        ACT_BC = [36, 37, 39, 40, 42, 43, 45, 46]

        def rows_of(k):
            return (k % 2) * NS + k // 2 * 2

        def tiles_of(u):
            return bass.ds((u % NG) * GT, GT)

        def units(eng, body):
            def two(i, first, last):
                body(2 * i, 0, first, False)
                body(2 * i + 1, 1, False, last)
            turns(eng, UNITS // 2, two)

        @block.sync
        def _(sp):
            def load_in(layer):
                sp.dma_start(w_in[:], a["w_in"][layer]).then_inc(s_w, 16)
                sp.dma_start(w_x[:], a["w_x"][layer]).then_inc(s_w, 16)
                sp.dma_start(w_dt[:], a["w_dt"][layer]).then_inc(s_w, 16)

            sp.dma_start(packs[:], a["packs"]).then_inc(s_load, 16)
            sp.dma_start(spread[:], a["spread"]).then_inc(s_load, 16)
            load_in(0)

            def two(i, first, last):
                sp.wait_ge(pe_t.sem, pe_t.at(2 * i - 1, "out"))
                sp.dma_start(w_out[:], a["w_out"][i // 2]).then_inc(s_wo, 16)
                if not last:
                    sp.wait_ge(pe_f.sem, pe_f.at(2 * i + 1, "dt2"))
                    load_in((i + 1) // 2)
            turns(sp, UNITS // 2, two)
            sp.wait_ge(s_wo, 16 * UNITS // 2)

        @block.gpsimd
        def _(pool):
            def params(u, p):
                pool.wait_ge(act_f.sem, act_f.at(u - 1, f"bc{NS - 1}"))
                pool.wait_ge(dve_f.sem, dve_f.at(u - 1, "dt"))
                pool.tensor_copy(pf[:], packs[:, u // NG, P_F:NPACK]).then_inc(pool_f.next("pf"), 1)
                pool.wait_ge(act_s.sem, act_s.at(u - 2, f"a{STEPS - 1}"))
                pool.wait_ge(dve_t.sem, dve_t.at(u - 2, "yd2"))
                pool.tensor_copy(ps[p][:], packs[:, u // NG, 0:P_F]).then_inc(pool_f.next("ps"), 1)

            def rstd_of(u):
                pool.wait_ge(dve_f.sem, dve_f.at(u, "vare"))
                pool.wait_ge(dve_f.sem, dve_f.at(u - 1, "xn"))
                pool.tensor_tensor(rstd[:], vare[:], minus_half[:], ALU.pow).then_inc(pool_f.next("rstd"), 1)

            pool.memset(minus_half[:], -0.5)
            pool.memset(xpad[:], 0.0)
            pool.memset(da[:], 0.0).then_inc(s_zero, 1)
            pool.wait_ge(s_zero, 1)
            pool.wait_ge(s_neg, 1)
            params(0, 0)
            rstd_of(0)

            def body(u, p, first, last):
                for n in range(STEPS):
                    if n == 6 and not last:
                        params(u + 1, 1 - p)
                    if n == 8 and not last:
                        rstd_of(u + 1)
                    if n < NS and n % 2 == 0:
                        pool.wait_ge(act_f.sem, act_f.at(u, f"bc{n + 1}"))
                    pool.wait_ge(dve_s.sem, dve_s.at(u, f"s{n}"))
                    if n >= NQ:
                        pool.wait_ge(pe_s.sem, pe_s.at(u, f"y{n - NQ}"))
                    else:
                        pool.wait_ge(pe_s.sem, pe_s.at(u - 1, f"y{STEPS - NQ + n}"))
                    pool.tensor_tensor(hc[:, n % NQ, :], hs[:, n % NH, :], bc[p][:, NS + n % NS, :], ALU.mult).then_inc(pool_s.next(f"h{n}"), 1)

            units(pool, body)

        @block.vector
        def _(dve):
            dtx = bank[0][:, 0:W]

            def dbx(n):
                return two[:, (n % 3) * W:(n % 3 + 1) * W]

            def norm_stats(u):
                src = res[:, tiles_of(u), :]
                for t in range(GT):
                    last = dve.bn_stats(stats[:, t, :], src[:, t, :])
                last.then_inc(dve_f.next("stats"), 1)
                dve.wait_ge(dve_f.sem, dve_f.at(u, "stats"))
                dve.memset(spare[:], 0.0)
                for t in range(GT):
                    last = dve.bn_aggr(mv[:, t, :], stats[:, t, :])
                last.then_inc(dve_f.next("aggr"), 1)
                dve.wait_ge(dve_f.sem, dve_f.at(u, "aggr"))
                dve.wait_ge(pool_f.sem, pool_f.at(u - 1, "rstd"))
                dve.tensor_scalar(vare[:], mv[:, :, 1], EPS, None, ALU.add).then_inc(dve_f.next("vare"), 1)

            def norm_apply(u):
                src = res[:, tiles_of(u), :]
                dve.wait_ge(pool_f.sem, pool_f.at(u, "rstd"))
                dve.wait_ge(pe_f.sem, pe_f.at(u - 1, "xt"))
                for t in range(GT):
                    last = dve.tensor_scalar(xn[:, t, :], src[:, t, :], mv[:, t, 0:1], rstd[:, t:t + 1], ALU.subtract, ALU.mult)
                last.then_inc(dve_f.next("xn"), 1)

            def convolve(u, k):
                if k == 0:
                    dve.wait_ge(act_f.sem, act_f.at(u, "x2"))
                    dve.wait_ge(act_f.sem, act_f.at(u - 1, "x"))
                    dve.wait_ge(pool_f.sem, pool_f.at(u, "pf"))
                else:
                    dve.wait_ge(dve_f.sem, dve_f.at(u, f"c{k - 1}"))
                for c in range(NC):
                    w = pf[:, P_CW + c * TAPS + k:P_CW + c * TAPS + k + 1]
                    src = xpad[:, c, :, k:k + L]
                    dst = conv[:, c, :].rearrange("p (b l) -> p b l", b=GB)
                    if k == 0:
                        last = dve.tensor_scalar(dst, src, w, pf[:, P_CB + c:P_CB + c + 1], ALU.mult, ALU.add)
                    else:
                        last = dve.scalar_tensor_tensor(dst, src, w, dst, ALU.mult, ALU.add)
                last.then_inc(dve_f.next(f"c{k}"), 1)

            def split_bc(u):
                dve.wait_ge(pe_f.sem, pe_f.at(u, "xp"))
                dve.wait_ge(pe_f.sem, pe_f.at(u - 1, "dt2"))
                dve.wait_ge(act_f.sem, act_f.at(u, "hi"))
                dve.tensor_copy(dtr[:], pair[0][0:RANK, 0, 0:W]).then_inc(dve_f.next("dtr"), 1)
                dve.tensor_tensor(bcr[:], pair[0][:, 0, 0:W], bcs[:], ALU.subtract).then_inc(dve_f.next("rest"), 1)
                dve.wait_ge(dve_f.sem, dve_f.at(u, "rest"))
                dve.tensor_copy(bcs[64:128, :], bcr[64:128, :]).then_inc(dve_f.next("mid"), 1)
                dve.wait_ge(dve_f.sem, dve_f.at(u, "mid"))
                dve.tensor_tensor(bcs[96:128, :], bcr[96:128, :], bcs[96:128, :], ALU.subtract).then_inc(dve_f.next("lo"), 1)

            def softplus(u, p):
                for c in range(NC):
                    dve.wait_ge(pe_f.sem, pe_f.at(u, "dt01" if c < 2 else "dt2"))
                    dve.wait_ge(act_f.sem, act_f.at(u, "abs1" if c < 2 else "abs2"))
                    src = pair[1][:, c, 0:W] if c < 2 else pair[0][:, 0, 0:W]
                    dve.tensor_scalar(dt[p][:, c, :], src, pf[:, P_DTB + c:P_DTB + c + 1], 0.0, ALU.add, ALU.max).then_inc(dve_f.next(f"sp{c}"), 1)
                dve.wait_ge(act_f.sem, act_f.at(u, "ln"))
                dve.wait_ge(dve_f.sem, dve_f.at(u, "sp2"))
                dve.tensor_tensor(dt[p][:], dt[p][:], sp_abs[:], ALU.add).then_inc(dve_f.next("dt"), 1)

            def gate(steps, u, p, c):
                dve.wait_ge(pe_s.sem, pe_s.at(u, f"y{NS * (c + 1) - 1}"))
                dve.wait_ge(pe_t.sem, pe_t.at(u - 1, "out"))
                dve.scalar_tensor_tensor(y[:, c, :], x[p][:, c, :], ps[p][:, P_D + c:P_D + c + 1], bank[3][:, 0:W],
                                                    ALU.mult, ALU.add).then_inc(steps.next(f"yd{c}"), 1)
                dve.wait_ge(steps.sem, steps.at(u, f"yd{c}"))
                dve.tensor_tensor(y[:, c, :], y[:, c, :], z[p][:, c, :], ALU.mult).then_inc(steps.next(f"g{c}"), 1)

            def scan(u, n):
                dve.wait_ge(act_s.sem, act_s.at(u, f"a{n}"))
                dve.wait_ge(dve_s.sem, dve_s.at(u, f"m{n}"))
                if n >= NH:
                    dve.wait_ge(pool_s.sem, pool_s.at(u, f"h{n - NH}"))
                else:
                    dve.wait_ge(pool_s.sem, pool_s.at(u - 1, f"h{STEPS - NH + n}"))
                dve.tensor_tensor_scan(hs[:, n % NH, :], da[:, n % NA, :, :].rearrange("p b l -> p (b l)"),
                                                  dbx(n), 0.0, ALU.mult, ALU.add).then_inc(dve_s.next(f"s{n}"), 1)

            def add_out(u):
                dve.wait_ge(pe_t.sem, pe_t.at(u, "out"))
                t = res[:, tiles_of(u), :].rearrange("p (k t) d -> p k (t d)", k=2)
                dve.tensor_tensor(t, t, pair[1][0:HL, :, 0:2 * D], ALU.add).then_inc(dve_t.next("add"), 1)

            dve.wait_ge(s_a, 1)
            dve.tensor_scalar(packs[:, :, 0:P_D], packs[:, :, 0:P_D], -1.0, None, ALU.mult).then_inc(s_neg, 1)
            norm_stats(0)
            norm_apply(0)
            for k in range(TAPS):
                convolve(0, k)
            split_bc(0)
            softplus(0, 0)

            def body(u, p, first, last):
                for n in range(STEPS):
                    if n % NS == 0:
                        c = n // NS
                        if c == 0:
                            dve.wait_ge(dve_f.sem, dve_f.at(u, "dt"))
                            dve.wait_ge(act_f.sem, act_f.at(u, "x"))
                        dve.wait_ge(dve_s.sem, dve_s.at(u if n else u - 1, f"m{(n - 1) % STEPS}"))
                        dve.tensor_tensor(dtx, dt[p][:, c, :], x[p][:, c, :], ALU.mult).then_inc(dve_s.next(f"dtx{c}"), 1)
                        dve.wait_ge(dve_s.sem, dve_s.at(u, f"dtx{c}"))
                    if n < NS and n % 2 == 0:
                        dve.wait_ge(act_f.sem, act_f.at(u, f"bc{n}"))
                    if n >= 3:
                        dve.wait_ge(dve_s.sem, dve_s.at(u, f"s{n - 3}"))
                    else:
                        dve.wait_ge(dve_s.sem, dve_s.at(u - 1, f"s{STEPS - 3 + n}"))
                    dve.tensor_tensor(dbx(n), dtx, bc[p][:, n % NS, :], ALU.mult).then_inc(dve_s.next(f"m{n}"), 1)
                    if n:
                        scan(u, n - 1)
                    if n == 3 and not first:
                        gate(dve_t, u - 1, 1 - p, NC - 1)
                    if n == 13 and not first:
                        add_out(u - 1)
                    if not last:
                        if n == 6:
                            norm_stats(u + 1)
                        if n == 10:
                            norm_apply(u + 1)
                        if 16 <= n < 16 + TAPS:
                            convolve(u + 1, n - 16)
                        if n == 26:
                            split_bc(u + 1)
                        if n == 33:
                            softplus(u + 1, 1 - p)
                    if n % NS == 4 and n > NS:
                        gate(dve_s, u, p, n // NS - 1)
                scan(u, STEPS - 1)
                if last:
                    gate(dve_t, u, p, NC - 1)
                    add_out(u)

            units(dve, body)

        @block.scalar
        def _(act):
            def batches(t):
                return t.rearrange("p (b l) -> p b l", b=GB)

            def copy_xt(u):
                act.wait_ge(pool_f.sem, pool_f.at(u, "pf"))
                act.wait_ge(pe_f.sem, pe_f.at(u, "xt"))
                act.wait_ge(pe_f.sem, pe_f.at(u - 1, "in5"))
                for k in range(2):
                    act.activation(xt[:, k, :], pair[0][0:DH2, k, 0:W], ACT.Identity, scale=pf[0:DH2, P_NW + k:P_NW + k + 1],
                                              bias=pf[0:DH2, P_NB + k:P_NB + k + 1]).then_inc(act_f.next(f"xt{k}"), 1)

            def copy_x(u):
                act.wait_ge(pe_f.sem, pe_f.at(u, "in1"))
                act.wait_ge(dve_f.sem, dve_f.at(u - 1, f"c{TAPS - 1}"))
                act.activation(xpad[:, 0:2, :, TAPS - 1:], pair[1][:, :, 0:W].rearrange("p c (b l) -> p c b l", b=GB), ACT.Copy).then_inc(act_f.next("x01"), 1)
                act.wait_ge(pe_f.sem, pe_f.at(u, "in2"))
                act.activation(xpad[:, 2, :, TAPS - 1:], batches(pair[0][:, 0, 0:W]), ACT.Copy).then_inc(act_f.next("x2"), 1)

            def silus(u, p):
                act.wait_ge(dve_t.sem, dve_t.at(u - 2, "g2"))
                act.wait_ge(pe_f.sem, pe_f.at(u, "in5"))
                act.activation(z[p][:, 0:2, :], pair[1][:, :, 0:W], ACT.Silu).then_inc(act_f.next("z01"), 1)
                act.activation(z[p][:, 2, :], pair[0][:, 1, 0:W], ACT.Silu).then_inc(act_f.next("z2"), 1)
                act.wait_ge(dve_f.sem, dve_f.at(u, f"c{TAPS - 1}"))
                act.activation(x[p][:], conv[:], ACT.Silu).then_inc(act_f.next("x"), 1)

            def high_part(u):
                act.wait_ge(pe_f.sem, pe_f.at(u, "xp"))
                act.wait_ge(pe_f.sem, pe_f.at(u - 1, f"bc{NS - 1}"))
                act.activation(bcs[:], pair[0][:, 0, 0:W], ACT.Copy).then_inc(act_f.next("hi"), 1)

            def soft(u):
                act.wait_ge(dve_f.sem, dve_f.at(u - 1, "dt"))
                for c in range(NC):
                    act.wait_ge(pe_f.sem, pe_f.at(u, "dt01" if c < 2 else "dt2"))
                    src = pair[1][:, c, 0:W] if c < 2 else pair[0][:, 0, 0:W]
                    act.activation(sp_abs[:, c, :], src, ACT.Abs, bias=pf[:, P_DTB + c:P_DTB + c + 1]).then_inc(act_f.next(f"abs{c}"), 1)
                act.wait_ge(act_f.sem, act_f.at(u, "abs2"))
                act.activation(sp_abs[:], sp_abs[:], ACT.Exp, scale=-1.0).then_inc(act_f.next("exp"), 1)
                act.wait_ge(act_f.sem, act_f.at(u, "exp"))
                act.activation(sp_abs[:], sp_abs[:], ACT.Ln, bias=1.0).then_inc(act_f.next("ln"), 1)

            def copy_bc(u, p, k):
                if k == 0:
                    act.wait_ge(pool_s.sem, pool_s.at(u - 2, f"h{STEPS - 1}"))
                act.wait_ge(pe_f.sem, pe_f.at(u, f"bc{k}"))
                act.activation(bc[p][:, rows_of(k):rows_of(k) + 2, :], pair[(k + 1) % 2][:, :, 0:W], ACT.Copy).then_inc(act_f.next(f"bc{k}"), 1)

            act.wait_ge(s_load, 32)
            act.activation(packs[:, :, 0:P_D], packs[:, :, 0:P_D], ACT.Exp).then_inc(s_a, 1)
            act.wait_ge(s_zero, 1)
            copy_xt(0)
            copy_x(0)
            silus(0, 0)
            high_part(0)
            soft(0)
            for k in range(8):
                copy_bc(0, 0, k)

            def body(u, p, first, last):
                for n in range(STEPS):
                    if n == 0:
                        act.wait_ge(dve_f.sem, dve_f.at(u, "dt"))
                        act.wait_ge(pool_f.sem, pool_f.at(u, "ps"))
                    if n in (0, 2):
                        copy_bc(u, p, 8 + n // 2)
                    if 7 <= n < 7 + NS - BC_BEFORE:
                        copy_bc(u, p, n - 7 + BC_BEFORE)
                    if n >= NA:
                        act.wait_ge(dve_s.sem, dve_s.at(u, f"s{n - NA}"))
                    else:
                        act.wait_ge(dve_s.sem, dve_s.at(u - 1, f"s{STEPS - NA + n}"))
                    src = batches(dt[p][:, n // NS, :])
                    act.activation(da[:, n % NA, :, 1:L], src[:, :, 1:L], ACT.Exp, scale=ps[p][:, P_A + n:P_A + n + 1]).then_inc(act_s.next(f"a{n}"), 1)
                    if not last:
                        if n == 14:
                            copy_xt(u + 1)
                        if n == 17:
                            copy_x(u + 1)
                        if n == 23:
                            silus(u + 1, 1 - p)
                        if n == 27:
                            high_part(u + 1)
                        if n == 32:
                            soft(u + 1)
                        if n in ACT_BC:
                            copy_bc(u + 1, 1 - p, ACT_BC.index(n))

            units(act, body)

        @block.tensor
        def _(pe):
            def transpose_x(u):
                pe.wait_ge(dve_f.sem, dve_f.at(u, "xn"))
                pe.wait_ge(act_f.sem, act_f.at(u - 1, f"bc{NS - 1}"))
                for k in range(2):
                    for t in range(GT):
                        last = pe.transpose(pair[0][0:DH2, k, t * HL:(t + 1) * HL], xn[:, t, k * DH2:(k + 1) * DH2], ident[0:HL, 0:HL])
                last.then_inc(pe_f.next("xt"), 1)

            def project(dst, m):
                for k in range(2):
                    last = pe.matmul(dst, w_in[:, k, m * 128:(m + 1) * 128], xt[:, k, :], start=(k == 0), stop=(k == 1))
                return last

            def project_in(u, step):
                m = (0, 1, 2, NC + 2, NC, NC + 1)[step]
                if step == 0:
                    pe.wait_ge(s_w, (u // 2) * 48 + 48)
                    pe.wait_ge(act_f.sem, act_f.at(u, "xt1"))
                    pe.wait_ge(dve_t.sem, dve_t.at(u - 2, "add"))
                if step == 4:
                    pe.wait_ge(act_f.sem, act_f.at(u, "x01"))
                last = project(pair[(1, 0, 1)[step // 2]][:, step % 2, 0:W], m)
                last.then_inc(pe_f.next(f"in{step}"), 1)

            def project_bc(u, p):
                pe.wait_ge(act_f.sem, act_f.at(u, "x"))
                pe.wait_ge(act_f.sem, act_f.at(u, "z2"))
                for c in range(NC):
                    last = pe.matmul(pair[0][:, 0, 0:W], w_x[:, c, :], x[p][:, c, :], start=(c == 0), stop=(c == NC - 1))
                last.then_inc(pe_f.next("xp"), 1)

            def project_dt(u):
                pe.wait_ge(dve_f.sem, dve_f.at(u, "dtr"))
                for c in range(2):
                    last = pe.matmul(pair[1][:, c, 0:W], w_dt[:, c * 128:(c + 1) * 128], dtr[:], start=True, stop=True)
                last.then_inc(pe_f.next("dt01"), 1)
                pe.wait_ge(act_f.sem, act_f.at(u, "hi"))
                pe.wait_ge(dve_f.sem, dve_f.at(u, "rest"))
                pe.matmul(pair[0][:, 0, 0:W], w_dt[:, 2 * 128:3 * 128], dtr[:], start=True, stop=True).then_inc(pe_f.next("dt2"), 1)

            def spread_bc(u, k):
                if k == 0:
                    pe.wait_ge(dve_f.sem, dve_f.at(u, "lo"))
                    pe.wait_ge(dve_f.sem, dve_f.at(u, "sp1"))
                elif k == 1:
                    pe.wait_ge(dve_f.sem, dve_f.at(u, "sp2"))
                else:
                    pe.wait_ge(act_f.sem, act_f.at(u, f"bc{k - 2}"))
                for j in range(2):
                    last = pe.matmul(pair[(k + 1) % 2][:, j, 0:W], spread[:, rows_of(k) + j, :], bcs[:], start=True, stop=True)
                last.then_inc(pe_f.next(f"bc{k}"), 1)

            def sum_states(u, n):
                if n % NS == 0:
                    if n:
                        pe.wait_ge(dve_s.sem, dve_s.at(u, f"yd{n // NS - 1}"))
                    else:
                        pe.wait_ge(dve_t.sem, dve_t.at(u - 1, "yd2"))
                pe.wait_ge(pool_s.sem, pool_s.at(u, f"h{n}"))
                pe.matmul(bank[3][:, 0:W], ident[:], hc[:, n % NQ, :], start=(n % NS == 0), stop=(n % NS == NS - 1)).then_inc(pe_s.next(f"y{n}"), 1)

            def project_out(u, last_unit):
                pe.wait_ge(dve_t.sem, dve_t.at(u, "g2"))
                pe.wait_ge(s_wo, (u // 2) * 16 + 16)
                pe.wait_ge(act_f.sem, act_f.at(u if last_unit else u + 1, f"bc{NS - 2}"))
                for t in range(GT):
                    for c in range(NC):
                        last = pe.matmul(pair[1][0:HL, t // 2, (t % 2) * D:(t % 2 + 1) * D], y[:, c, t * HL:(t + 1) * HL], w_out[:, c, :],
                                         start=(c == 0), stop=(c == NC - 1))
                last.then_inc(pe_t.next("out"), 1)

            pe.wait_ge(s_load, 32)
            transpose_x(0)
            for m in range(2 * NC):
                project_in(0, m)
            project_bc(0, 0)
            project_dt(0)
            for k in range(BC_BEFORE):
                spread_bc(0, k)

            def body(u, p, first, last):
                for n in range(STEPS):
                    if BC_BEFORE + n < NS:
                        spread_bc(u, BC_BEFORE + n)
                    if n == 9 and not first:
                        project_out(u - 1, False)
                    if not last:
                        if n == 11:
                            transpose_x(u + 1)
                        if 13 <= n < 13 + 2 * NC:
                            project_in(u + 1, n - 13)
                        if n == 22:
                            project_bc(u + 1, 1 - p)
                        if n == 25:
                            project_dt(u + 1)
                        if n in PE_BC:
                            spread_bc(u + 1, PE_BC.index(n))
                    sum_states(u, n)
                if last:
                    project_out(u, True)

            units(pe, body)


def _mamba_arrays(f):
    import numpy as np

    def per_channel(t):
        return t.reshape(NL, NC, 128, -1).transpose(2, 0, 1, 3).reshape(128, NL, -1)

    pack = np.zeros((128, NL, NPACK), np.float32)
    at = 0
    for name in ("A_log", "D_skip", "conv_w", "conv_b", "dt_proj_b"):
        t = per_channel(f["L1_attn_" + name])
        pack[:, :, at:at + t.shape[2]] = t
        at += t.shape[2]
    for name in ("norm_w", "norm_b"):
        pack[:DH2, :, at:at + 2] = f["L1_attn_" + name].reshape(NL, 2, DH2).transpose(2, 0, 1)
        at += 2
    wx = np.zeros((NL, DI, 128), np.float32)
    xp = f["L1_attn_x_proj_w"].transpose(0, 2, 1)
    wx[:, :, :RANK] = xp[:, :, :RANK]
    for k in (32, 64, 96):
        wx[:, :, k:k + 2 * NS] = xp[:, :, RANK:]
    spread = np.zeros((128, 2 * NS, 128), mybir.dt.np(BF16))
    for s in range(2 * NS):
        spread[[32 + s, 64 + s, 96 + s], s, :] = 1
    return {
        "packs": pack, "spread": spread,
        "w_in": f["L1_attn_in_proj_w"].transpose(0, 2, 1).reshape(NL, 2, DH2, 2 * DI).transpose(0, 2, 1, 3),
        "w_x": wx.reshape(NL, NC, 128, 128).transpose(0, 2, 1, 3),
        "w_dt": f["L1_attn_dt_proj_w"].transpose(0, 2, 1),
        "w_out": f["L1_attn_out_proj_w"].transpose(0, 2, 1).reshape(NL, NC, 128, D).transpose(0, 2, 1, 3),
    }


def _host_arrays(x):
    import numpy as np
    f = {k: np.asarray(v) for k, v in x.items()}
    c = np.ascontiguousarray

    def chunks(w, p):
        return c(w.reshape(-1, p, w.shape[1]).transpose(1, 0, 2))

    img = f["x"].reshape(B, 3, 6, 16, 6, 16).transpose(1, 3, 5, 0, 2, 4).reshape(768, B * IMG)
    pos = np.arange(L, dtype=np.float32)
    inv = (np.float32(1.0) / np.float32(10000.0) ** (np.arange(0, DH, 2, dtype=np.float32) / np.float32(DH))).astype(np.float32)
    ang = (pos[:, None] * inv[None, :]).astype(np.float32)
    cos = np.concatenate([np.cos(ang), np.cos(ang)], -1)
    sin = np.concatenate([-np.sin(ang), np.sin(ang)], -1)
    scale = np.float32(DH ** -0.5)
    rope = np.stack([np.concatenate([np.tile(t * scale, (1, H)), np.tile(t, (1, H))], 1) for t in (cos, sin)])
    rope = rope.reshape(2, 2, HL, 2 * D).transpose(2, 0, 1, 3).astype(np.float32)
    lat = (np.arange(L) >= CTX).astype(np.float32)
    pad = np.zeros((L, 2 * H, 32), np.float32)
    pad[:, :H, DH] = ((1 - lat) * np.float32(-1e30))[:, None]
    pad[:, H:, DH] = lat[:, None]
    pad[:, H:, DH + 1] = -1
    pad = pad.reshape(2, HL, 2 * H, 32).transpose(1, 0, 2, 3)
    widths, ratios = (96, 144, 192), (2, 3, 4)
    rows = np.array([[(np.arange(HID) < r * e) for r in ratios] for e in widths], np.float32)
    cols = np.array([np.arange(D) < e for e in widths], np.float32)
    arrays = {
        "patches": chunks(img, 128), "tok_w": chunks(f["L0_tok_W"].T, 128), "tok_b": f["L0_tok_b"][None], "txt": f["txt"],
        "ident": np.eye(128, dtype=np.float32),
        "w_qkv": chunks(np.concatenate([f["L0_attn_Wq"], f["L0_attn_Wkv"]], 1), DH2), "rope": rope, "qk_pad": pad,
        "w_ctx": chunks(f["L0_attn_Wo_ctx"], DH2), "w_lat": chunks(f["L0_attn_Wo_lat"], DH2),
        "b_out": np.stack([f["L0_attn_bo_ctx"], f["L0_attn_bo_lat"]]), "kind": np.stack([1 - lat, lat]),
        "ln_g": f["L0_attn_ln_g"], "ln_b": f["L0_attn_ln_b"],
        "w_up1": chunks(f["L0_ffn_in_weight"].T, DH2), "b_up1": f["L0_ffn_in_bias"].reshape(HM, 128).T,
        "w_down1": chunks(f["L0_ffn_out_weight"], 128),
        "w_up2": chunks(f["L1_ffn_w_fc"].T, DH2), "b_up2": f["L1_ffn_b_fc"].reshape(HM, 128).T,
        "w_down2": chunks(f["L1_ffn_w_proj"].T, 128), "b_down2": f["L1_ffn_b_proj"][None],
        "alpha_e": f["L1_ffn_alpha_e"][:, None], "alpha_r": f["L1_ffn_alpha_r"], "mix_rows": rows, "mix_cols": cols,
        "one3": np.ones((3, 1), np.float32),
        **_mamba_arrays(f),
        "final_w": f["L1_attn_norm_f_w"], "final_b": f["L1_attn_norm_f_b"],
    }
    return {k: c(v) for k, v in arrays.items()}


def kernel(**inputs):
    import concourse.bacc as bacc
    from concourse import mybir
    from concourse.bass_utils import run_bass_kernel_spmd

    arrays = _host_arrays(inputs)
    nc = bacc.Bacc("TRN2", target_bir_lowering=False, num_devices=1)
    aps = {k: nc.dram_tensor("in_" + k, v.shape, mybir.dt.from_np(v.dtype), kind="ExternalInput").ap() for k, v in arrays.items()}
    out = nc.dram_tensor("out", (B, L, D), F32, kind="ExternalOutput").ap()
    build(nc, aps, out)
    r = run_bass_kernel_spmd(nc, [{"in_" + k: v for k, v in arrays.items()}], core_ids=[0])
    return r.results[0]["out"]
```

```python
from contextlib import ExitStack

import concourse.bass as bass
from concourse import mybir

F32 = mybir.dt.float32
BF16 = mybir.dt.bfloat16
ALU = mybir.AluOpType
ACT = mybir.ActivationFunctionType
AX = mybir.AxisListType

B = 8
IMG, TXT = 36, 128
L = IMG + TXT
HL = L // 2
NT = 2 * B
D = 192
DH2 = D // 2
PK = 768 // 128
H, DH = 12, 16
LAT = 32
CTX = L - LAT
HC, HR = 3, 4
HID = 768
HM = HID // 128
EPS = 1e-5
NL = 4
DI = 384
NC = DI // 128
NS = 16
TAPS = 4
RANK = 12
GB = 2
NG = B // GB
GT = 2 * GB
W = GB * L
UNITS = NL * NG
STEPS = NC * NS
P_A, P_D = 0, NC * NS
P_F = P_D + NC
P_CW, P_CB = 0, NC * TAPS
P_DTB = P_CB + NC
P_NW = P_DTB + NC
P_NB = P_NW + 2
NPF = P_NB + 2
NPACK = P_F + NPF


class Steps:

    def __init__(self, sem, names):
        self.sem = sem
        self.order = {name: k + 1 for k, name in enumerate(names)}
        assert len(self.order) == len(names)
        self.said = 0

    def next(self, name):
        assert self.order[name] == self.said % len(self.order) + 1, name
        self.said += 1
        return self.sem

    def at(self, turn, name):
        value = turn * len(self.order) + self.order[name]
        return max(value, 0) if isinstance(value, int) else value


def turns(eng, n, body, ahead=1):
    for turn in range(ahead):
        body(turn, turn == 0, False)
    with eng.Fori(ahead, n - 1) as turn:
        body(turn, False, False)
    body(n - 1, False, True)


def build(nc, a, out):
    with ExitStack() as ctx:
        def sb(name, shape, dt=F32, where=ctx):
            return where.enter_context(nc.sbuf_tensor(name, shape, dt))

        def sem(name):
            return ctx.enter_context(nc.semaphore(name))

        bank0 = ctx.enter_context(nc.psum_tensor("bank0", [128, 512], F32))
        two = ctx.enter_context(nc.psum_tensor("bank12", [128, 1024], F32))
        bank3 = ctx.enter_context(nc.psum_tensor("bank3", [128, 512], F32))
        pair = [ctx.enter_context(nc.psum_tensor(f"pair{k}", [128, 2, 512], F32)) for k in range(2)]
        bank = [bank0[:, :], two[:, 0:512], two[:, 512:1024], bank3[:, :]] + [pair[0][:, 0, :], pair[0][:, 1, :], pair[1][:, 0, :], pair[1][:, 1, :]]

        h = sb("h", [HL, NT, D])
        res = sb("res", [HL, NT, D])
        ident = sb("ident", [128, 128])
        ones = sb("ones", [1, HL])
        eps = sb("eps", [128, 1])
        s_base = sem("s_base")
        embed(nc, a, sb, sem, bank, h, ident, ones, eps, s_base)
        attention(nc, a, sb, sem, bank, h, ident, eps)
        mlp(nc, a, sb, sem, bank, pair, h, ident, ones, eps, 1, None)
        normalise(nc, a, sb, sem, h, res, eps, False)
        mamba(nc, a, sb, sem, bank, two, pair, res, ident, eps)
        normalise(nc, a, sb, sem, res, h, eps, True)
        mlp(nc, a, sb, sem, bank, pair, h, ident, ones, eps, 2, out)


def embed(nc, a, sb, sem, bank, h, ident, ones, eps, s_base):
    with ExitStack() as ctx, nc.Block() as block:
        patches = sb("patches", [128, PK, B * IMG], where=ctx)
        tok_w = sb("tok_w", [128, PK, D], where=ctx)
        tok_b = sb("tok_b", [1, D], where=ctx)
        s_load = sem("s_patches")
        s_txt = sem("s_txt")
        s_const = sem("s_const")
        s_img = sem("s_img")
        s_copied = sem("s_img_copied")

        @block.sync
        def _(sp):
            sp.dma_start(patches[:], a["patches"]).then_inc(s_load, 16)
            sp.dma_start(tok_w[:], a["tok_w"]).then_inc(s_load, 16)
            sp.dma_start(tok_b[:], a["tok_b"]).then_inc(s_load, 16)
            sp.dma_start(ident[:], a["ident"]).then_inc(s_base, 16)
            sp.dma_start(h[IMG:HL, 0:NT:2, :], a["txt"][:, 0:HL - IMG, :].rearrange("b t d -> t b d")).then_inc(s_txt, 16)
            sp.dma_start(h[:, 1:NT:2, :], a["txt"][:, HL - IMG:TXT, :].rearrange("b t d -> t b d")).then_inc(s_txt, 16)
            sp.wait_ge(s_txt, 32)
            sp.wait_ge(s_base, 16)

        @block.gpsimd
        def _(pool):
            pool.memset(ones[:], 1.0).then_inc(s_const, 1)
            pool.memset(eps[:], EPS).then_inc(s_const, 1)

        @block.tensor
        def _(pe):
            pe.wait_ge(s_load, 48)
            pe.wait_ge(s_const, 2)
            for b in range(B):
                o = bank[b // 2][0:IMG, (b % 2) * D:(b % 2 + 1) * D]
                for k in range(PK):
                    pe.matmul(o, patches[:, k, b * IMG:(b + 1) * IMG], tok_w[:, k, :], start=(k == 0), stop=False)
                pe.matmul(o, ones[:, 0:IMG], tok_b[:], start=False, stop=True).then_inc(s_img, 1)

        @block.vector
        def _(dve):
            for n in range(B // 2):
                dve.wait_ge(s_img, 2 * n + 2)
                for k in range(2):
                    dve.tensor_copy(h[0:IMG, 2 * (2 * n + k), :], bank[n][0:IMG, k * D:(k + 1) * D]).then_inc(s_copied, 1)


def attention(nc, a, sb, sem, bank, h, ident, eps):
    with ExitStack() as ctx, nc.Block() as block:
        w_qkv = sb("w_qkv", [DH2, 2, 2 * D], where=ctx)
        w_ctx = sb("w_ctx", [DH2, 2, D], where=ctx)
        w_lat = sb("w_lat", [DH2, 2, D], where=ctx)
        b_out = sb("b_out", [2, D], where=ctx)
        kind = sb("kind", [2, L], where=ctx)
        rope = sb("rope", [HL, 2, 2, 2 * D], where=ctx)
        gain = sb("gain", [HL, DH], where=ctx)
        shift = sb("shift", [HL, DH], where=ctx)
        stats = sb("a_stats", [HL, 2, 6], where=ctx)
        mv = sb("a_mv", [HL, 2, 2], where=ctx)
        vare = sb("a_vare", [HL, 2], where=ctx)
        minus_half = sb("a_minus_half", [HL, 2, H], where=ctx)
        spare = sb("a_spare", [HL, 1], where=ctx)
        rstd = sb("a_rstd", [HL, 2], where=ctx)
        xn = sb("a_xn", [HL, 2, D], where=ctx)
        xt = sb("a_xt", [DH2, 2, L], where=ctx)
        t_cos = sb("t_cos", [HL, 2, 2 * D], where=ctx)
        t_sin = sb("t_sin", [HL, 2, 2 * D], where=ctx)
        qk = sb("qk", [HL, 2, 2 * H, 32], where=ctx)
        qt = sb("qt", [128, HC, L], where=ctx)
        kt = sb("kt", [128, HC, L], where=ctx)
        mu = sb("k_mu", [HL, 2, H], where=ctx)
        var = sb("k_var", [HL, 2, H], where=ctx)
        krs = sb("k_rs", [HL, 2, H], where=ctx)
        kc = sb("k_c", [HL, 2, H, DH], where=ctx)
        ksq = sb("k_sq", [HL, 2, H, DH], where=ctx)
        v = sb("v", [HL, 2, H, DH + 1], where=ctx)
        pt = sb("pt", [HL, 2, HR, HC * L], where=ctx)
        rsum = sb("rsum", [HL, 2, H, 1], where=ctx)
        o = sb("o", [HL, 2, H, DH], where=ctx)
        ot_ctx = sb("ot_ctx", [DH2, 2, L], where=ctx)
        ot_lat = sb("ot_lat", [DH2, 2, L], where=ctx)

        s_load = sem("s_attn_load")
        s_zero = sem("s_attn_zero")
        s_half = sem("s_attn_half")
        dve_a = Steps(sem("dve_project"), ["stats", "aggr", "vare", "xn", "cos0", "sin0", "rope0", "cos1", "sin1", "rope1", "ksum", "kmu",
                                           "kvar", "kvare"])
        act_a = Steps(sem("act_project"), ["xt", "qt", "kt"])
        pe_a = Steps(sem("pe_project"), ["xt", "qkv0", "qkv1", "qt", "kt"])
        pool_a = Steps(sem("pool_project"), ["rstd", "kc", "ksq", "krs", "kn", "kg"])
        pool_v = Steps(sem("pool_values"), ["v"])
        dve_c = Steps(sem("dve_scores"), [f"max{n}" for n in range(8)])
        act_c = Steps(sem("act_scores"), ["qt"] + [f"exp{n}" for n in range(8)])
        pe_c = Steps(sem("pe_scores"), [f"s{n}" for n in range(8)] + ["qt"] + [f"p{n}" for n in range(8)])
        dve_t = Steps(sem("dve_output"), ["recip", "o", "add"])
        act_t = Steps(sem("act_output"), ["ot"])
        pe_t = Steps(sem("pe_output"), ["pv", "ot", "out"])
        n_loads = 9

        @block.sync
        def _(sp):
            for dst, name in ((w_qkv, "w_qkv"), (rope, "rope"), (qk, "qk_pad"), (w_ctx, "w_ctx"), (w_lat, "w_lat"),
                              (b_out, "b_out"), (kind, "kind")):
                sp.dma_start(dst[:], a[name]).then_inc(s_load, 16)
            sp.dma_start(gain[:], a["ln_g"].partition_broadcast(HL)).then_inc(s_load, 16)
            sp.dma_start(shift[:], a["ln_b"].partition_broadcast(HL)).then_inc(s_load, 16)

        @block.vector
        def _(dve):
            def stats_of(b):
                for j in range(2):
                    last = dve.bn_stats(stats[:, j, :], h[:, 2 * b + j, :])
                last.then_inc(dve_a.next("stats"), 1)
                dve.wait_ge(dve_a.sem, dve_a.at(b, "stats"))
                dve.memset(spare[:], 0.0)
                for j in range(2):
                    last = dve.bn_aggr(mv[:, j, :], stats[:, j, :])
                last.then_inc(dve_a.next("aggr"), 1)
                dve.wait_ge(dve_a.sem, dve_a.at(b, "aggr"))
                dve.wait_ge(pool_a.sem, pool_a.at(b - 1, "rstd"))
                dve.tensor_scalar(vare[:], mv[:, :, 1], EPS, None, ALU.add).then_inc(dve_a.next("vare"), 1)

            def normalised(b):
                dve.wait_ge(pool_a.sem, pool_a.at(b, "rstd"))
                dve.wait_ge(pe_a.sem, pe_a.at(b - 1, "xt"))
                for j in range(2):
                    last = dve.tensor_scalar(xn[:, j, :], h[:, 2 * b + j, :], mv[:, j, 0:1], rstd[:, j:j + 1], ALU.subtract, ALU.mult)
                last.then_inc(dve_a.next("xn"), 1)

            def rotate(b):
                for j in range(2):
                    src = bank[5 - j][0:HL, 0:2 * D]
                    dve.wait_ge(pe_a.sem, pe_a.at(b, f"qkv{j}"))
                    dve.tensor_tensor(t_cos[:, j, :], src, rope[:, 0, j, :], ALU.mult).then_inc(dve_a.next(f"cos{j}"), 1)
                    half = "p (h u e) -> p h u e"
                    x = src.rearrange(half, u=2, e=DH // 2)
                    s = rope[:, 1, j, :].rearrange(half, u=2, e=DH // 2)
                    y = t_sin[:, j, :].rearrange(half, u=2, e=DH // 2)
                    dve.tensor_tensor(y[:, :, 0, :], x[:, :, 1, :], s[:, :, 0, :], ALU.mult)
                    dve.tensor_tensor(y[:, :, 1, :], x[:, :, 0, :], s[:, :, 1, :], ALU.mult).then_inc(dve_a.next(f"sin{j}"), 1)
                    dve.wait_ge(dve_a.sem, dve_a.at(b, f"sin{j}"))
                    dve.wait_ge(pe_c.sem, pe_c.at(b - 1, "qt"))
                    if j == 0:
                        dve.wait_ge(pool_a.sem, pool_a.at(b - 1, "kc"))
                    dve.tensor_tensor(qk[:, j, :, 0:DH], t_cos[:, j, :].rearrange("p (h e) -> p h e", e=DH),
                                                 t_sin[:, j, :].rearrange("p (h e) -> p h e", e=DH), ALU.add).then_inc(dve_a.next(f"rope{j}"), 1)
                dve.wait_ge(dve_a.sem, dve_a.at(b, "rope1"))
                dve.wait_ge(pool_a.sem, pool_a.at(b - 1, "kc"))
                dve.tensor_reduce(mu[:], qk[:, :, H:2 * H, 0:DH], AX.X, ALU.add).then_inc(dve_a.next("ksum"), 1)
                dve.wait_ge(dve_a.sem, dve_a.at(b, "ksum"))
                dve.tensor_scalar(mu[:], mu[:], 1.0 / DH, None, ALU.mult).then_inc(dve_a.next("kmu"), 1)

            def variance(b):
                dve.wait_ge(pool_a.sem, pool_a.at(b, "ksq"))
                dve.tensor_reduce(var[:], ksq[:], AX.X, ALU.add).then_inc(dve_a.next("kvar"), 1)
                dve.wait_ge(dve_a.sem, dve_a.at(b, "kvar"))
                dve.tensor_scalar(var[:], var[:], 1.0 / DH, EPS, ALU.mult, ALU.add).then_inc(dve_a.next("kvare"), 1)

            def maxima(b, groups):
                for n in groups:
                    j, r = divmod(n, HR)
                    dve.wait_ge(pe_c.sem, pe_c.at(b, f"s{n}"))
                    dve.tensor_reduce(qk[:, j, r:H:HR, DH + 1], bank[n % 4][0:HL, 0:HC * L].rearrange("p (c k) -> p c k", c=HC),
                                      AX.X, ALU.max).then_inc(dve_c.next(f"max{n}"), 1)

            def weigh(b):
                pv = bank[6][0:HL, 0:2 * H * (DH + 1)].rearrange("p (j h e) -> p j h e", j=2, h=H)
                dve.wait_ge(pe_t.sem, pe_t.at(b, "pv"))
                dve.reciprocal(rsum[:], pv[:, :, :, DH:DH + 1]).then_inc(dve_t.next("recip"), 1)
                dve.wait_ge(dve_t.sem, dve_t.at(b, "recip"))
                dve.wait_ge(pe_t.sem, pe_t.at(b - 1, "ot"))
                dve.tensor_tensor(o[:], pv[:, :, :, 0:DH], rsum[:].to_broadcast([HL, 2, H, DH]), ALU.mult).then_inc(dve_t.next("o"), 1)

            def add(b):
                dve.wait_ge(pe_t.sem, pe_t.at(b, "out"))
                t = h[:, bass.ds(2 * b, 2), :].rearrange("p t d -> p (t d)")
                dve.tensor_tensor(t, t, bank[6][0:HL, 0:2 * D], ALU.add).then_inc(dve_t.next("add"), 1)

            dve.memset(v[:], 1.0)
            dve.memset(ot_ctx[:], 0.0)
            dve.memset(ot_lat[:], 0.0).then_inc(s_zero, 1)
            stats_of(0)
            normalised(0)
            dve.wait_ge(s_load, 16 * n_loads)
            rotate(0)
            variance(0)

            def body(b, first, last):
                if not last:
                    stats_of(b + 1)
                maxima(b, range(4))
                if not last:
                    normalised(b + 1)
                maxima(b, range(4, 8))
                if not first:
                    weigh(b - 1)
                if not last:
                    rotate(b + 1)
                if not first:
                    add(b - 1)
                if not last:
                    variance(b + 1)
                if last:
                    weigh(b)
                    add(b)

            turns(dve, B, body, 2)

        @block.gpsimd
        def _(pool):
            def rstd_of(b):
                pool.wait_ge(dve_a.sem, dve_a.at(b, "vare"))
                pool.wait_ge(dve_a.sem, dve_a.at(b - 1, "xn"))
                pool.tensor_tensor(rstd[:], vare[:], minus_half[:, 0, 0:2], ALU.pow).then_inc(pool_a.next("rstd"), 1)

            def each(t):
                return t.unsqueeze(3).to_broadcast([HL, 2, H, DH])

            def all_heads(t):
                return t.unsqueeze(1).unsqueeze(1).to_broadcast([HL, 2, H, DH])

            def norm_keys(b):
                pool.wait_ge(dve_a.sem, dve_a.at(b, "kmu"))
                pool.wait_ge(pool_v.sem, pool_v.at(b - 1, "v"))
                pool.tensor_tensor(kc[:], qk[:, :, H:2 * H, 0:DH], each(mu[:]), ALU.subtract).then_inc(pool_a.next("kc"), 1)
                pool.wait_ge(pool_a.sem, pool_a.at(b, "kc"))
                pool.wait_ge(dve_a.sem, dve_a.at(b - 1, "kvar"))
                pool.tensor_tensor(ksq[:], kc[:], kc[:], ALU.mult).then_inc(pool_a.next("ksq"), 1)
                pool.wait_ge(dve_a.sem, dve_a.at(b, "kvare"))
                pool.tensor_tensor(krs[:], var[:], minus_half[:], ALU.pow).then_inc(pool_a.next("krs"), 1)
                pool.wait_ge(pool_a.sem, pool_a.at(b, "krs"))
                pool.tensor_tensor(kc[:], kc[:], each(krs[:]), ALU.mult).then_inc(pool_a.next("kn"), 1)
                pool.wait_ge(pool_a.sem, pool_a.at(b, "kn"))
                pool.tensor_tensor(kc[:], kc[:], all_heads(gain[:]), ALU.mult).then_inc(pool_a.next("kg"), 1)

            def values(b):
                pool.wait_ge(pool_a.sem, pool_a.at(b, "kg"))
                pool.wait_ge(pe_t.sem, pe_t.at(b - 1, "pv"))
                pool.tensor_tensor(v[:, :, :, 0:DH], kc[:], all_heads(shift[:]), ALU.add).then_inc(pool_v.next("v"), 1)

            pool.memset(minus_half[:], -0.5).then_inc(s_half, 1)
            pool.wait_ge(s_half, 1)
            rstd_of(0)
            pool.wait_ge(s_load, 16 * n_loads)
            pool.wait_ge(s_zero, 1)
            norm_keys(0)

            def body(b, first, last):
                if not last:
                    rstd_of(b + 1)
                values(b)
                if not last:
                    norm_keys(b + 1)

            turns(pool, B, body, 2)

        @block.scalar
        def _(act):
            def copy_xt(b):
                act.wait_ge(pe_a.sem, pe_a.at(b, "xt"))
                act.activation(xt[:], bank[4][0:DH2, 0:2 * L].rearrange("p (k l) -> p k l", k=2), ACT.Copy).then_inc(act_a.next("xt"), 1)

            def copy_qkt(b):
                act.wait_ge(pe_a.sem, pe_a.at(b, "qt"))
                act.activation(qt[:], bank[4][:, 0:HC * L].rearrange("p (c l) -> p c l", c=HC), ACT.Copy).then_inc(act_a.next("qt"), 1)
                act.wait_ge(pe_a.sem, pe_a.at(b, "kt"))
                act.activation(kt[:], bank[5][:, 0:HC * L].rearrange("p (c l) -> p c l", c=HC), ACT.Copy).then_inc(act_a.next("kt"), 1)

            def copy_q_with_max(b):
                act.wait_ge(pe_c.sem, pe_c.at(b, "qt"))
                act.activation(qt[:], bank[7][:, 0:HC * L].rearrange("p (c l) -> p c l", c=HC), ACT.Copy).then_inc(act_c.next("qt"), 1)

            def exps(b):
                act.wait_ge(pe_t.sem, pe_t.at(b - 1, "pv"))
                for n in range(8):
                    kj, r = divmod(n, HR)
                    act.wait_ge(pe_c.sem, pe_c.at(b, f"p{n}"))
                    act.activation(pt[:, kj, r, :], bank[n % 4][0:HL, 0:HC * L], ACT.Exp).then_inc(act_c.next(f"exp{n}"), 1)

            def copy_ot(b):
                act.wait_ge(pe_t.sem, pe_t.at(b, "ot"))
                act.wait_ge(pe_t.sem, pe_t.at(b - 1, "out"))
                src = bank[7][0:DH2, 0:2 * L].rearrange("p (k l) -> p k l", k=2)
                act.activation(ot_ctx[:, :, 0:CTX], src[:, :, 0:CTX], ACT.Copy)
                act.activation(ot_lat[:, :, CTX:L], src[:, :, CTX:L], ACT.Copy).then_inc(act_t.next("ot"), 1)

            act.wait_ge(s_zero, 1)
            copy_xt(0)
            copy_qkt(0)

            def body(b, first, last):
                copy_q_with_max(b)
                if not last:
                    copy_xt(b + 1)
                if not first:
                    copy_ot(b - 1)
                exps(b)
                if not last:
                    copy_qkt(b + 1)
                if last:
                    copy_ot(b)

            turns(act, B, body, 2)

        @block.tensor
        def _(pe):
            def transpose_x(b):
                pe.wait_ge(dve_a.sem, dve_a.at(b, "xn"))
                pe.wait_ge(dve_a.sem, dve_a.at(b - 1, "sin1"))
                pe.wait_ge(act_a.sem, act_a.at(b - 1, "qt"))
                for k in range(2):
                    for j in range(2):
                        last = pe.transpose(bank[4][0:DH2, k * L + j * HL:k * L + (j + 1) * HL], xn[:, j, k * DH2:(k + 1) * DH2], ident[0:HL, 0:HL])
                last.then_inc(pe_a.next("xt"), 1)

            def project(b):
                pe.wait_ge(act_a.sem, act_a.at(b, "xt"))
                pe.wait_ge(act_a.sem, act_a.at(b - 1, "kt"))
                for j in range(2):
                    for k in range(2):
                        last = pe.matmul(bank[5 - j][0:HL, 0:2 * D], xt[:, k, j * HL:(j + 1) * HL], w_qkv[:, k, :], start=(k == 0), stop=(k == 1))
                    last.then_inc(pe_a.next(f"qkv{j}"), 1)

            def transpose_heads(dst, first_head):
                for j in range(2):
                    for c in range(HC):
                        src = qk[:, j, first_head + HR * c:first_head + HR * (c + 1), :].rearrange("p h e -> p (h e)")
                        last = pe.transpose(dst[:, c * L + j * HL:c * L + (j + 1) * HL], src, ident[0:HL, 0:HL])
                return last

            def transpose_qk(b):
                pe.wait_ge(dve_a.sem, dve_a.at(b, "rope1"))
                transpose_heads(bank[4], 0).then_inc(pe_a.next("qt"), 1)
                transpose_heads(bank[5], H).then_inc(pe_a.next("kt"), 1)

            def scores(b):
                pe.wait_ge(act_a.sem, act_a.at(b, "kt"))
                for n in range(8):
                    j, r = divmod(n, HR)
                    if n < 4:
                        pe.wait_ge(act_c.sem, act_c.at(b - 1, f"exp{n + 4}"))
                    else:
                        pe.wait_ge(dve_c.sem, dve_c.at(b, f"max{n - 4}"))
                    rows = slice(32 * r, 32 * r + DH + 1)
                    for c in range(HC):
                        last = pe.matmul(bank[n % 4][0:HL, c * L:(c + 1) * L], qt[rows, c, j * HL:(j + 1) * HL], kt[rows, c, :],
                                         start=True, stop=True)
                    last.then_inc(pe_c.next(f"s{n}"), 1)

            def transpose_q_with_max(b):
                pe.wait_ge(dve_c.sem, dve_c.at(b, "max7"))
                pe.wait_ge(act_t.sem, act_t.at(b - 2, "ot"))
                transpose_heads(bank[7], 0).then_inc(pe_c.next("qt"), 1)

            def shifted_scores(b, groups):
                pe.wait_ge(act_c.sem, act_c.at(b, "qt"))
                for n in groups:
                    j, r = divmod(n, HR)
                    if n >= 4:
                        pe.wait_ge(act_c.sem, act_c.at(b, f"exp{n - 4}"))
                    rows = slice(32 * r, 32 * r + DH + 2)
                    for c in range(HC):
                        last = pe.matmul(bank[n % 4][0:HL, c * L:(c + 1) * L], kt[rows, c, j * HL:(j + 1) * HL], qt[rows, c, :],
                                         start=True, stop=True)
                    last.then_inc(pe_c.next(f"p{n}"), 1)

            def weigh_values(b):
                pe.wait_ge(act_c.sem, act_c.at(b, "exp7"))
                pe.wait_ge(pool_v.sem, pool_v.at(b, "v"))
                pe.wait_ge(dve_t.sem, dve_t.at(b - 1, "add"))
                for j in range(2):
                    for hd in range(H):
                        c, r = divmod(hd, HR)
                        at = (j * H + hd) * (DH + 1)
                        for kj in range(2):
                            last = pe.matmul(bank[6][0:HL, at:at + DH + 1], pt[:, kj, r, c * L + j * HL:c * L + (j + 1) * HL],
                                             v[:, kj, hd, :], start=(kj == 0), stop=(kj == 1))
                last.then_inc(pe_t.next("pv"), 1)

            def transpose_o(b, last_batch):
                pe.wait_ge(dve_t.sem, dve_t.at(b, "o"))
                if not last_batch:
                    pe.wait_ge(act_c.sem, act_c.at(b + 1, "qt"))
                for k in range(2):
                    for j in range(2):
                        src = o[:, j, :, :].rearrange("p h e -> p (h e)")[:, k * DH2:(k + 1) * DH2]
                        last = pe.transpose(bank[7][0:DH2, k * L + j * HL:k * L + (j + 1) * HL], src, ident[0:HL, 0:HL])
                last.then_inc(pe_t.next("ot"), 1)

            def project_out(b):
                pe.wait_ge(act_t.sem, act_t.at(b, "ot"))
                for j in range(2):
                    dst = bank[6][0:HL, j * D:(j + 1) * D]
                    cols = slice(j * HL, (j + 1) * HL)
                    pe.matmul(dst, kind[:, cols], b_out[:], start=True, stop=False)
                    for t, w in ((ot_ctx, w_ctx), (ot_lat, w_lat)):
                        for k in range(2):
                            last = pe.matmul(dst, t[:, k, cols], w[:, k, :], start=False, stop=(t is ot_lat and k == 1))
                last.then_inc(pe_t.next("out"), 1)

            pe.wait_ge(s_load, 16 * n_loads)
            transpose_x(0)
            project(0)
            transpose_qk(0)

            def body(b, first, last):
                scores(b)
                if not first:
                    weigh_values(b - 1)
                transpose_q_with_max(b)
                if not last:
                    transpose_x(b + 1)
                if not first:
                    transpose_o(b - 1, False)
                shifted_scores(b, range(4))
                if not last:
                    project(b + 1)
                if not first:
                    project_out(b - 1)
                shifted_scores(b, range(4, 8))
                if not last:
                    transpose_qk(b + 1)
                if last:
                    weigh_values(b)
                    transpose_o(b, True)
                    project_out(b)

            turns(pe, B, body, 2)


def mlp(nc, a, sb, sem, bank, pair, h, ident, ones, eps, which, out):
    mixed = which == 2
    n = f"m{which}_"
    with ExitStack() as ctx, nc.Block() as block:
        w_up = sb(n + "w_up", [DH2, 2, HID], where=ctx)
        b_up = sb(n + "b_up", [128, HM], where=ctx)
        w_down = sb(n + "w_down", [128, HM, D], where=ctx)
        stats = sb(n + "stats", [HL, GT, 6], where=ctx)
        mv = sb(n + "mv", [HL, GT, 2], where=ctx)
        lv = sb(n + "lv", [HL, GT], where=ctx)
        spare = sb(n + "spare", [HL, 1], where=ctx)
        rstd = sb(n + "rstd", [HL, GT], where=ctx)
        xn = sb(n + "xn", [HL, GT, D], where=ctx)
        xt = sb(n + "xt", [DH2, 2, W], where=ctx)
        act_out = sb(n + "hidden", [128, HM, W], where=ctx)
        s_load = sem(n + "s_load")
        s_stats = sem(n + "dve_stats")
        s_stored = sem(n + "s_stored")
        dve_s = Steps(sem(n + "dve"), ["aggr", "xn"])
        s_add = Steps(sem(n + "dve_add"), ["add"])
        act_s = Steps(sem(n + "act_norm"), ["lv", "rstd", "xt"])
        act_g = Steps(sem(n + "act_gelu"), [f"g{m}" for m in range(HM)])
        pe_x = Steps(sem(n + "pe_xt"), ["xt"])
        pe_s = Steps(sem(n + "pe"), [f"up{m}" for m in range(HM)] + ["down"])
        n_loads = 3
        if mixed:
            b_down = sb("b_down", [1, D], where=ctx)
            alpha_e = sb("alpha_e", [3, 1], where=ctx)
            alpha_r = sb("alpha_r", [3, 3], where=ctx)
            rows = sb("mix_rows", [3, 3, HID], where=ctx)
            cols = sb("mix_cols", [3, D], where=ctx)
            one3 = sb("one3", [3, 1], where=ctx)
            coef = sb("mix_coef", [3, HID], where=ctx)
            sum_r = sb("mix_sum", [3, 2], where=ctx)
            n_loads += 6
            s_mix = Steps(sem("dve_mix"), ["c0", "c1", "c2", "coef", "sum", "esum", "b_up", "b_down", "w"])
            s_mixed = Steps(sem("pe_mix"), ["b", "up0", "up1", "down0", "down1", "down2"])

        @block.sync
        def _(sp):
            for dst, name in ((w_up, "w_up"), (b_up, "b_up"), (w_down, "w_down")):
                sp.dma_start(dst[:], a[f"{name}{which}"]).then_inc(s_load, 16)
            if mixed:
                for dst, name in ((b_down, "b_down2"), (alpha_e, "alpha_e"), (rows, "mix_rows"), (cols, "mix_cols"), (one3, "one3")):
                    sp.dma_start(dst[:], a[name]).then_inc(s_load, 16)
                sp.dma_start(alpha_r[:], a["alpha_r"].partition_broadcast(3)).then_inc(s_load, 16)
                out_v = out.rearrange("b (j p) d -> p (b j) d", j=2)
                for q in range(NG):
                    sp.wait_ge(s_add.sem, s_add.at(q, "add"))
                    sp.dma_start(out_v[:, bass.ds(GT * q, GT), :], h[:, bass.ds(GT * q, GT), :]).then_inc(s_stored, 16)
                sp.wait_ge(s_stored, 16 * NG)

        @block.vector
        def _(dve):
            def norm(q):
                for t in range(GT):
                    last = dve.bn_stats(stats[:, t, :], h[:, GT * q + t, :])
                last.then_inc(s_stats, 1)
                dve.wait_ge(s_stats, 1 * q + 1)
                dve.wait_ge(act_s.sem, act_s.at(q - 1, "lv"))
                dve.memset(spare[:], 0.0)
                for t in range(GT):
                    last = dve.bn_aggr(mv[:, t, :], stats[:, t, :])
                last.then_inc(dve_s.next("aggr"), 1)
                dve.wait_ge(act_s.sem, act_s.at(q, "rstd"))
                dve.wait_ge(pe_x.sem, pe_x.at(q - 1, "xt"))
                for t in range(GT):
                    last = dve.tensor_scalar(xn[:, t, :], h[:, GT * q + t, :], mv[:, t, 0:1], rstd[:, t:t + 1], ALU.subtract, ALU.mult)
                last.then_inc(dve_s.next("xn"), 1)

            def add(q):
                dve.wait_ge(pe_s.sem, pe_s.at(q, "down"))
                t = h[:, bass.ds(GT * q, GT), :].rearrange("p (k t) d -> p k (t d)", k=2)
                dve.tensor_tensor(t, t, pair[1][0:HL, :, 0:2 * D], ALU.add).then_inc(s_add.next("add"), 1)

            if mixed:
                dve.wait_ge(s_load, 16 * n_loads)
                dve.tensor_scalar(coef[:], rows[:, 0, :], alpha_r[:, 0:1], None, ALU.mult).then_inc(s_mix.next("c0"), 1)
                for j in range(1, 3):
                    dve.wait_ge(s_mix.sem, s_mix.at(0, f"c{j - 1}"))
                    dve.scalar_tensor_tensor(coef[:], rows[:, j, :], alpha_r[:, j:j + 1], coef[:], ALU.mult, ALU.add).then_inc(s_mix.next(f"c{j}"), 1)
                dve.wait_ge(s_mix.sem, s_mix.at(0, "c2"))
                dve.tensor_scalar(coef[:], coef[:], alpha_e[:, 0:1], None, ALU.mult).then_inc(s_mix.next("coef"), 1)
                dve.tensor_reduce(sum_r[:, 0:1], alpha_r[:], AX.X, ALU.add).then_inc(s_mix.next("sum"), 1)
                dve.wait_ge(s_mix.sem, s_mix.at(0, "sum"))
                dve.tensor_scalar(sum_r[:, 1:2], sum_r[:, 0:1], alpha_e[:, 0:1], None, ALU.mult).then_inc(s_mix.next("esum"), 1)
                dve.wait_ge(s_mixed.sem, s_mixed.at(0, "b"))
                dve.tensor_tensor(b_up[:], b_up[:], bank[0][:, 0:HM], ALU.mult).then_inc(s_mix.next("b_up"), 1)
                dve.tensor_tensor(b_down[:], b_down[:], bank[0][0:1, 64:64 + D], ALU.mult).then_inc(s_mix.next("b_down"), 1)
                for k in range(2):
                    dve.wait_ge(s_mixed.sem, s_mixed.at(0, f"up{k}"))
                    for half in range(2):
                        part = w_up[:, k, half * DI:(half + 1) * DI]
                        dve.tensor_tensor(part, part, pair[k][0:DH2, half, 0:DI], ALU.mult)
                for k in range(3):
                    dve.wait_ge(s_mixed.sem, s_mixed.at(0, f"down{k}"))
                    part = w_down[:, 2 * k:2 * k + 2, :].rearrange("p m d -> p (m d)")
                    last = dve.tensor_tensor(part, part, bank[1 + k][:, 0:2 * D], ALU.mult)
                last.then_inc(s_mix.next("w"), 1)
            norm(0)

            def body(q, first, last):
                if not last:
                    norm(q + 1)
                add(q)

            turns(dve, NG, body)

        @block.scalar
        def _(act):
            def norm(q):
                act.wait_ge(dve_s.sem, dve_s.at(q, "aggr"))
                act.wait_ge(dve_s.sem, dve_s.at(q - 1, "xn"))
                act.activation(lv[:], mv[:, :, 1], ACT.Ln, bias=eps[0:HL, :]).then_inc(act_s.next("lv"), 1)
                act.wait_ge(act_s.sem, act_s.at(q, "lv"))
                act.activation(rstd[:], lv[:], ACT.Exp, scale=-0.5).then_inc(act_s.next("rstd"), 1)

            def copy_xt(q):
                act.wait_ge(pe_x.sem, pe_x.at(q, "xt"))
                act.wait_ge(pe_s.sem, pe_s.at(q - 1, f"up{HM - 1}"))
                act.activation(xt[:], pair[0][0:DH2, :, 0:W], ACT.Copy).then_inc(act_s.next("xt"), 1)

            norm(0)
            copy_xt(0)
            act.wait_ge(s_load, 16 * n_loads)
            if mixed:
                act.wait_ge(s_mix.sem, s_mix.at(0, "w"))

            def body(q, first, last):
                if not last:
                    norm(q + 1)
                act.wait_ge(pe_s.sem, pe_s.at(q - 1, "down"))
                for m in range(HM):
                    act.wait_ge(pe_s.sem, pe_s.at(q, f"up{m}"))
                    act.activation(act_out[:, m, :], bank[m % 4][:, 0:W], ACT.Gelu_apprx_tanh if mixed else ACT.Gelu,
                                              bias=b_up[:, m:m + 1]).then_inc(act_g.next(f"g{m}"), 1)
                if not last:
                    copy_xt(q + 1)

            turns(act, NG, body)

        @block.tensor
        def _(pe):
            def transpose_x(q):
                pe.wait_ge(dve_s.sem, dve_s.at(q, "xn"))
                pe.wait_ge(act_s.sem, act_s.at(q - 1, "xt"))
                for k in range(2):
                    for t in range(GT):
                        last = pe.transpose(pair[0][0:DH2, k, t * HL:(t + 1) * HL], xn[:, t, k * DH2:(k + 1) * DH2], ident[0:HL, 0:HL])
                last.then_inc(pe_x.next("xt"), 1)

            pe.wait_ge(s_load, 16 * n_loads)
            if mixed:
                pe.wait_ge(s_mix.sem, s_mix.at(0, "esum"))
                for m in range(HM):
                    pe.matmul(bank[0][:, m:m + 1], coef[:, m * 128:(m + 1) * 128], one3[:], start=True, stop=True)
                pe.matmul(bank[0][0:1, 64:64 + D], sum_r[:, 1:2], cols[:], start=True, stop=True).then_inc(s_mixed.next("b"), 1)
                for k in range(2):
                    for half in range(2):
                        last = pe.matmul(pair[k][0:DH2, half, 0:DI], cols[:, k * DH2:(k + 1) * DH2], coef[:, half * DI:(half + 1) * DI], start=True, stop=True)
                    last.then_inc(s_mixed.next(f"up{k}"), 1)
                for k in range(3):
                    for m in range(2):
                        last = pe.matmul(bank[1 + k][:, m * D:(m + 1) * D], coef[:, (2 * k + m) * 128:(2 * k + m + 1) * 128], cols[:], start=True, stop=True)
                    last.then_inc(s_mixed.next(f"down{k}"), 1)
                pe.wait_ge(s_mix.sem, s_mix.at(0, "w"))
            transpose_x(0)

            def body(q, first, last):
                pe.wait_ge(act_s.sem, act_s.at(q, "xt"))
                for m in range(HM):
                    if m < 4:
                        pe.wait_ge(act_g.sem, act_g.at(q - 1, f"g{m + 4 if m + 4 < HM else m}"))
                    else:
                        pe.wait_ge(act_g.sem, act_g.at(q, f"g{m - 4}"))
                    for k in range(2):
                        last_mm = pe.matmul(bank[m % 4][:, 0:W], w_up[:, k, m * 128:(m + 1) * 128], xt[:, k, :], start=(k == 0), stop=(k == 1))
                    last_mm.then_inc(pe_s.next(f"up{m}"), 1)
                if not last:
                    transpose_x(q + 1)
                pe.wait_ge(s_add.sem, s_add.at(q - 1, "add"))
                pe.wait_ge(act_g.sem, act_g.at(q, f"g{HM - 1}"))
                for t in range(GT):
                    dst = pair[1][0:HL, t // 2, (t % 2) * D:(t % 2 + 1) * D]
                    for m in range(HM):
                        last_mm = pe.matmul(dst, act_out[:, m, t * HL:(t + 1) * HL], w_down[:, m, :], start=(m == 0), stop=(m == HM - 1 and not mixed))
                    if mixed:
                        last_mm = pe.matmul(dst, ones[:], b_down[:], start=False, stop=True)
                last_mm.then_inc(pe_s.next("down"), 1)

            turns(pe, NG, body)


def normalise(nc, a, sb, sem, src, dst, eps, final):
    n = "nf_" if final else "n0_"
    with ExitStack() as ctx, nc.Block() as block:
        stats = sb(n + "stats", [HL, GT, 6], where=ctx)
        mv = sb(n + "mv", [HL, GT, 2], where=ctx)
        lv = sb(n + "lv", [HL, GT], where=ctx)
        spare = sb(n + "spare", [HL, 1], where=ctx)
        rstd = sb(n + "rstd", [HL, GT], where=ctx)
        s_dve = Steps(sem(n + "dve"), ["stats", "aggr", "xn"] + (["w", "b", "add"] if final else []))
        s_act = Steps(sem(n + "act"), ["lv", "rstd"])
        if final:
            s_load = sem("s_final_load")
            fw = sb("final_w", [HL, D], where=ctx)
            fb = sb("final_b", [HL, D], where=ctx)
            xn = sb("final_xn", [HL, GT, D], where=ctx)

            @block.sync
            def _(sp):
                sp.dma_start(fw[:], a["final_w"].partition_broadcast(HL)).then_inc(s_load, 16)
                sp.dma_start(fb[:], a["final_b"].partition_broadcast(HL)).then_inc(s_load, 16)

        @block.vector
        def _(dve):
            def body(q, first, last):
                for t in range(GT):
                    ins = dve.bn_stats(stats[:, t, :], src[:, GT * q + t, :])
                ins.then_inc(s_dve.next("stats"), 1)
                dve.wait_ge(s_dve.sem, s_dve.at(q, "stats"))
                dve.memset(spare[:], 0.0)
                for t in range(GT):
                    ins = dve.bn_aggr(mv[:, t, :], stats[:, t, :])
                ins.then_inc(s_dve.next("aggr"), 1)
                dve.wait_ge(s_act.sem, s_act.at(q, "rstd"))
                for t in range(GT):
                    to = xn[:, t, :] if final else dst[:, GT * q + t, :]
                    ins = dve.tensor_scalar(to, src[:, GT * q + t, :], mv[:, t, 0:1], rstd[:, t:t + 1], ALU.subtract, ALU.mult)
                ins.then_inc(s_dve.next("xn"), 1)
                if final:
                    dve.wait_ge(s_dve.sem, s_dve.at(q, "xn"))
                    dve.tensor_tensor(xn[:], xn[:], fw[:].unsqueeze(1).to_broadcast([HL, GT, D]), ALU.mult).then_inc(s_dve.next("w"), 1)
                    dve.wait_ge(s_dve.sem, s_dve.at(q, "w"))
                    dve.tensor_tensor(xn[:], xn[:], fb[:].unsqueeze(1).to_broadcast([HL, GT, D]), ALU.add).then_inc(s_dve.next("b"), 1)
                    dve.wait_ge(s_dve.sem, s_dve.at(q, "b"))
                    to = dst[:, bass.ds(GT * q, GT), :]
                    dve.tensor_tensor(to, to, xn[:], ALU.add).then_inc(s_dve.next("add"), 1)

            if final:
                dve.wait_ge(s_load, 32)
            turns(dve, NG, body)

        @block.scalar
        def _(act):
            def body(q, first, last):
                act.wait_ge(s_dve.sem, s_dve.at(q, "aggr"))
                act.activation(lv[:], mv[:, :, 1], ACT.Ln, bias=eps[0:HL, :]).then_inc(s_act.next("lv"), 1)
                act.wait_ge(s_act.sem, s_act.at(q, "lv"))
                act.activation(rstd[:], lv[:], ACT.Exp, scale=-0.5).then_inc(s_act.next("rstd"), 1)

            turns(act, NG, body)


def mamba(nc, a, sb, sem, bank, two, pair, res, ident, eps):
    with ExitStack() as ctx, nc.Block() as block:
        packs = sb("packs", [128, NL, NPACK], where=ctx)
        w_in = sb("w_in", [DH2, 2, 2 * DI], where=ctx)
        w_x = sb("w_x", [128, NC, 128], where=ctx)
        w_dt = sb("w_dt", [RANK, DI], where=ctx)
        w_out = sb("w_out", [128, NC, D], where=ctx)
        spread = sb("spread", [128, 2 * NS, 128], BF16, where=ctx)
        pf = sb("pf", [128, NPF], where=ctx)
        ps = [sb(f"ps{p}", [128, P_F], where=ctx) for p in range(2)]
        stats = sb("b_stats", [HL, GT, 6], where=ctx)
        mv = sb("b_mv", [HL, GT, 2], where=ctx)
        vare = sb("b_vare", [HL, GT], where=ctx)
        minus_half = sb("minus_half", [HL, GT], where=ctx)
        rstd = sb("b_rstd", [HL, GT], where=ctx)
        spare = sb("b_spare", [HL, 1], where=ctx)
        xn = sb("b_xn", [HL, GT, D], where=ctx)
        xt = sb("b_xt", [DH2, 2, W], where=ctx)
        xpad = sb("xpad", [128, NC, GB, L + TAPS - 1], where=ctx)
        conv = sb("conv", [128, NC, W], where=ctx)
        dtr = sb("dtr", [RANK, W], where=ctx)
        bcr = sb("bcr", [128, W], where=ctx)
        bcs = sb("bcs", [128, W], BF16, where=ctx)
        sp_abs = sb("sp_abs", [128, NC, W], where=ctx)
        x = [sb(f"x{p}", [128, NC, W], where=ctx) for p in range(2)]
        z = [sb(f"z{p}", [128, NC, W], where=ctx) for p in range(2)]
        dt = [sb(f"dt{p}", [128, NC, W], where=ctx) for p in range(2)]
        bc = [sb(f"bc{p}", [128, 2 * NS, W], where=ctx) for p in range(2)]
        NA, NH, NQ = 6, 4, 8
        da = sb("da", [128, NA, GB, L], where=ctx)
        hs = sb("hs", [128, NH, W], where=ctx)
        hc = sb("hc", [128, NQ, W], where=ctx)
        y = [sb(f"y{p}", [128, NC, W], where=ctx) for p in range(2)]

        s_load = sem("s_mamba_load")
        s_w = sem("s_w_in")
        s_wo = sem("s_w_out")
        s_zero = sem("s_mamba_zero")
        s_a = sem("s_a")
        s_neg = sem("s_neg")
        s_half = sem("s_half")
        dve_f = Steps(sem("dve_front"), ["stats", "aggr", "vare", "xn"] + [f"c{k}" for k in range(1, TAPS)] +
                      ["rest", "mid", "lo", "sp0", "sp1", "sp2"])
        act_f = Steps(sem("act_front"), ["xt0", "xt1", "x01", "x2", "c0", "z01", "z2", "x", "hi", "dtr", "abs0", "abs1", "abs2", "exp", "ln"] +
                      [f"bc{k}" for k in range(NS)])
        pe_f = Steps(sem("pe_front"), ["xt"] + [f"in{k}" for k in range(2 * NC)] + ["xp", "dt01", "dt2"] + [f"bc{k}" for k in range(NS)])
        pool_f = Steps(sem("pool_front"), ["rstd", "pf", "ps", "dt"])
        names = []
        for n in range(STEPS):
            names += [f"dtx{n // NS}"] if n % NS == 0 else []
            names += [f"m{n}"]
            names += [f"s{n - 1}"] if n else []
            names += [f"yd{n // NS - 1}"] if n % NS == 4 and n > NS else []
        dve_s = Steps(sem("dve_scan"), names + [f"s{STEPS - 1}"])
        dve_t = Steps(sem("dve_tail"), ["yd2", "add"])
        act_s = Steps(sem("act_scan"), [f"a{n}" for n in range(STEPS)])
        pool_s = Steps(sem("pool_scan"), [f"h{n}" for n in range(STEPS)])
        pool_g = Steps(sem("pool_gate"), [f"g{c}" for c in range(NC)])
        pe_s = Steps(sem("pe_scan"), [f"y{n}" for n in range(STEPS)])
        pe_t = Steps(sem("pe_tail"), ["out"])

        DVE_STATS, DVE_NORM, DVE_CONV, DVE_SPLIT, DVE_SOFT = 1, 9, 18, 27, 34
        DVE_SKIP = 3
        DVE_ADD = 30
        POOL_RSTD, POOL_DT = 4, 38
        ACT_XT, ACT_X, ACT_SILU, ACT_HI, ACT_SOFT = 14, 19, 23, 31, 35
        PE_XT, PE_XP, PE_DT = 6, 20, 27
        PE_IN = (7, 8, 10, 11, 13, 14)
        PE_OUT = (21, 22, 23, 24)
        PE_BC = (30, 31, 33, 34, 36, 37, 39, 40, 43, 45)
        PE_BC_LATE = (0, 1, 2, 3, 4, 5)
        ACT_BC = (36, 37, 39, 40, 42, 43, 45, 46)
        ACT_BC_LATE = (1, 3, 8, 9, 10, 11, 12, 13)

        def rows_of(k):
            return (k % 2) * NS + k // 2 * 2

        def batches(t):
            return t.rearrange("p (b l) -> p b l", b=GB)

        def tiles_of(u):
            return bass.ds((u % NG) * GT, GT)

        def units(eng, body):
            def two(i, first, last):
                body(2 * i, 0, first, False)
                body(2 * i + 1, 1, False, last)
            turns(eng, UNITS // 2, two)

        @block.sync
        def _(sp):
            def load_in(layer):
                sp.dma_start(w_in[:], a["w_in"][layer]).then_inc(s_w, 16)
                sp.dma_start(w_x[:], a["w_x"][layer]).then_inc(s_w, 16)
                sp.dma_start(w_dt[:], a["w_dt"][layer]).then_inc(s_w, 16)

            sp.dma_start(packs[:], a["packs"]).then_inc(s_load, 16)
            sp.dma_start(spread[:], a["spread"]).then_inc(s_load, 16)
            load_in(0)

            def two(i, first, last):
                sp.wait_ge(pe_t.sem, pe_t.at(2 * i - 1, "out"))
                sp.dma_start(w_out[:], a["w_out"][i // 2]).then_inc(s_wo, 16)
                if not last:
                    sp.wait_ge(pe_f.sem, pe_f.at(2 * i + 1, "dt2"))
                    load_in((i + 1) // 2)
            turns(sp, UNITS // 2, two)
            sp.wait_ge(s_wo, 16 * UNITS // 2)

        @block.gpsimd
        def _(pool):
            def rstd_of(u):
                pool.wait_ge(dve_f.sem, dve_f.at(u, "vare"))
                pool.wait_ge(dve_f.sem, dve_f.at(u - 1, "xn"))
                pool.tensor_tensor(rstd[:], vare[:], minus_half[:], ALU.pow).then_inc(pool_f.next("rstd"), 1)

            def front_params(u):
                pool.wait_ge(act_f.sem, act_f.at(u - 1, "abs2"))
                pool.wait_ge(dve_f.sem, dve_f.at(u - 1, "sp2"))
                pool.tensor_copy(pf[:], packs[:, u // NG, P_F:NPACK]).then_inc(pool_f.next("pf"), 1)

            def scan_params(u, p):
                pool.wait_ge(act_s.sem, act_s.at(u - 2, f"a{STEPS - 1}"))
                pool.wait_ge(dve_t.sem, dve_t.at(u - 2, "yd2"))
                pool.tensor_copy(ps[p][:], packs[:, u // NG, 0:P_F]).then_inc(pool_f.next("ps"), 1)

            def finish_dt(u, p):
                pool.wait_ge(act_f.sem, act_f.at(u, "ln"))
                pool.wait_ge(dve_f.sem, dve_f.at(u, "sp2"))
                pool.tensor_tensor(dt[p][:], dt[p][:], sp_abs[:], ALU.add).then_inc(pool_f.next("dt"), 1)

            def gate(u, p, c):
                if c < NC - 1:
                    pool.wait_ge(dve_s.sem, dve_s.at(u, f"yd{c}"))
                else:
                    pool.wait_ge(dve_t.sem, dve_t.at(u, "yd2"))
                pool.tensor_tensor(y[p][:, c, :], y[p][:, c, :], z[p][:, c, :], ALU.mult).then_inc(pool_g.next(f"g{c}"), 1)

            pool.memset(minus_half[:], -0.5)
            pool.memset(xpad[:], 0.0)
            pool.memset(da[:], 0.0).then_inc(s_zero, 1)
            pool.wait_ge(s_zero, 1)
            pool.wait_ge(s_neg, 1)
            rstd_of(0)
            front_params(0)
            scan_params(0, 0)
            finish_dt(0, 0)

            def body(u, p, first, last):
                for n in range(STEPS):
                    if n == 5 and not first:
                        gate(u - 1, 1 - p, NC - 1)
                    if n % NS == 6 and n > NS:
                        gate(u, p, n // NS - 1)
                    if not last:
                        if n == POOL_RSTD:
                            rstd_of(u + 1)
                        if n == POOL_RSTD + 1:
                            front_params(u + 1)
                        if n == 7:
                            scan_params(u + 1, 1 - p)
                        if n == POOL_DT:
                            finish_dt(u + 1, 1 - p)
                    if n < NS and n % 2 == 0:
                        pool.wait_ge(act_f.sem, act_f.at(u, f"bc{n + 1}"))
                    pool.wait_ge(dve_s.sem, dve_s.at(u, f"s{n}"))
                    if n >= NQ:
                        pool.wait_ge(pe_s.sem, pe_s.at(u, f"y{n - NQ}"))
                    else:
                        pool.wait_ge(pe_s.sem, pe_s.at(u - 1, f"y{STEPS - NQ + n}"))
                    pool.tensor_tensor(hc[:, n % NQ, :], hs[:, n % NH, :], bc[p][:, NS + n % NS, :], ALU.mult).then_inc(pool_s.next(f"h{n}"), 1)
                if last:
                    gate(u, p, NC - 1)

            units(pool, body)

        @block.vector
        def _(dve):
            dtx = bank[0][:, 0:W]

            def dbx(n):
                return two[:, (n % 3) * W:(n % 3 + 1) * W]

            def norm_stats(u):
                src = res[:, tiles_of(u), :]
                for t in range(GT):
                    last = dve.bn_stats(stats[:, t, :], src[:, t, :])
                last.then_inc(dve_f.next("stats"), 1)
                dve.wait_ge(dve_f.sem, dve_f.at(u, "stats"))
                dve.memset(spare[:], 0.0)
                for t in range(GT):
                    last = dve.bn_aggr(mv[:, t, :], stats[:, t, :])
                last.then_inc(dve_f.next("aggr"), 1)
                dve.wait_ge(dve_f.sem, dve_f.at(u, "aggr"))
                dve.wait_ge(pool_f.sem, pool_f.at(u - 1, "rstd"))
                dve.tensor_scalar(vare[:], mv[:, :, 1], EPS, None, ALU.add).then_inc(dve_f.next("vare"), 1)

            def norm_apply(u):
                src = res[:, tiles_of(u), :]
                dve.wait_ge(pool_f.sem, pool_f.at(u, "rstd"))
                dve.wait_ge(pe_f.sem, pe_f.at(u - 1, "xt"))
                for t in range(GT):
                    last = dve.tensor_scalar(xn[:, t, :], src[:, t, :], mv[:, t, 0:1], rstd[:, t:t + 1], ALU.subtract, ALU.mult)
                last.then_inc(dve_f.next("xn"), 1)

            def convolve(u, k):
                if k == 1:
                    dve.wait_ge(act_f.sem, act_f.at(u, "c0"))
                else:
                    dve.wait_ge(dve_f.sem, dve_f.at(u, f"c{k - 1}"))
                for c in range(NC):
                    w = pf[:, P_CW + c * TAPS + k:P_CW + c * TAPS + k + 1]
                    dst = batches(conv[:, c, :])
                    last = dve.scalar_tensor_tensor(dst, xpad[:, c, :, k:k + L], w, dst, ALU.mult, ALU.add)
                last.then_inc(dve_f.next(f"c{k}"), 1)

            def split_bc(u):
                dve.wait_ge(act_f.sem, act_f.at(u, "dtr"))
                dve.tensor_tensor(bcr[:], pair[0][:, 0, 0:W], bcs[:], ALU.subtract).then_inc(dve_f.next("rest"), 1)
                dve.wait_ge(dve_f.sem, dve_f.at(u, "rest"))
                dve.tensor_copy(bcs[64:128, :], bcr[64:128, :]).then_inc(dve_f.next("mid"), 1)
                dve.wait_ge(dve_f.sem, dve_f.at(u, "mid"))
                dve.tensor_tensor(bcs[96:128, :], bcr[96:128, :], bcs[96:128, :], ALU.subtract).then_inc(dve_f.next("lo"), 1)

            def softplus(u, p):
                for c in range(NC):
                    dve.wait_ge(pe_f.sem, pe_f.at(u, "dt01" if c < 2 else "dt2"))
                    dve.wait_ge(act_f.sem, act_f.at(u, "abs1" if c < 2 else "abs2"))
                    src = pair[1][:, c, 0:W] if c < 2 else pair[0][:, 0, 0:W]
                    dve.tensor_scalar(dt[p][:, c, :], src, pf[:, P_DTB + c:P_DTB + c + 1], 0.0, ALU.add, ALU.max).then_inc(dve_f.next(f"sp{c}"), 1)

            def skip(u, p, c):
                dve.wait_ge(pe_s.sem, pe_s.at(u, f"y{NS * (c + 1) - 1}"))
                dve.wait_ge(pe_t.sem, pe_t.at(u - 2, "out"))
                steps = dve_t if c == NC - 1 else dve_s
                dve.scalar_tensor_tensor(y[p][:, c, :], x[p][:, c, :], ps[p][:, P_D + c:P_D + c + 1], bank[3][:, 0:W],
                                         ALU.mult, ALU.add).then_inc(steps.next(f"yd{c}"), 1)

            def scan(u, n):
                dve.wait_ge(act_s.sem, act_s.at(u, f"a{n}"))
                dve.wait_ge(dve_s.sem, dve_s.at(u, f"m{n}"))
                if n >= NH:
                    dve.wait_ge(pool_s.sem, pool_s.at(u, f"h{n - NH}"))
                else:
                    dve.wait_ge(pool_s.sem, pool_s.at(u - 1, f"h{STEPS - NH + n}"))
                dve.tensor_tensor_scan(hs[:, n % NH, :], da[:, n % NA, :, :].rearrange("p b l -> p (b l)"),
                                                  dbx(n), 0.0, ALU.mult, ALU.add).then_inc(dve_s.next(f"s{n}"), 1)

            def add_out(u):
                dve.wait_ge(pe_t.sem, pe_t.at(u, "out"))
                t = res[:, tiles_of(u), :].rearrange("p (k t) d -> p k (t d)", k=2)
                dve.tensor_tensor(t, t, pair[1][0:HL, :, 0:2 * D], ALU.add).then_inc(dve_t.next("add"), 1)

            dve.wait_ge(s_a, 1)
            dve.tensor_scalar(packs[:, :, 0:P_D], packs[:, :, 0:P_D], -1.0, None, ALU.mult).then_inc(s_neg, 1)
            norm_stats(0)
            norm_apply(0)
            for k in range(1, TAPS):
                convolve(0, k)
            split_bc(0)
            softplus(0, 0)

            def body(u, p, first, last):
                for n in range(STEPS):
                    if n % NS == 0:
                        c = n // NS
                        if c == 0:
                            dve.wait_ge(pool_f.sem, pool_f.at(u, "dt"))
                            dve.wait_ge(act_f.sem, act_f.at(u, "x"))
                        dve.wait_ge(dve_s.sem, dve_s.at(u if n else u - 1, f"m{(n - 1) % STEPS}"))
                        dve.tensor_tensor(dtx, dt[p][:, c, :], x[p][:, c, :], ALU.mult).then_inc(dve_s.next(f"dtx{c}"), 1)
                        dve.wait_ge(dve_s.sem, dve_s.at(u, f"dtx{c}"))
                    if n < NS and n % 2 == 0:
                        dve.wait_ge(act_f.sem, act_f.at(u, f"bc{n}"))
                    if n >= 3:
                        dve.wait_ge(dve_s.sem, dve_s.at(u, f"s{n - 3}"))
                    else:
                        dve.wait_ge(dve_s.sem, dve_s.at(u - 1, f"s{STEPS - 3 + n}"))
                    dve.tensor_tensor(dbx(n), dtx, bc[p][:, n % NS, :], ALU.mult).then_inc(dve_s.next(f"m{n}"), 1)
                    if n:
                        scan(u, n - 1)
                    if n == DVE_SKIP and not first:
                        skip(u - 1, 1 - p, NC - 1)
                    if n == DVE_ADD and not first:
                        add_out(u - 1)
                    if not last:
                        if n == DVE_STATS:
                            norm_stats(u + 1)
                        if n == DVE_NORM:
                            norm_apply(u + 1)
                        if DVE_CONV <= n < DVE_CONV + TAPS - 1:
                            convolve(u + 1, n - DVE_CONV + 1)
                        if n == DVE_SPLIT:
                            split_bc(u + 1)
                        if n == DVE_SOFT:
                            softplus(u + 1, 1 - p)
                    if n % NS == 4 and n > NS:
                        skip(u, p, n // NS - 1)
                scan(u, STEPS - 1)
                if last:
                    skip(u, p, NC - 1)
                    add_out(u)

            units(dve, body)

        @block.scalar
        def _(act):
            def copy_xt(u):
                act.wait_ge(pool_f.sem, pool_f.at(u, "pf"))
                act.wait_ge(pe_f.sem, pe_f.at(u, "xt"))
                act.wait_ge(pe_f.sem, pe_f.at(u - 1, "in5"))
                for k in range(2):
                    act.activation(xt[:, k, :], pair[0][0:DH2, k, 0:W], ACT.Identity, scale=pf[0:DH2, P_NW + k:P_NW + k + 1],
                                              bias=pf[0:DH2, P_NB + k:P_NB + k + 1]).then_inc(act_f.next(f"xt{k}"), 1)

            def copy_x(u):
                act.wait_ge(pe_f.sem, pe_f.at(u, "in1"))
                act.wait_ge(dve_f.sem, dve_f.at(u - 1, f"c{TAPS - 1}"))
                act.activation(xpad[:, 0:2, :, TAPS - 1:], pair[1][:, :, 0:W].rearrange("p c (b l) -> p c b l", b=GB), ACT.Copy).then_inc(act_f.next("x01"), 1)
                act.wait_ge(pe_f.sem, pe_f.at(u, "in2"))
                act.activation(xpad[:, 2, :, TAPS - 1:], batches(pair[0][:, 0, 0:W]), ACT.Copy).then_inc(act_f.next("x2"), 1)

            def first_tap(u):
                act.wait_ge(act_f.sem, act_f.at(u, "x2"))
                for c in range(NC):
                    last = act.activation(batches(conv[:, c, :]), xpad[:, c, :, 0:L], ACT.Identity, scale=pf[:, P_CW + c * TAPS:P_CW + c * TAPS + 1],
                                          bias=pf[:, P_CB + c:P_CB + c + 1])
                last.then_inc(act_f.next("c0"), 1)

            def silus(u, p):
                act.wait_ge(dve_t.sem, dve_t.at(u - 2, "yd2"))
                act.wait_ge(pool_g.sem, pool_g.at(u - 2, "g2"))
                act.wait_ge(pe_f.sem, pe_f.at(u, "in5"))
                act.activation(z[p][:, 0:2, :], pair[1][:, :, 0:W], ACT.Silu).then_inc(act_f.next("z01"), 1)
                act.activation(z[p][:, 2, :], pair[0][:, 1, 0:W], ACT.Silu).then_inc(act_f.next("z2"), 1)
                act.wait_ge(dve_f.sem, dve_f.at(u, f"c{TAPS - 1}"))
                act.activation(x[p][:], conv[:], ACT.Silu).then_inc(act_f.next("x"), 1)

            def high_part(u):
                act.wait_ge(pe_f.sem, pe_f.at(u, "xp"))
                act.wait_ge(pe_f.sem, pe_f.at(u - 1, f"bc{NS - 1}"))
                act.activation(bcs[:], pair[0][:, 0, 0:W], ACT.Copy).then_inc(act_f.next("hi"), 1)
                act.wait_ge(pe_f.sem, pe_f.at(u - 1, "dt2"))
                act.activation(dtr[:], pair[0][0:RANK, 0, 0:W], ACT.Copy).then_inc(act_f.next("dtr"), 1)

            def soft(u):
                act.wait_ge(pool_f.sem, pool_f.at(u - 1, "dt"))
                for c in range(NC):
                    act.wait_ge(pe_f.sem, pe_f.at(u, "dt01" if c < 2 else "dt2"))
                    src = pair[1][:, c, 0:W] if c < 2 else pair[0][:, 0, 0:W]
                    act.activation(sp_abs[:, c, :], src, ACT.Abs, bias=pf[:, P_DTB + c:P_DTB + c + 1]).then_inc(act_f.next(f"abs{c}"), 1)
                act.wait_ge(act_f.sem, act_f.at(u, "abs2"))
                act.activation(sp_abs[:], sp_abs[:], ACT.Exp, scale=-1.0).then_inc(act_f.next("exp"), 1)
                act.wait_ge(act_f.sem, act_f.at(u, "exp"))
                act.activation(sp_abs[:], sp_abs[:], ACT.Ln, bias=1.0).then_inc(act_f.next("ln"), 1)

            def copy_bc(u, p, k):
                if k == 0:
                    act.wait_ge(pool_s.sem, pool_s.at(u - 2, f"h{STEPS - 1}"))
                act.wait_ge(pe_f.sem, pe_f.at(u, f"bc{k}"))
                act.activation(bc[p][:, rows_of(k):rows_of(k) + 2, :], pair[(k + 1) % 2][:, :, 0:W], ACT.Copy).then_inc(act_f.next(f"bc{k}"), 1)

            act.wait_ge(s_load, 32)
            act.activation(packs[:, :, 0:P_D], packs[:, :, 0:P_D], ACT.Exp).then_inc(s_a, 1)
            act.wait_ge(s_zero, 1)
            copy_xt(0)
            copy_x(0)
            first_tap(0)
            silus(0, 0)
            high_part(0)
            soft(0)
            for k in range(8):
                copy_bc(0, 0, k)

            def body(u, p, first, last):
                for n in range(STEPS):
                    if n == 0:
                        act.wait_ge(pool_f.sem, pool_f.at(u, "dt"))
                        act.wait_ge(pool_f.sem, pool_f.at(u, "ps"))
                    if n in ACT_BC_LATE:
                        copy_bc(u, p, len(ACT_BC) + ACT_BC_LATE.index(n))
                    if n >= NA:
                        act.wait_ge(dve_s.sem, dve_s.at(u, f"s{n - NA}"))
                    else:
                        act.wait_ge(dve_s.sem, dve_s.at(u - 1, f"s{STEPS - NA + n}"))
                    src = batches(dt[p][:, n // NS, :])
                    act.activation(da[:, n % NA, :, 1:L], src[:, :, 1:L], ACT.Exp, scale=ps[p][:, P_A + n:P_A + n + 1]).then_inc(act_s.next(f"a{n}"), 1)
                    if not last:
                        if n == ACT_XT:
                            copy_xt(u + 1)
                        if n == ACT_X:
                            copy_x(u + 1)
                            first_tap(u + 1)
                        if n == ACT_SILU:
                            silus(u + 1, 1 - p)
                        if n == ACT_HI:
                            high_part(u + 1)
                        if n == ACT_SOFT:
                            soft(u + 1)
                        if n in ACT_BC:
                            copy_bc(u + 1, 1 - p, ACT_BC.index(n))

            units(act, body)

        @block.tensor
        def _(pe):
            def transpose_x(u):
                pe.wait_ge(dve_f.sem, dve_f.at(u, "xn"))
                pe.wait_ge(act_f.sem, act_f.at(u - 1, f"bc{NS - 1}"))
                for k in range(2):
                    for t in range(GT):
                        last = pe.transpose(pair[0][0:DH2, k, t * HL:(t + 1) * HL], xn[:, t, k * DH2:(k + 1) * DH2], ident[0:HL, 0:HL])
                last.then_inc(pe_f.next("xt"), 1)

            def project(dst, m):
                for k in range(2):
                    last = pe.matmul(dst, w_in[:, k, m * 128:(m + 1) * 128], xt[:, k, :], start=(k == 0), stop=(k == 1))
                return last

            def project_in(u, step):
                m = (0, 1, 2, NC + 2, NC, NC + 1)[step]
                if step == 0:
                    pe.wait_ge(s_w, (u // 2) * 48 + 48)
                    pe.wait_ge(act_f.sem, act_f.at(u, "xt1"))
                    pe.wait_ge(act_f.sem, act_f.at(u - 1, f"bc{NS - 2}"))
                if step == 4:
                    pe.wait_ge(act_f.sem, act_f.at(u, "x01"))
                last = project(pair[(1, 0, 1)[step // 2]][:, step % 2, 0:W], m)
                last.then_inc(pe_f.next(f"in{step}"), 1)

            def project_bc(u, p):
                pe.wait_ge(act_f.sem, act_f.at(u, "x"))
                pe.wait_ge(act_f.sem, act_f.at(u, "z2"))
                for c in range(NC):
                    last = pe.matmul(pair[0][:, 0, 0:W], w_x[:, c, :], x[p][:, c, :], start=(c == 0), stop=(c == NC - 1))
                last.then_inc(pe_f.next("xp"), 1)

            def project_dt(u):
                pe.wait_ge(act_f.sem, act_f.at(u, "dtr"))
                pe.wait_ge(dve_t.sem, dve_t.at(u - 2, "add"))
                for c in range(2):
                    last = pe.matmul(pair[1][:, c, 0:W], w_dt[:, c * 128:(c + 1) * 128], dtr[:], start=True, stop=True)
                last.then_inc(pe_f.next("dt01"), 1)
                pe.wait_ge(act_f.sem, act_f.at(u, "hi"))
                pe.wait_ge(dve_f.sem, dve_f.at(u, "rest"))
                pe.matmul(pair[0][:, 0, 0:W], w_dt[:, 2 * 128:3 * 128], dtr[:], start=True, stop=True).then_inc(pe_f.next("dt2"), 1)

            def spread_bc(u, k):
                if k == 0:
                    pe.wait_ge(dve_f.sem, dve_f.at(u, "lo"))
                    pe.wait_ge(dve_f.sem, dve_f.at(u, "sp1"))
                elif k == 1:
                    pe.wait_ge(dve_f.sem, dve_f.at(u, "sp2"))
                else:
                    pe.wait_ge(act_f.sem, act_f.at(u, f"bc{k - 2}"))
                for j in range(2):
                    last = pe.matmul(pair[(k + 1) % 2][:, j, 0:W], spread[:, rows_of(k) + j, :], bcs[:], start=True, stop=True)
                last.then_inc(pe_f.next(f"bc{k}"), 1)

            def sum_states(u, n):
                if n % NS == 0:
                    if n:
                        pe.wait_ge(dve_s.sem, dve_s.at(u, f"yd{n // NS - 1}"))
                    else:
                        pe.wait_ge(dve_t.sem, dve_t.at(u - 1, "yd2"))
                pe.wait_ge(pool_s.sem, pool_s.at(u, f"h{n}"))
                pe.matmul(bank[3][:, 0:W], ident[:], hc[:, n % NQ, :], start=(n % NS == 0), stop=(n % NS == NS - 1)).then_inc(pe_s.next(f"y{n}"), 1)

            def project_out(u, p, t, last_unit):
                if t == 0:
                    pe.wait_ge(pool_g.sem, pool_g.at(u, f"g{NC - 1}"))
                    pe.wait_ge(s_wo, (u // 2) * 16 + 16)
                    if not last_unit:
                        pe.wait_ge(act_f.sem, act_f.at(u + 2, "z01"))
                for c in range(NC):
                    last = pe.matmul(pair[1][0:HL, t // 2, (t % 2) * D:(t % 2 + 1) * D], y[p][:, c, t * HL:(t + 1) * HL], w_out[:, c, :],
                                     start=(c == 0), stop=(c == NC - 1))
                if t == GT - 1:
                    last.then_inc(pe_t.next("out"), 1)

            pe.wait_ge(s_load, 32)
            transpose_x(0)
            for m in range(2 * NC):
                project_in(0, m)
            project_bc(0, 0)
            project_dt(0)
            for k in range(len(PE_BC)):
                spread_bc(0, k)

            def body(u, p, first, last):
                for n in range(STEPS):
                    if n in PE_BC_LATE:
                        spread_bc(u, len(PE_BC) + PE_BC_LATE.index(n))
                    if n in PE_OUT and not first:
                        project_out(u - 1, 1 - p, PE_OUT.index(n), last)
                    if not last:
                        if n == PE_XT:
                            transpose_x(u + 1)
                        if n in PE_IN:
                            project_in(u + 1, PE_IN.index(n))
                        if n == PE_XP:
                            project_bc(u + 1, 1 - p)
                        if n == PE_DT:
                            project_dt(u + 1)
                        if n in PE_BC:
                            spread_bc(u + 1, PE_BC.index(n))
                    sum_states(u, n)
                if last:
                    for t in range(GT):
                        project_out(u, p, t, True)

            units(pe, body)


def _mamba_arrays(f):
    import numpy as np

    def per_channel(t):
        return t.reshape(NL, NC, 128, -1).transpose(2, 0, 1, 3).reshape(128, NL, -1)

    pack = np.zeros((128, NL, NPACK), np.float32)
    at = 0
    for name in ("A_log", "D_skip", "conv_w", "conv_b", "dt_proj_b"):
        t = per_channel(f["L1_attn_" + name])
        pack[:, :, at:at + t.shape[2]] = t
        at += t.shape[2]
    for name in ("norm_w", "norm_b"):
        pack[:DH2, :, at:at + 2] = f["L1_attn_" + name].reshape(NL, 2, DH2).transpose(2, 0, 1)
        at += 2
    wx = np.zeros((NL, DI, 128), np.float32)
    xp = f["L1_attn_x_proj_w"].transpose(0, 2, 1)
    wx[:, :, :RANK] = xp[:, :, :RANK]
    for k in (32, 64, 96):
        wx[:, :, k:k + 2 * NS] = xp[:, :, RANK:]
    spread = np.zeros((128, 2 * NS, 128), mybir.dt.np(BF16))
    for s in range(2 * NS):
        spread[[32 + s, 64 + s, 96 + s], s, :] = 1
    return {
        "packs": pack, "spread": spread,
        "w_in": f["L1_attn_in_proj_w"].transpose(0, 2, 1).reshape(NL, 2, DH2, 2 * DI).transpose(0, 2, 1, 3),
        "w_x": wx.reshape(NL, NC, 128, 128).transpose(0, 2, 1, 3),
        "w_dt": f["L1_attn_dt_proj_w"].transpose(0, 2, 1),
        "w_out": f["L1_attn_out_proj_w"].transpose(0, 2, 1).reshape(NL, NC, 128, D).transpose(0, 2, 1, 3),
    }


def _host_arrays(x):
    import numpy as np
    f = {k: np.asarray(v) for k, v in x.items()}
    c = np.ascontiguousarray

    def chunks(w, p):
        return c(w.reshape(-1, p, w.shape[1]).transpose(1, 0, 2))

    img = f["x"].reshape(B, 3, 6, 16, 6, 16).transpose(1, 3, 5, 0, 2, 4).reshape(768, B * IMG)
    pos = np.arange(L, dtype=np.float32)
    inv = (np.float32(1.0) / np.float32(10000.0) ** (np.arange(0, DH, 2, dtype=np.float32) / np.float32(DH))).astype(np.float32)
    ang = (pos[:, None] * inv[None, :]).astype(np.float32)
    cos = np.concatenate([np.cos(ang), np.cos(ang)], -1)
    sin = np.concatenate([-np.sin(ang), np.sin(ang)], -1)
    scale = np.float32(DH ** -0.5)
    rope = np.stack([np.concatenate([np.tile(t * scale, (1, H)), np.tile(t, (1, H))], 1) for t in (cos, sin)])
    rope = rope.reshape(2, 2, HL, 2 * D).transpose(2, 0, 1, 3).astype(np.float32)
    lat = (np.arange(L) >= CTX).astype(np.float32)
    pad = np.zeros((L, 2 * H, 32), np.float32)
    pad[:, :H, DH] = ((1 - lat) * np.float32(-1e30))[:, None]
    pad[:, H:, DH] = lat[:, None]
    pad[:, H:, DH + 1] = -1
    pad = pad.reshape(2, HL, 2 * H, 32).transpose(1, 0, 2, 3)
    widths, ratios = (96, 144, 192), (2, 3, 4)
    rows = np.array([[(np.arange(HID) < r * e) for r in ratios] for e in widths], np.float32)
    cols = np.array([np.arange(D) < e for e in widths], np.float32)
    arrays = {
        "patches": chunks(img, 128), "tok_w": chunks(f["L0_tok_W"].T, 128), "tok_b": f["L0_tok_b"][None], "txt": f["txt"],
        "ident": np.eye(128, dtype=np.float32),
        "w_qkv": chunks(np.concatenate([f["L0_attn_Wq"], f["L0_attn_Wkv"]], 1), DH2), "rope": rope, "qk_pad": pad,
        "w_ctx": chunks(f["L0_attn_Wo_ctx"], DH2), "w_lat": chunks(f["L0_attn_Wo_lat"], DH2),
        "b_out": np.stack([f["L0_attn_bo_ctx"], f["L0_attn_bo_lat"]]), "kind": np.stack([1 - lat, lat]),
        "ln_g": f["L0_attn_ln_g"], "ln_b": f["L0_attn_ln_b"],
        "w_up1": chunks(f["L0_ffn_in_weight"].T, DH2), "b_up1": f["L0_ffn_in_bias"].reshape(HM, 128).T,
        "w_down1": chunks(f["L0_ffn_out_weight"], 128),
        "w_up2": chunks(f["L1_ffn_w_fc"].T, DH2), "b_up2": f["L1_ffn_b_fc"].reshape(HM, 128).T,
        "w_down2": chunks(f["L1_ffn_w_proj"].T, 128), "b_down2": f["L1_ffn_b_proj"][None],
        "alpha_e": f["L1_ffn_alpha_e"][:, None], "alpha_r": f["L1_ffn_alpha_r"], "mix_rows": rows, "mix_cols": cols,
        "one3": np.ones((3, 1), np.float32),
        **_mamba_arrays(f),
        "final_w": f["L1_attn_norm_f_w"], "final_b": f["L1_attn_norm_f_b"],
    }
    return {k: c(v) for k, v in arrays.items()}


def kernel(**inputs):
    import concourse.bacc as bacc
    from concourse import mybir
    from concourse.bass_utils import run_bass_kernel_spmd

    arrays = _host_arrays(inputs)
    nc = bacc.Bacc("TRN2", target_bir_lowering=False, num_devices=1)
    aps = {k: nc.dram_tensor("in_" + k, v.shape, mybir.dt.from_np(v.dtype), kind="ExternalInput").ap() for k, v in arrays.items()}
    out = nc.dram_tensor("out", (B, L, D), F32, kind="ExternalOutput").ap()
    build(nc, aps, out)
    r = run_bass_kernel_spmd(nc, [{"in_" + k: v for k, v in arrays.items()}], core_ids=[0])
    return r.results[0]["out"]
```

```python
from contextlib import ExitStack

import concourse.bass as bass
from concourse import mybir

F32 = mybir.dt.float32
BF16 = mybir.dt.bfloat16
ALU = mybir.AluOpType
ACT = mybir.ActivationFunctionType
AX = mybir.AxisListType

B = 8
IMG, TXT = 36, 128
L = IMG + TXT
HL = L // 2
NT = 2 * B
D = 192
DH2 = D // 2
PK = 768 // 128
PAIR_AT = 64
H, DH = 12, 16
LAT = 32
CTX = L - LAT
GH = 3
HG = H // GH
HH = H // 2
S_MASK = 6 * DH
SW = S_MASK + 4
HID = 768
HM = HID // 128
EPS = 1e-5
NL = 4
DI = 384
NC = DI // 128
NS = 16
TAPS = 4
RANK = 12
GB = 2
NG = B // GB
GT = 2 * GB
W = GB * L
UNITS = NL * NG
STEPS = NC * NS
P_A, P_D = 0, NC * NS
P_F = P_D + NC
P_CW, P_CB = 0, NC * TAPS
P_DTB = P_CB + NC
P_NW = P_DTB + NC
P_NB = P_NW + 2
NPF = P_NB + 2
NPACK = P_F + NPF


class Steps:

    def __init__(self, sem, names):
        self.sem = sem
        self.order = {name: k + 1 for k, name in enumerate(names)}
        assert len(self.order) == len(names)
        self.said = 0

    def next(self, name):
        assert self.order[name] == self.said % len(self.order) + 1, name
        self.said += 1
        return self.sem

    def at(self, turn, name):
        value = turn * len(self.order) + self.order[name]
        return max(value, 0) if isinstance(value, int) else value


def turns(eng, n, body, ahead=1, behind=1):
    for turn in range(ahead):
        body(turn, turn == 0, False)
    with eng.Fori(ahead, n - behind) as turn:
        body(turn, False, False)
    for turn in range(n - behind, n):
        body(turn, False, turn == n - 1)


def build(nc, a, out):
    with ExitStack() as ctx:
        def sb(name, shape, dt=F32, where=ctx):
            return where.enter_context(nc.sbuf_tensor(name, shape, dt))

        def sem(name):
            return ctx.enter_context(nc.semaphore(name))

        bank0 = ctx.enter_context(nc.psum_tensor("bank0", [128, 512], F32))
        two = ctx.enter_context(nc.psum_tensor("bank12", [128, 1024], F32))
        bank3 = ctx.enter_context(nc.psum_tensor("bank3", [128, 512], F32))
        pair = [ctx.enter_context(nc.psum_tensor(f"pair{k}", [128, 2, 512], F32)) for k in range(2)]
        bank = [bank0[:, :], two[:, 0:512], two[:, 512:1024], bank3[:, :]] + [pair[0][:, 0, :], pair[0][:, 1, :], pair[1][:, 0, :], pair[1][:, 1, :]]

        h = sb("h", [HL, NT, D])
        res = sb("res", [HL, NT, D])
        ident = sb("ident", [128, 128])
        ones = sb("ones", [1, HL])
        mixed = {"w_up": sb("m2_w_up", [DH2, 2, HID]), "b_up": sb("m2_b_up", [128, HM]), "w_down": sb("m2_w_down", [128, HM, D]),
                 "b_down": sb("m2_b_down", [1, D])}
        embed(nc, a, sb, sem, bank, pair, h, ident, ones, mixed)
        attention(nc, a, sb, sem, bank, h, ident)
        mlp(nc, a, sb, sem, bank, pair, h, res, ident, ones, None, None)
        mamba(nc, a, sb, sem, bank, two, pair, res, ident)
        mlp(nc, a, sb, sem, bank, pair, h, res, ident, ones, mixed, out)


def embed(nc, a, sb, sem, bank, pair, h, ident, ones, mixed):
    with ExitStack() as ctx, nc.Block() as block:
        patches = sb("patches", [128, PK, B // 2, PAIR_AT + IMG], where=ctx)
        tok_w = sb("tok_w", [128, PK, D], where=ctx)
        tok_b = sb("tok_b", [1, D], where=ctx)
        alpha_e = sb("alpha_e", [3, 1], where=ctx)
        alpha_r = sb("alpha_r", [3, 3], where=ctx)
        rows = sb("mix_rows", [3, 3, HID], where=ctx)
        cols = sb("mix_cols", [3, D], where=ctx)
        one3 = sb("one3", [3, 1], where=ctx)
        coef = sb("mix_coef", [3, HID], where=ctx)
        sum_r = sb("mix_sum", [3, 2], where=ctx)
        s_alpha = sem("s_alpha")
        s_patches = sem("s_patches")
        s_base = sem("s_ident")
        s_mlp = sem("s_mlp2_load")
        s_txt = sem("s_txt")
        s_const = sem("s_const")
        s_img = sem("s_img")
        s_copied = sem("s_img_copied")
        dve_m = Steps(sem("dve_mix"), ["c0", "c1", "c2", "coef", "sum", "esum"])
        pe_m = Steps(sem("pe_mix"), ["b", "up0", "up1", "down0", "down1"])
        s_scaled = sem("s_scaled")

        @block.sync
        def _(sp):
            for dst, name in ((alpha_e, "alpha_e"), (rows, "mix_rows"), (cols, "mix_cols"), (one3, "one3")):
                sp.dma_start(dst[:], a[name]).then_inc(s_alpha, 16)
            sp.dma_start(alpha_r[:], a["alpha_r"].partition_broadcast(3)).then_inc(s_alpha, 16)
            sp.dma_start(patches[:], a["patches"]).then_inc(s_patches, 16)
            sp.dma_start(tok_w[:], a["tok_w"]).then_inc(s_patches, 16)
            sp.dma_start(tok_b[:], a["tok_b"]).then_inc(s_patches, 16)
            sp.dma_start(mixed["w_up"][:], a["w_up2"]).then_inc(s_mlp, 16)
            sp.dma_start(mixed["w_down"][:], a["w_down2"]).then_inc(s_mlp, 16)
            sp.dma_start(mixed["b_up"][:], a["b_up2"]).then_inc(s_mlp, 16)
            sp.dma_start(mixed["b_down"][:], a["b_down2"]).then_inc(s_mlp, 16)
            sp.dma_start(ident[:], a["ident"]).then_inc(s_base, 16)
            sp.dma_start(h[IMG:HL, 0:NT:2, :], a["txt"][:, 0:HL - IMG, :].rearrange("b t d -> t b d")).then_inc(s_txt, 16)
            sp.dma_start(h[:, 1:NT:2, :], a["txt"][:, HL - IMG:TXT, :].rearrange("b t d -> t b d")).then_inc(s_txt, 16)
            sp.wait_ge(s_txt, 32)
            sp.wait_ge(s_base, 16)

        @block.gpsimd
        def _(pool):
            pool.memset(ones[:], 1.0).then_inc(s_const, 1)

        @block.tensor
        def _(pe):
            pe.wait_ge(s_alpha, 80)
            pe.wait_ge(dve_m.sem, dve_m.at(0, "esum"))
            for m in range(HM):
                pe.matmul(bank[3][:, m:m + 1], coef[:, m * 128:(m + 1) * 128], one3[:], start=True, stop=True)
            pe.matmul(bank[3][0:1, 64:64 + D], sum_r[:, 1:2], cols[:], start=True, stop=True).then_inc(pe_m.next("b"), 1)
            for k in range(2):
                for half in range(2):
                    last = pe.matmul(pair[k][0:DH2, half, 0:DI], cols[:, k * DH2:(k + 1) * DH2], coef[:, half * DI:(half + 1) * DI], start=True, stop=True)
                last.then_inc(pe_m.next(f"up{k}"), 1)
            pe.wait_ge(s_patches, 48)
            pe.wait_ge(s_const, 1)
            for n in range(B // 2):
                o = bank[n // 2][0:PAIR_AT + IMG, (n % 2) * D:(n % 2 + 1) * D]
                for k in range(PK):
                    pe.matmul(o, patches[:, k, n, :], tok_w[:, k, :], start=(k == 0), stop=False)
                pe.matmul(o, ones[:, 0:1].to_broadcast([1, PAIR_AT + IMG]), tok_b[:], start=False, stop=True).then_inc(s_img, 1)
            for k in range(2):
                if k == 1:
                    pe.wait_ge(s_scaled, 6)
                for m in range(4 - 2 * k):
                    at = bank[2][:, m * D:(m + 1) * D] if m < 2 and k == 0 else pair[0][:, m % 2, 0:D] if k == 0 else pair[1][:, m % 2, 0:D]
                    if k == 0 and m == 2:
                        pe.wait_ge(s_scaled, 4)
                    j = 4 * k + m
                    last = pe.matmul(at, coef[:, j * 128:(j + 1) * 128], cols[:], start=True, stop=True)
                last.then_inc(pe_m.next(f"down{k}"), 1)

        @block.vector
        def _(dve):
            dve.wait_ge(s_alpha, 80)
            dve.tensor_scalar(coef[:], rows[:, 0, :], alpha_r[:, 0:1], None, ALU.mult).then_inc(dve_m.next("c0"), 1)
            for j in range(1, 3):
                dve.wait_ge(dve_m.sem, dve_m.at(0, f"c{j - 1}"))
                dve.scalar_tensor_tensor(coef[:], rows[:, j, :], alpha_r[:, j:j + 1], coef[:], ALU.mult, ALU.add).then_inc(dve_m.next(f"c{j}"), 1)
            dve.wait_ge(dve_m.sem, dve_m.at(0, "c2"))
            dve.tensor_scalar(coef[:], coef[:], alpha_e[:, 0:1], None, ALU.mult).then_inc(dve_m.next("coef"), 1)
            dve.tensor_reduce(sum_r[:, 0:1], alpha_r[:], AX.X, ALU.add).then_inc(dve_m.next("sum"), 1)
            dve.wait_ge(dve_m.sem, dve_m.at(0, "sum"))
            dve.tensor_scalar(sum_r[:, 1:2], sum_r[:, 0:1], alpha_e[:, 0:1], None, ALU.mult).then_inc(dve_m.next("esum"), 1)
            dve.wait_ge(s_mlp, 64)
            dve.wait_ge(pe_m.sem, pe_m.at(0, "b"))
            dve.tensor_tensor(mixed["b_up"][:], mixed["b_up"][:], bank[3][:, 0:HM], ALU.mult).then_inc(s_scaled, 1)
            dve.tensor_tensor(mixed["b_down"][:], mixed["b_down"][:], bank[3][0:1, 64:64 + D], ALU.mult).then_inc(s_scaled, 1)
            for k in range(2):
                dve.wait_ge(pe_m.sem, pe_m.at(0, f"up{k}"))
                for half in range(2):
                    part = mixed["w_up"][:, k, half * DI:(half + 1) * DI]
                    dve.tensor_tensor(part, part, pair[k][0:DH2, half, 0:DI], ALU.mult).then_inc(s_scaled, 1)
            for n in range(B // 2):
                dve.wait_ge(s_img, 2 * (n // 2) + 2)
                for k in range(2):
                    src = bank[n // 2][k * PAIR_AT:k * PAIR_AT + IMG, (n % 2) * D:(n % 2 + 1) * D]
                    dve.tensor_copy(h[0:IMG, 2 * (2 * n + k), :], src).then_inc(s_copied, 1)
            for k in range(2):
                dve.wait_ge(pe_m.sem, pe_m.at(0, f"down{k}"))
                for m in range(0, 4 - 2 * k, 2):
                    part = mixed["w_down"][:, 4 * k + m:4 * k + m + 2, :]
                    src = bank[2][:, 0:2 * D].rearrange("p (m d) -> p m d", m=2) if k == 0 and m == 0 else pair[k][:, :, 0:D]
                    dve.tensor_tensor(part, part, src, ALU.mult).then_inc(s_scaled, 1)


def attention(nc, a, sb, sem, bank, h, ident):
    with ExitStack() as ctx, nc.Block() as block:
        w_qkv = sb("w_qkv", [DH2, 2, 2 * D], where=ctx)
        w_ctx = sb("w_ctx", [DH2, 2, D], where=ctx)
        w_lat = sb("w_lat", [DH2, 2, D], where=ctx)
        b_out = sb("b_out", [2, D], where=ctx)
        kind = sb("kind", [2, L], where=ctx)
        rope = sb("rope", [HL, 2, 2, 2 * D], where=ctx)
        gain = sb("gain", [HL, DH], where=ctx)
        shift = sb("shift", [HL, DH], where=ctx)
        stats = sb("a_stats", [HL, 2, 6], where=ctx)
        mv = sb("a_mv", [HL, 2, 2], where=ctx)
        vare = sb("a_vare", [HL, 2], where=ctx)
        minus_half = sb("a_minus_half", [HL, 2, H], where=ctx)
        spare = sb("a_spare", [HL, 1], where=ctx)
        rstd = sb("a_rstd", [HL, 2], where=ctx)
        xn = sb("a_xn", [HL, 2, D], where=ctx)
        xt = sb("a_xt", [DH2, 2, L], where=ctx)
        t_cos = sb("t_cos", [HL, 2, 2 * D], where=ctx)
        t_sin = sb("t_sin", [HL, 2, 2 * D], where=ctx)
        qk = sb("qk", [HL, 2, 2, D], where=ctx)
        rest = sb("qk_rest", [HL, 2, 2, D], where=ctx)
        stack = sb("qk_stack", [HL, 2, 2, H, SW], BF16, where=ctx)
        pad = sb("qk_pad", [HL, 2, 2, H, SW - S_MASK], BF16, where=ctx)
        mx = sb("score_max", [HL, 2, H], where=ctx)
        mx_rest = sb("score_max_rest", [HL, 2, H], where=ctx)
        ident16 = sb("ident16", [HL, HL], BF16, where=ctx)
        qt = sb("qt", [SW, H, L], BF16, where=ctx)
        kt = sb("kt", [SW, H, L], BF16, where=ctx)
        mu = sb("k_mu", [HL, 2, H], where=ctx)
        var = sb("k_var", [HL, 2, H], where=ctx)
        krs = sb("k_rs", [HL, 2, H], where=ctx)
        kc = sb("k_c", [HL, 2, H, DH], where=ctx)
        ksq = sb("k_sq", [HL, 2, H, DH], where=ctx)
        v = sb("v", [HL, 2, H, DH + 1], where=ctx)
        pt = sb("pt", [HL, 2, HG, GH * L], where=ctx)
        rsum = sb("rsum", [HL, 2, H, 1], where=ctx)
        o = sb("o", [HL, 2, H, DH], where=ctx)
        ot_ctx = sb("ot_ctx", [DH2, 2, L], where=ctx)
        ot_lat = sb("ot_lat", [DH2, 2, L], where=ctx)

        s_load = sem("s_attn_load")
        s_zero = sem("s_attn_zero")
        s_half = sem("s_attn_half")
        dve_n = Steps(sem("dve_norm"), ["stats", "aggr", "vare"])
        pool_n = Steps(sem("pool_norm"), ["rstd"])
        dve_a = Steps(sem("dve_project"), ["xn", "cos0", "sin0", "rope0", "cos1", "sin1", "rope1", "k1", "rest",
                                           "k2", "q3", "k3", "ksum", "kmu", "kvar", "kvare", "kt0", "kt1"])
        act_a = Steps(sem("act_project"), ["xt", "q1", "q2", "qt0", "qt1"])
        pe_a = Steps(sem("pe_project"), ["xt", "qkv0", "qkv1", "qt0", "kt0", "qt1", "kt1"])
        pool_a = Steps(sem("pool_project"), ["kc", "ksq", "krs", "kn", "kg"])
        pool_v = Steps(sem("pool_values"), ["v"])
        dve_c = Steps(sem("dve_scores"), [f"max{n}" for n in range(8)] + ["m1", "mrest", "m2", "m3"])
        act_c = Steps(sem("act_scores"), ["qt0", "qt1"] + [f"exp{n}" for n in range(8)])
        pe_c = Steps(sem("pe_scores"), [f"s{n}" for n in range(8)] + ["qt0", "qt1"] + [f"p{n}" for n in range(8)])
        dve_t = Steps(sem("dve_output"), ["recip", "o", "add"])
        act_t = Steps(sem("act_output"), ["ot"])
        pe_t = Steps(sem("pe_output"), ["pv", "ot", "out"])
        s_pad = sem("s_attn_pad")
        n_loads = 10

        def group(n):
            half, j, g = n // 4, n // 2 % 2, n // 4 * 2 + n % 2
            return half, j, g

        def heads(t, kind):
            return t[:, kind, :, :].rearrange("p j (h e) -> p (j h) e", e=DH).unsqueeze(2)

        def blocks(kind, first_block, count, step):
            t = stack[:, kind, :, :, 0:S_MASK].rearrange("p j h (s e) -> p (j h) s e", e=DH)
            return t[:, :, first_block:first_block + (count - 1) * step + 1:step, :]

        def turned(k):
            return bank[k].bitcast(BF16)[0:SW, 0:HH * L].rearrange("p (h l) -> p h l", h=HH)

        @block.sync
        def _(sp):
            for dst, name in ((w_qkv, "w_qkv"), (rope, "rope"), (pad, "qk_pad"), (ident16, "ident16"), (w_ctx, "w_ctx"), (w_lat, "w_lat"),
                              (b_out, "b_out"), (kind, "kind")):
                sp.dma_start(dst[:], a[name]).then_inc(s_load, 16)
            sp.dma_start(gain[:], a["ln_g"].partition_broadcast(HL)).then_inc(s_load, 16)
            sp.dma_start(shift[:], a["ln_b"].partition_broadcast(HL)).then_inc(s_load, 16)

        @block.vector
        def _(dve):
            def stats_of(b):
                for j in range(2):
                    last = dve.bn_stats(stats[:, j, :], h[:, 2 * b + j, :])
                last.then_inc(dve_n.next("stats"), 1)
                dve.wait_ge(dve_n.sem, dve_n.at(b, "stats"))
                dve.memset(spare[:], 0.0)
                for j in range(2):
                    last = dve.bn_aggr(mv[:, j, :], stats[:, j, :])
                last.then_inc(dve_n.next("aggr"), 1)
                dve.wait_ge(dve_n.sem, dve_n.at(b, "aggr"))
                dve.wait_ge(pool_n.sem, pool_n.at(b - 1, "rstd"))
                dve.tensor_scalar(vare[:], mv[:, :, 1], EPS, None, ALU.add).then_inc(dve_n.next("vare"), 1)

            def normalised(b):
                dve.wait_ge(pool_n.sem, pool_n.at(b, "rstd"))
                dve.wait_ge(pe_a.sem, pe_a.at(b - 1, "xt"))
                for j in range(2):
                    last = dve.tensor_scalar(xn[:, j, :], h[:, 2 * b + j, :], mv[:, j, 0:1], rstd[:, j:j + 1], ALU.subtract, ALU.mult)
                last.then_inc(dve_a.next("xn"), 1)

            def rotate(b):
                for j in range(2):
                    src = bank[4 + j][0:HL, 0:2 * D]
                    dve.wait_ge(pe_a.sem, pe_a.at(b, f"qkv{j}"))
                    dve.tensor_tensor(t_cos[:, j, :], src, rope[:, 0, j, :], ALU.mult).then_inc(dve_a.next(f"cos{j}"), 1)
                    half = "p (h u e) -> p h u e"
                    x = src.rearrange(half, u=2, e=DH // 2)
                    s = rope[:, 1, j, :].rearrange(half, u=2, e=DH // 2)
                    y = t_sin[:, j, :].rearrange(half, u=2, e=DH // 2)
                    dve.tensor_tensor(y[:, :, 0, :], x[:, :, 1, :], s[:, :, 0, :], ALU.mult)
                    dve.tensor_tensor(y[:, :, 1, :], x[:, :, 0, :], s[:, :, 1, :], ALU.mult).then_inc(dve_a.next(f"sin{j}"), 1)
                    dve.wait_ge(dve_a.sem, dve_a.at(b, f"sin{j}"))
                    if j == 0:
                        dve.wait_ge(act_a.sem, act_a.at(b - 1, "q1"))
                        dve.wait_ge(dve_a.sem, dve_a.at(b - 1, "ksum"))
                        dve.wait_ge(pool_a.sem, pool_a.at(b - 1, "kc"))
                    dve.tensor_tensor(qk[:, :, j, :], t_cos[:, j, :].rearrange("p (q d) -> p q d", q=2),
                                      t_sin[:, j, :].rearrange("p (q d) -> p q d", q=2), ALU.add).then_inc(dve_a.next(f"rope{j}"), 1)

            def split(b):
                dve.wait_ge(dve_a.sem, dve_a.at(b, "rope1"))
                dve.wait_ge(pe_a.sem, pe_a.at(b - 1, "kt1"))
                dve.tensor_copy(blocks(1, 0, 3, 1), heads(qk, 1).to_broadcast([HL, 2 * H, 3, DH])).then_inc(dve_a.next("k1"), 1)
                dve.wait_ge(dve_a.sem, dve_a.at(b, "k1"))
                dve.wait_ge(act_a.sem, act_a.at(b, "q1"))
                dve.wait_ge(act_a.sem, act_a.at(b - 1, "q2"))
                dve.tensor_tensor(rest[:].rearrange("p q j (h e) -> p (q j h) e", e=DH), qk[:].rearrange("p q j (h e) -> p (q j h) e", e=DH),
                                  stack[:, :, :, :, 2 * DH:3 * DH].rearrange("p q j h e -> p (q j h) e"), ALU.subtract).then_inc(dve_a.next("rest"), 1)
                dve.wait_ge(dve_a.sem, dve_a.at(b, "rest"))
                dve.tensor_copy(blocks(1, 3, 2, 2), heads(rest, 1).to_broadcast([HL, 2 * H, 2, DH])).then_inc(dve_a.next("k2"), 1)
                dve.wait_ge(act_a.sem, act_a.at(b, "q2"))
                dve.wait_ge(pe_c.sem, pe_c.at(b - 1, "qt1"))
                dve.tensor_tensor(blocks(0, 0, 1, 1), heads(rest, 0), blocks(0, 5, 1, 1), ALU.subtract).then_inc(dve_a.next("q3"), 1)
                dve.wait_ge(dve_a.sem, dve_a.at(b, "k2"))
                dve.tensor_tensor(blocks(1, 4, 1, 1), heads(rest, 1), blocks(1, 5, 1, 1), ALU.subtract).then_inc(dve_a.next("k3"), 1)

            def key_means(b):
                dve.wait_ge(pool_a.sem, pool_a.at(b - 1, "kc"))
                dve.tensor_reduce(mu[:], qk[:, 1, :, :].rearrange("p j (h e) -> p j h e", e=DH), AX.X, ALU.add).then_inc(dve_a.next("ksum"), 1)
                dve.wait_ge(dve_a.sem, dve_a.at(b, "ksum"))
                dve.tensor_scalar(mu[:], mu[:], 1.0 / DH, None, ALU.mult).then_inc(dve_a.next("kmu"), 1)

            def variance(b):
                dve.wait_ge(pool_a.sem, pool_a.at(b, "ksq"))
                dve.tensor_reduce(var[:], ksq[:], AX.X, ALU.add).then_inc(dve_a.next("kvar"), 1)
                dve.wait_ge(dve_a.sem, dve_a.at(b, "kvar"))
                dve.tensor_scalar(var[:], var[:], 1.0 / DH, EPS, ALU.mult, ALU.add).then_inc(dve_a.next("kvare"), 1)

            def copy_kt(b):
                for half in range(2):
                    dve.wait_ge(pe_a.sem, pe_a.at(b, f"kt{half}"))
                    dve.tensor_copy(kt[:, half * HH:(half + 1) * HH, :], turned(5 - half)).then_inc(dve_a.next(f"kt{half}"), 1)

            def maxima(b, groups):
                for n in groups:
                    half, j, g = group(n)
                    dve.wait_ge(pe_c.sem, pe_c.at(b, f"s{n}"))
                    dve.tensor_reduce(mx[:, j, g * GH:(g + 1) * GH], bank[n % 4][0:HL, 0:GH * L].rearrange("p (c k) -> p c k", c=GH),
                                      AX.X, ALU.max).then_inc(dve_c.next(f"max{n}"), 1)

            def split_maxima(b):
                at = [stack[:, 0, :, :, S_MASK + k] for k in (1, 2, 3)]
                dve.wait_ge(dve_c.sem, dve_c.at(b, "max7"))
                dve.tensor_copy(at[0], mx[:]).then_inc(dve_c.next("m1"), 1)
                dve.wait_ge(dve_c.sem, dve_c.at(b, "m1"))
                dve.tensor_tensor(mx_rest[:], mx[:], at[0], ALU.subtract).then_inc(dve_c.next("mrest"), 1)
                dve.wait_ge(dve_c.sem, dve_c.at(b, "mrest"))
                dve.tensor_copy(at[1], mx_rest[:]).then_inc(dve_c.next("m2"), 1)
                dve.wait_ge(dve_c.sem, dve_c.at(b, "m2"))
                dve.tensor_tensor(at[2], mx_rest[:], at[1], ALU.subtract).then_inc(dve_c.next("m3"), 1)

            def weigh(b):
                pv = bank[6][0:HL, 0:2 * H * (DH + 1)].rearrange("p (j h e) -> p j h e", j=2, h=H)
                dve.wait_ge(pe_t.sem, pe_t.at(b, "pv"))
                dve.reciprocal(rsum[:], pv[:, :, :, DH:DH + 1]).then_inc(dve_t.next("recip"), 1)
                dve.wait_ge(dve_t.sem, dve_t.at(b, "recip"))
                dve.wait_ge(pe_t.sem, pe_t.at(b - 1, "ot"))
                dve.tensor_tensor(o[:], pv[:, :, :, 0:DH], rsum[:].to_broadcast([HL, 2, H, DH]), ALU.mult).then_inc(dve_t.next("o"), 1)

            def add(b):
                dve.wait_ge(pe_t.sem, pe_t.at(b, "out"))
                t = h[:, bass.ds(2 * b, 2), :].rearrange("p t d -> p (t d)")
                dve.tensor_tensor(t, t, bank[6][0:HL, 0:2 * D], ALU.add).then_inc(dve_t.next("add"), 1)

            dve.memset(v[:], 1.0)
            dve.memset(ot_ctx[:], 0.0)
            dve.memset(ot_lat[:], 0.0).then_inc(s_zero, 1)
            stats_of(0)
            normalised(0)
            stats_of(1)
            dve.wait_ge(s_load, 16 * n_loads)
            rotate(0)
            dve.wait_ge(s_pad, 1)
            split(0)
            key_means(0)
            variance(0)
            copy_kt(0)

            def body(b, first, last):
                maxima(b, range(4))
                if not last:
                    normalised(b + 1)
                maxima(b, range(4, 8))
                split_maxima(b)
                if not first:
                    weigh(b - 1)
                if not isinstance(b, int) or b + 2 < B:
                    stats_of(b + 2)
                if not last:
                    rotate(b + 1)
                    split(b + 1)
                    key_means(b + 1)
                if not first:
                    add(b - 1)
                if not last:
                    variance(b + 1)
                    copy_kt(b + 1)
                if last:
                    weigh(b)
                    add(b)

            turns(dve, B, body, 2, 2)

        @block.gpsimd
        def _(pool):
            def rstd_of(b):
                pool.wait_ge(dve_n.sem, dve_n.at(b, "vare"))
                pool.wait_ge(dve_a.sem, dve_a.at(b - 1, "xn"))
                pool.tensor_tensor(rstd[:], vare[:], minus_half[:, 0, 0:2], ALU.pow).then_inc(pool_n.next("rstd"), 1)

            def each(t):
                return t.unsqueeze(3).to_broadcast([HL, 2, H, DH])

            def all_heads(t):
                return t.unsqueeze(1).unsqueeze(1).to_broadcast([HL, 2, H, DH])

            def norm_keys(b):
                pool.wait_ge(dve_a.sem, dve_a.at(b, "kmu"))
                pool.wait_ge(pool_v.sem, pool_v.at(b - 1, "v"))
                pool.tensor_tensor(kc[:], qk[:, 1, :, :].rearrange("p j (h e) -> p j h e", e=DH), each(mu[:]), ALU.subtract).then_inc(pool_a.next("kc"), 1)
                pool.wait_ge(pool_a.sem, pool_a.at(b, "kc"))
                pool.wait_ge(dve_a.sem, dve_a.at(b - 1, "kvar"))
                pool.tensor_tensor(ksq[:], kc[:], kc[:], ALU.mult).then_inc(pool_a.next("ksq"), 1)
                pool.wait_ge(dve_a.sem, dve_a.at(b, "kvare"))
                pool.tensor_tensor(krs[:], var[:], minus_half[:], ALU.pow).then_inc(pool_a.next("krs"), 1)
                pool.wait_ge(pool_a.sem, pool_a.at(b, "krs"))
                pool.tensor_tensor(kc[:], kc[:], each(krs[:]), ALU.mult).then_inc(pool_a.next("kn"), 1)
                pool.wait_ge(pool_a.sem, pool_a.at(b, "kn"))
                pool.tensor_tensor(kc[:], kc[:], all_heads(gain[:]), ALU.mult).then_inc(pool_a.next("kg"), 1)

            def values(b):
                pool.wait_ge(pool_a.sem, pool_a.at(b, "kg"))
                pool.wait_ge(pe_t.sem, pe_t.at(b - 1, "pv"))
                pool.tensor_tensor(v[:, :, :, 0:DH], kc[:], all_heads(shift[:]), ALU.add).then_inc(pool_v.next("v"), 1)

            pool.memset(minus_half[:], -0.5).then_inc(s_half, 1)
            pool.wait_ge(s_half, 1)
            rstd_of(0)
            rstd_of(1)
            pool.wait_ge(s_load, 16 * n_loads)
            pool.tensor_copy(stack[:, :, :, :, S_MASK:SW].rearrange("p q j h e -> p (q j h) e"), pad[:].rearrange("p q j h e -> p (q j h) e")).then_inc(s_pad, 1)
            pool.wait_ge(s_zero, 1)
            norm_keys(0)

            def body(b, first, last):
                values(b)
                if not isinstance(b, int) or b + 2 < B:
                    rstd_of(b + 2)
                if not last:
                    norm_keys(b + 1)

            turns(pool, B, body, 2, 2)

        @block.scalar
        def _(act):
            def copy_xt(b):
                act.wait_ge(pe_a.sem, pe_a.at(b, "xt"))
                act.activation(xt[:], bank[4][0:DH2, 0:2 * L].rearrange("p (k l) -> p k l", k=2), ACT.Copy).then_inc(act_a.next("xt"), 1)

            def split_q(b):
                act.wait_ge(dve_a.sem, dve_a.at(b, "rope1"))
                act.wait_ge(pe_c.sem, pe_c.at(b - 1, "qt1"))
                act.activation(blocks(0, 2, 3, 1), heads(qk, 0).to_broadcast([HL, 2 * H, 3, DH]), ACT.Copy).then_inc(act_a.next("q1"), 1)
                act.wait_ge(dve_a.sem, dve_a.at(b, "rest"))
                act.activation(blocks(0, 1, 2, 4), heads(rest, 0).to_broadcast([HL, 2 * H, 2, DH]), ACT.Copy).then_inc(act_a.next("q2"), 1)

            def copy_qt(b):
                for half in range(2):
                    act.wait_ge(pe_a.sem, pe_a.at(b, f"qt{half}"))
                    act.activation(qt[:, half * HH:(half + 1) * HH, :], turned((4, 7)[half]), ACT.Copy).then_inc(act_a.next(f"qt{half}"), 1)

            def copy_maxima(b):
                for half in range(2):
                    act.wait_ge(pe_c.sem, pe_c.at(b, f"qt{half}"))
                    act.activation(qt[S_MASK:SW, half * HH:(half + 1) * HH, :], turned((7, 5)[half])[S_MASK:SW], ACT.Copy).then_inc(act_c.next(f"qt{half}"), 1)

            def exps(b):
                act.wait_ge(pe_t.sem, pe_t.at(b - 1, "pv"))
                for n in range(8):
                    half, kj, g = group(n)
                    act.wait_ge(pe_c.sem, pe_c.at(b, f"p{n}"))
                    act.activation(pt[:, kj, g, :], bank[n % 4][0:HL, 0:GH * L], ACT.Exp).then_inc(act_c.next(f"exp{n}"), 1)

            def copy_ot(b):
                act.wait_ge(pe_t.sem, pe_t.at(b, "ot"))
                act.wait_ge(pe_t.sem, pe_t.at(b - 1, "out"))
                src = bank[7][0:DH2, 0:2 * L].rearrange("p (k l) -> p k l", k=2)
                act.activation(ot_ctx[:, :, 0:CTX], src[:, :, 0:CTX], ACT.Copy)
                act.activation(ot_lat[:, :, CTX:L], src[:, :, CTX:L], ACT.Copy).then_inc(act_t.next("ot"), 1)

            act.wait_ge(s_zero, 1)
            copy_xt(0)
            act.wait_ge(s_pad, 1)
            split_q(0)
            copy_qt(0)

            def body(b, first, last):
                if not last:
                    copy_xt(b + 1)
                copy_maxima(b)
                exps(b)
                if not first:
                    copy_ot(b - 1)
                if not last:
                    split_q(b + 1)
                    copy_qt(b + 1)
                if last:
                    copy_ot(b)

            turns(act, B, body, 2)

        @block.tensor
        def _(pe):
            def transpose_x(b):
                pe.wait_ge(dve_a.sem, dve_a.at(b, "xn"))
                pe.wait_ge(dve_a.sem, dve_a.at(b - 1, "kt1"))
                for k in range(2):
                    for j in range(2):
                        last = pe.transpose(bank[4][0:DH2, k * L + j * HL:k * L + (j + 1) * HL], xn[:, j, k * DH2:(k + 1) * DH2], ident[0:HL, 0:HL])
                last.then_inc(pe_a.next("xt"), 1)

            def project(b):
                pe.wait_ge(act_a.sem, act_a.at(b, "xt"))
                for j in range(2):
                    if j == 1:
                        pe.wait_ge(act_c.sem, act_c.at(b - 1, "qt1"))
                    for k in range(2):
                        last = pe.matmul(bank[4 + j][0:HL, 0:2 * D], xt[:, k, j * HL:(j + 1) * HL], w_qkv[:, k, :], start=(k == 0), stop=(k == 1))
                    last.then_inc(pe_a.next(f"qkv{j}"), 1)

            def transpose_heads(k, kind, half):
                for j in range(2):
                    for hd in range(HH):
                        last = pe.transpose(turned(k)[:, hd, j * HL:(j + 1) * HL], stack[:, kind, j, half * HH + hd, :], ident16[:])
                return last

            def transpose_qk(b):
                pe.wait_ge(dve_a.sem, dve_a.at(b, "k3"))
                transpose_heads(4, 0, 0).then_inc(pe_a.next("qt0"), 1)
                transpose_heads(5, 1, 0).then_inc(pe_a.next("kt0"), 1)
                transpose_heads(7, 0, 1).then_inc(pe_a.next("qt1"), 1)
                pe.wait_ge(act_a.sem, act_a.at(b, "qt0"))
                transpose_heads(4, 1, 1).then_inc(pe_a.next("kt1"), 1)

            def weighted_values(k):
                j, hd = divmod(k, H)
                g, c = divmod(hd, GH)
                for kj in range(2):
                    last = pe.matmul(bank[6][0:HL, k * (DH + 1):(k + 1) * (DH + 1)], pt[:, kj, g, c * L + j * HL:c * L + (j + 1) * HL],
                                     v[:, kj, hd, :], start=(kj == 0), stop=(kj == 1))
                if k == 2 * H - 1:
                    last.then_inc(pe_t.next("pv"), 1)

            def scores(b, values_too):
                if values_too:
                    pe.wait_ge(act_c.sem, act_c.at(b - 1, "exp7"))
                    pe.wait_ge(pool_v.sem, pool_v.at(b - 1, "v"))
                    pe.wait_ge(dve_t.sem, dve_t.at(b - 2, "add"))
                for n in range(8):
                    half, j, g = group(n)
                    if n % 4 == 0:
                        pe.wait_ge(act_a.sem, act_a.at(b, f"qt{half}"))
                        pe.wait_ge(dve_a.sem, dve_a.at(b, f"kt{half}"))
                    if n < 4:
                        pe.wait_ge(act_c.sem, act_c.at(b - 1, f"exp{n + 4}"))
                    else:
                        pe.wait_ge(dve_c.sem, dve_c.at(b, f"max{n - 4}"))
                    rows = slice(0, S_MASK + 1)
                    for c in range(GH):
                        last = pe.matmul(bank[n % 4][0:HL, c * L:(c + 1) * L], qt[rows, g * GH + c, j * HL:(j + 1) * HL], kt[rows, g * GH + c, :],
                                         start=True, stop=True)
                        if c == GH - 1:
                            last.then_inc(pe_c.next(f"s{n}"), 1)
                        if values_too:
                            weighted_values(n * GH + c)

            def transpose_q_with_max(b):
                pe.wait_ge(dve_c.sem, dve_c.at(b, "m3"))
                transpose_heads(7, 0, 0).then_inc(pe_c.next("qt0"), 1)
                transpose_heads(5, 0, 1).then_inc(pe_c.next("qt1"), 1)

            def shifted_scores(b):
                for n in range(8):
                    half, j, g = group(n)
                    if n % 4 == 0:
                        pe.wait_ge(act_c.sem, act_c.at(b, f"qt{half}"))
                    if n >= 4:
                        pe.wait_ge(act_c.sem, act_c.at(b, f"exp{n - 4}"))
                    for c in range(GH):
                        last = pe.matmul(bank[n % 4][0:HL, c * L:(c + 1) * L], kt[:, g * GH + c, j * HL:(j + 1) * HL], qt[:, g * GH + c, :],
                                         start=True, stop=True)
                    last.then_inc(pe_c.next(f"p{n}"), 1)

            def weigh_values(b):
                pe.wait_ge(act_c.sem, act_c.at(b, "exp7"))
                pe.wait_ge(pool_v.sem, pool_v.at(b, "v"))
                pe.wait_ge(dve_t.sem, dve_t.at(b - 1, "add"))
                for k in range(2 * H):
                    weighted_values(k)

            def transpose_o(b):
                pe.wait_ge(dve_t.sem, dve_t.at(b, "o"))
                for k in range(2):
                    for j in range(2):
                        src = o[:, j, :, :].rearrange("p h e -> p (h e)")[:, k * DH2:(k + 1) * DH2]
                        last = pe.transpose(bank[7][0:DH2, k * L + j * HL:k * L + (j + 1) * HL], src, ident[0:HL, 0:HL])
                last.then_inc(pe_t.next("ot"), 1)

            def project_out(b):
                pe.wait_ge(act_t.sem, act_t.at(b, "ot"))
                for j in range(2):
                    dst = bank[6][0:HL, j * D:(j + 1) * D]
                    cols = slice(j * HL, (j + 1) * HL)
                    pe.matmul(dst, kind[:, cols], b_out[:], start=True, stop=False)
                    for t, w in ((ot_ctx, w_ctx), (ot_lat, w_lat))[:2 if (j + 1) * HL > CTX else 1]:
                        for k in range(2):
                            last = pe.matmul(dst, t[:, k, cols], w[:, k, :], start=False, stop=(k == 1 and (t is ot_lat or (j + 1) * HL <= CTX)))
                last.then_inc(pe_t.next("out"), 1)

            pe.wait_ge(s_load, 16 * n_loads)
            transpose_x(0)
            project(0)
            transpose_qk(0)

            def body(b, first, last):
                scores(b, not first)
                if not last:
                    transpose_x(b + 1)
                transpose_q_with_max(b)
                if not last:
                    project(b + 1)
                shifted_scores(b)
                if not first:
                    transpose_o(b - 1)
                    project_out(b - 1)
                if not last:
                    transpose_qk(b + 1)
                if last:
                    weigh_values(b)
                    transpose_o(b)
                    project_out(b)

            turns(pe, B, body, 2)


def mlp(nc, a, sb, sem, bank, pair, h, res, ident, ones, mixed, out):
    n = "m2_" if mixed else "m1_"
    with ExitStack() as ctx, nc.Block() as block:
        w_up, b_up, w_down = (mixed[k] for k in ("w_up", "b_up", "w_down")) if mixed else (
            sb("m1_w_up", [DH2, 2, HID], where=ctx), sb("m1_b_up", [128, HM], where=ctx), sb("m1_w_down", [128, HM, D], where=ctx))
        minus_half = sb(n + "minus_half", [HL, GT], where=ctx)
        spare = sb(n + "spare", [HL, 1], where=ctx)
        norms = {}
        for k in "xr":
            norms[k] = {"stats": sb(n + k + "_stats", [HL, GT, 6], where=ctx), "mv": sb(n + k + "_mv", [HL, GT, 2], where=ctx),
                        "vare": sb(n + k + "_vare", [HL, GT], where=ctx), "rstd": sb(n + k + "_rstd", [HL, GT], where=ctx),
                        "dve": Steps(sem(n + k + "_dve"), ["stats", "aggr", "vare", "out"]), "pool": Steps(sem(n + k + "_pool"), ["rstd"])}
        xn = sb(n + "xn", [HL, GT, D], where=ctx)
        xt = sb(n + "xt", [DH2, 2, W], where=ctx)
        act_out = sb(n + "hidden", [128, HM, W], where=ctx)
        s_load = sem(n + "s_load")
        s_stored = sem(n + "s_stored")
        s_half = sem(n + "s_half")
        s_add = Steps(sem(n + "dve_add"), ["add"])
        act_s = Steps(sem(n + "act_norm"), ["xt"])
        act_g = Steps(sem(n + "act_gelu"), [f"g{m}" for m in range(HM)])
        pe_x = Steps(sem(n + "pe_xt"), ["xt"])
        pe_s = Steps(sem(n + "pe"), [f"up{m}" for m in range(HM)] + ["down"])
        x_norm, r_norm = norms["x"], norms["r"]
        if mixed:
            fw = sb("final_w", [HL, D], where=ctx)
            fb = sb("final_b", [HL, D], where=ctx)
            rn = sb("final_rn", [HL, GT, D], where=ctx)
            pool_r = Steps(sem("pool_final"), ["w", "b"])
            s_final = Steps(sem("dve_final"), ["add"])

        @block.sync
        def _(sp):
            if mixed:
                sp.dma_start(fw[:], a["final_w"].partition_broadcast(HL)).then_inc(s_load, 16)
                sp.dma_start(fb[:], a["final_b"].partition_broadcast(HL)).then_inc(s_load, 16)
                out_v = out.rearrange("b (j p) d -> p (b j) d", j=2)
                for q in range(NG):
                    sp.wait_ge(s_add.sem, s_add.at(q, "add"))
                    sp.dma_start(out_v[:, bass.ds(GT * q, GT), :], h[:, bass.ds(GT * q, GT), :]).then_inc(s_stored, 16)
                sp.wait_ge(s_stored, 16 * NG)
            else:
                for dst, name in ((w_up, "w_up1"), (b_up, "b_up1"), (w_down, "w_down1")):
                    sp.dma_start(dst[:], a[name]).then_inc(s_load, 16)

        @block.vector
        def _(dve):
            def statistics(q, norm, src):
                for t in range(GT):
                    last = dve.bn_stats(norm["stats"][:, t, :], src[:, GT * q + t, :])
                last.then_inc(norm["dve"].next("stats"), 1)
                dve.wait_ge(norm["dve"].sem, norm["dve"].at(q, "stats"))
                dve.memset(spare[:], 0.0)
                for t in range(GT):
                    last = dve.bn_aggr(norm["mv"][:, t, :], norm["stats"][:, t, :])
                last.then_inc(norm["dve"].next("aggr"), 1)
                dve.wait_ge(norm["dve"].sem, norm["dve"].at(q, "aggr"))
                dve.wait_ge(norm["pool"].sem, norm["pool"].at(q - 1, "rstd"))
                dve.tensor_scalar(norm["vare"][:], norm["mv"][:, :, 1], EPS, None, ALU.add).then_inc(norm["dve"].next("vare"), 1)

            def normed(q, norm, src, dst, at):
                dve.wait_ge(norm["pool"].sem, norm["pool"].at(q, "rstd"))
                for t in range(GT):
                    last = dve.tensor_scalar(dst[:, at + t, :], src[:, GT * q + t, :], norm["mv"][:, t, 0:1], norm["rstd"][:, t:t + 1],
                                             ALU.subtract, ALU.mult)
                last.then_inc(norm["dve"].next("out"), 1)

            def end_stack(q):
                dve.wait_ge(s_final.sem, s_final.at(q - 1, "add"))
                normed(q, r_norm, res, rn, 0)

            def add_stack(q):
                dve.wait_ge(pool_r.sem, pool_r.at(q, "b"))
                t = h[:, bass.ds(GT * q, GT), :]
                dve.tensor_tensor(t, t, rn[:], ALU.add).then_inc(s_final.next("add"), 1)
                dve.wait_ge(s_final.sem, s_final.at(q, "add"))

            def norm_x(q):
                dve.wait_ge(pe_x.sem, pe_x.at(q - 1, "xt"))
                normed(q, x_norm, h, xn, 0)

            def add(q):
                dve.wait_ge(pe_s.sem, pe_s.at(q, "down"))
                t = h[:, bass.ds(GT * q, GT), :].rearrange("p (k t) d -> p k (t d)", k=2)
                dve.tensor_tensor(t, t, pair[1][0:HL, :, 0:2 * D], ALU.add).then_inc(s_add.next("add"), 1)

            if mixed:
                statistics(0, r_norm, res)
                end_stack(0)
                statistics(1, r_norm, res)
                add_stack(0)
            statistics(0, x_norm, h)
            norm_x(0)
            if mixed:
                end_stack(1)

            def body(q, first, last):
                if not last:
                    if mixed:
                        add_stack(q + 1)
                    statistics(q + 1, x_norm, h)
                    if mixed and (not isinstance(q, int) or q + 2 < NG):
                        statistics(q + 2, r_norm, res)
                    norm_x(q + 1)
                    if mixed and (not isinstance(q, int) or q + 2 < NG):
                        end_stack(q + 2)
                add(q)
                if not mixed:
                    dve.wait_ge(s_add.sem, s_add.at(q, "add"))
                    statistics(q, r_norm, h)
                    normed(q, r_norm, h, res, GT * q)

            turns(dve, NG, body, 1, 2)

        @block.gpsimd
        def _(pool):
            def rstd(q, norm):
                pool.wait_ge(norm["dve"].sem, norm["dve"].at(q, "vare"))
                pool.wait_ge(norm["dve"].sem, norm["dve"].at(q - 1, "out"))
                pool.tensor_tensor(norm["rstd"][:], norm["vare"][:], minus_half[:], ALU.pow).then_inc(norm["pool"].next("rstd"), 1)

            def scale_and_shift(q):
                pool.wait_ge(r_norm["dve"].sem, r_norm["dve"].at(q, "out"))
                pool.tensor_tensor(rn[:], rn[:], fw[:].unsqueeze(1).to_broadcast([HL, GT, D]), ALU.mult).then_inc(pool_r.next("w"), 1)
                pool.wait_ge(pool_r.sem, pool_r.at(q, "w"))
                pool.tensor_tensor(rn[:], rn[:], fb[:].unsqueeze(1).to_broadcast([HL, GT, D]), ALU.add).then_inc(pool_r.next("b"), 1)

            pool.memset(minus_half[:], -0.5).then_inc(s_half, 1)
            pool.wait_ge(s_half, 1)
            if mixed:
                pool.wait_ge(s_load, 32)
                rstd(0, r_norm)
                scale_and_shift(0)
                rstd(1, r_norm)
            rstd(0, x_norm)
            if mixed:
                scale_and_shift(1)

            def body(q, first, last):
                if not last:
                    rstd(q + 1, x_norm)
                    if mixed and (not isinstance(q, int) or q + 2 < NG):
                        rstd(q + 2, r_norm)
                        scale_and_shift(q + 2)
                if not mixed:
                    rstd(q, r_norm)

            turns(pool, NG, body, 1, 2)

        @block.scalar
        def _(act):
            def copy_xt(q):
                act.wait_ge(pe_x.sem, pe_x.at(q, "xt"))
                act.wait_ge(pe_s.sem, pe_s.at(q - 1, f"up{HM - 1}"))
                act.activation(xt[:], pair[0][0:DH2, :, 0:W], ACT.Copy).then_inc(act_s.next("xt"), 1)

            copy_xt(0)
            if not mixed:
                act.wait_ge(s_load, 48)

            def body(q, first, last):
                act.wait_ge(pe_s.sem, pe_s.at(q - 1, "down"))
                for m in range(HM):
                    act.wait_ge(pe_s.sem, pe_s.at(q, f"up{m}"))
                    act.activation(act_out[:, m, :], bank[m % 4][:, 0:W], ACT.Gelu_apprx_tanh if mixed else ACT.Gelu,
                                   bias=b_up[:, m:m + 1]).then_inc(act_g.next(f"g{m}"), 1)
                if not last:
                    copy_xt(q + 1)

            turns(act, NG, body)

        @block.tensor
        def _(pe):
            def transpose_x(q):
                pe.wait_ge(x_norm["dve"].sem, x_norm["dve"].at(q, "out"))
                pe.wait_ge(act_s.sem, act_s.at(q - 1, "xt"))
                for k in range(2):
                    for t in range(GT):
                        last = pe.transpose(pair[0][0:DH2, k, t * HL:(t + 1) * HL], xn[:, t, k * DH2:(k + 1) * DH2], ident[0:HL, 0:HL])
                last.then_inc(pe_x.next("xt"), 1)

            transpose_x(0)
            if not mixed:
                pe.wait_ge(s_load, 48)

            def body(q, first, last):
                pe.wait_ge(act_s.sem, act_s.at(q, "xt"))
                for m in range(HM):
                    if m < 4:
                        pe.wait_ge(act_g.sem, act_g.at(q - 1, f"g{m + 4 if m + 4 < HM else m}"))
                    else:
                        pe.wait_ge(act_g.sem, act_g.at(q, f"g{m - 4}"))
                    for k in range(2):
                        last_mm = pe.matmul(bank[m % 4][:, 0:W], w_up[:, k, m * 128:(m + 1) * 128], xt[:, k, :], start=(k == 0), stop=(k == 1))
                    last_mm.then_inc(pe_s.next(f"up{m}"), 1)
                if not last:
                    transpose_x(q + 1)
                pe.wait_ge(s_add.sem, s_add.at(q - 1, "add"))
                pe.wait_ge(act_g.sem, act_g.at(q, f"g{HM - 1}"))
                for t in range(GT):
                    dst = pair[1][0:HL, t // 2, (t % 2) * D:(t % 2 + 1) * D]
                    for m in range(HM):
                        last_mm = pe.matmul(dst, act_out[:, m, t * HL:(t + 1) * HL], w_down[:, m, :], start=(m == 0), stop=(m == HM - 1 and not mixed))
                    if mixed:
                        last_mm = pe.matmul(dst, ones[:], mixed["b_down"][:], start=False, stop=True)
                last_mm.then_inc(pe_s.next("down"), 1)

            turns(pe, NG, body)


def mamba(nc, a, sb, sem, bank, two, pair, res, ident):
    with ExitStack() as ctx, nc.Block() as block:
        packs = sb("packs", [128, NL, NPACK], where=ctx)
        w_in = sb("w_in", [DH2, 2, 2 * DI], where=ctx)
        w_x = sb("w_x", [128, NC, 128], where=ctx)
        w_dt = sb("w_dt", [RANK, DI], where=ctx)
        w_out = sb("w_out", [128, NC, D], where=ctx)
        spread = sb("spread", [128, 2 * NS], BF16, where=ctx)
        pf = sb("pf", [128, NPF], where=ctx)
        ps = [sb(f"ps{p}", [128, P_F], where=ctx) for p in range(2)]
        stats = sb("b_stats", [HL, GT, 6], where=ctx)
        mv = sb("b_mv", [HL, GT, 2], where=ctx)
        vare = sb("b_vare", [HL, GT], where=ctx)
        minus_half = sb("minus_half", [HL, GT], where=ctx)
        rstd = sb("b_rstd", [HL, GT], where=ctx)
        spare = sb("b_spare", [HL, 1], where=ctx)
        xn = sb("b_xn", [HL, GT, D], where=ctx)
        xt = sb("b_xt", [DH2, 2, W], where=ctx)
        xpad = sb("xpad", [128, NC, GB, L + TAPS - 1], where=ctx)
        diag = sb("diag", [128, TAPS, 128], where=ctx)
        conv = sb("conv", [128, NC, W], where=ctx)
        dtr = sb("dtr", [RANK, W], where=ctx)
        bcr = conv[:, 0, :]
        bcs = sb("bcs", [128, W], BF16, where=ctx)
        x = [sb(f"x{p}", [128, NC, W], where=ctx) for p in range(2)]
        z = [sb(f"z{p}", [128, NC, W], where=ctx) for p in range(2)]
        dt = [sb(f"dt{p}", [128, NC, W], where=ctx) for p in range(2)]
        bc = [sb(f"bc{p}", [128, 2 * NS, W], where=ctx) for p in range(2)]
        NA, NH, NQ = 8, 6, 8
        da = sb("da", [128, NA, GB, L], where=ctx)
        hs = sb("hs", [128, NH, W], where=ctx)
        hc = sb("hc", [128, NQ, W], where=ctx)
        y = [sb(f"y{p}", [128, NC, W], where=ctx) for p in range(2)]

        s_load = sem("s_mamba_load")
        s_w = sem("s_w_in")
        s_wo = sem("s_w_out")
        s_zero = sem("s_mamba_zero")
        s_a = sem("s_a")
        s_neg = sem("s_neg")
        s_half = sem("s_half")
        dve_f = Steps(sem("dve_front"), ["stats", "aggr", "vare", "xn"] + [f"c{k}" for k in range(1, TAPS)] +
                      ["rest", "mid", "lo", "sp0", "sp1", "sp2"])
        act_f = Steps(sem("act_front"), ["xt0", "xt1", "x01", "x2", "c0", "z01", "z2", "xc", "x", "hi", "dtr", "abs0", "abs1", "abs2", "exp", "ln"] +
                      [f"bc{k}" for k in range(NS)])
        pe_f = Steps(sem("pe_front"), ["xt"] + [f"in{k}" for k in range(2 * NC)] + ["conv", "xp", "dt01", "dt2"] + [f"bc{k}" for k in range(NS)])
        pool_f = Steps(sem("pool_front"), ["rstd", "pf", "dw", "ps", "dt"])
        names = []
        for n in range(STEPS):
            names += [f"dtx{n // NS}"] if n % NS == 0 else []
            names += [f"m{n}"]
            names += [f"s{n - 1}"] if n else []
            names += [f"yd{n // NS - 1}"] if n % NS == 4 and n > NS else []
        dve_s = Steps(sem("dve_scan"), names + [f"s{STEPS - 1}"])
        dve_t = Steps(sem("dve_tail"), ["yd2", "add"])
        act_s = Steps(sem("act_scan"), [f"a{n}" for n in range(STEPS)])
        pool_s = Steps(sem("pool_scan"), [f"h{n}" for n in range(1, STEPS, 2)])
        pool_g = Steps(sem("pool_gate"), [f"g{c}" for c in range(NC)])
        pe_s = Steps(sem("pe_scan"), [f"y{n}" for n in range(STEPS)])
        pe_t = Steps(sem("pe_tail"), ["out"])

        DVE_STATS, DVE_NORM, DVE_CONV, DVE_SPLIT, DVE_SOFT = 4, 8, 18, 32, 36
        DVE_SKIP = 3
        DVE_ADD = 32
        POOL_RSTD, POOL_DT = 5, 36
        ACT_XT, ACT_X, ACT_SILU, ACT_HI, ACT_SOFT = 14, 17, 26, 32, 37
        PE_XT, PE_XP, PE_DT = 6, 20, 25
        PE_CONV = 16
        PE_IN = (7, 8, 10, 11, 13, 16)
        PE_OUT = (17, 18, 19, 20)
        PE_BC = (31, 32, 33, 34, 36, 37, 39, 40, 43, 45)
        PE_BC_LATE = (0, 1, 2, 3, 4, 5)
        ACT_BC = (37, 38, 40, 41, 43, 44, 46, 47)
        ACT_BC_LATE = (1, 3, 8, 9, 10, 11, 12, 13)

        def rows_of(k):
            return (k % 2) * NS + k // 2 * 2

        def batches(t):
            return t.rearrange("p (b l) -> p b l", b=GB)

        def tiles_of(u):
            return bass.ds((u % NG) * GT, GT)

        def units(eng, body):
            def two(i, first, last):
                body(2 * i, 0, first, False)
                body(2 * i + 1, 1, False, last)
            turns(eng, UNITS // 2, two)

        @block.sync
        def _(sp):
            def load_in(layer):
                sp.dma_start(w_in[:], a["w_in"][layer]).then_inc(s_w, 16)
                sp.dma_start(w_x[:], a["w_x"][layer]).then_inc(s_w, 16)
                sp.dma_start(w_dt[:], a["w_dt"][layer]).then_inc(s_w, 16)

            sp.dma_start(packs[:], a["packs"]).then_inc(s_load, 16)
            sp.dma_start(spread[:], a["spread"]).then_inc(s_load, 16)
            load_in(0)

            def two(i, first, last):
                sp.wait_ge(pe_t.sem, pe_t.at(2 * i - 1, "out"))
                sp.dma_start(w_out[:], a["w_out"][i // 2]).then_inc(s_wo, 16)
                if not last:
                    sp.wait_ge(pe_f.sem, pe_f.at(2 * i + 1, "dt2"))
                    load_in((i + 1) // 2)
            turns(sp, UNITS // 2, two)
            sp.wait_ge(s_wo, 16 * UNITS // 2)

        @block.gpsimd
        def _(pool):
            def rstd_of(u):
                pool.wait_ge(dve_f.sem, dve_f.at(u, "vare"))
                pool.wait_ge(dve_f.sem, dve_f.at(u - 1, "xn"))
                pool.tensor_tensor(rstd[:], vare[:], minus_half[:], ALU.pow).then_inc(pool_f.next("rstd"), 1)

            def front_params(u):
                pool.wait_ge(act_f.sem, act_f.at(u - 1, "abs2"))
                pool.wait_ge(dve_f.sem, dve_f.at(u - 1, "sp2"))
                pool.tensor_copy(pf[:], packs[:, u // NG, P_F:NPACK]).then_inc(pool_f.next("pf"), 1)
                pool.wait_ge(pe_f.sem, pe_f.at(u - 1, "conv"))
                pool.wait_ge(pool_f.sem, pool_f.at(u, "pf"))
                at = P_CW + (NC - 1) * TAPS
                pool.tensor_tensor(diag[:], ident[:].unsqueeze(1).to_broadcast([128, TAPS, 128]),
                                   pf[:, at:at + TAPS].unsqueeze(2).to_broadcast([128, TAPS, 128]), ALU.mult).then_inc(pool_f.next("dw"), 1)

            def scan_params(u, p):
                pool.wait_ge(act_s.sem, act_s.at(u - 2, f"a{STEPS - 1}"))
                pool.wait_ge(dve_t.sem, dve_t.at(u - 2, "yd2"))
                pool.tensor_copy(ps[p][:], packs[:, u // NG, 0:P_F]).then_inc(pool_f.next("ps"), 1)

            def finish_dt(u, p):
                pool.wait_ge(act_f.sem, act_f.at(u, "ln"))
                pool.wait_ge(dve_f.sem, dve_f.at(u, "sp2"))
                pool.tensor_tensor(dt[p][:], dt[p][:], conv[:], ALU.add).then_inc(pool_f.next("dt"), 1)

            def gate(u, p, c):
                if c < NC - 1:
                    pool.wait_ge(dve_s.sem, dve_s.at(u, f"yd{c}"))
                else:
                    pool.wait_ge(dve_t.sem, dve_t.at(u, "yd2"))
                pool.tensor_tensor(y[p][:, c, :], y[p][:, c, :], z[p][:, c, :], ALU.mult).then_inc(pool_g.next(f"g{c}"), 1)

            pool.memset(minus_half[:], -0.5).then_inc(s_half, 1)
            pool.wait_ge(s_half, 1)
            rstd_of(0)
            pool.memset(xpad[:], 0.0)
            pool.memset(da[:], 0.0).then_inc(s_zero, 1)
            pool.wait_ge(s_neg, 1)
            front_params(0)
            scan_params(0, 0)
            finish_dt(0, 0)

            def body(u, p, first, last):
                for n in range(STEPS):
                    if n == 5 and not first:
                        gate(u - 1, 1 - p, NC - 1)
                    if n % NS == 6 and n > NS:
                        gate(u, p, n // NS - 1)
                    if not last:
                        if n == POOL_RSTD:
                            rstd_of(u + 1)
                        if n == POOL_RSTD + 1:
                            front_params(u + 1)
                        if n == 7:
                            scan_params(u + 1, 1 - p)
                        if n == POOL_DT:
                            finish_dt(u + 1, 1 - p)
                    if n % 2:
                        if n < NS:
                            pool.wait_ge(act_f.sem, act_f.at(u, f"bc{n}"))
                        pool.wait_ge(dve_s.sem, dve_s.at(u, f"s{n}"))
                        if n >= NQ:
                            pool.wait_ge(pe_s.sem, pe_s.at(u, f"y{n - NQ}"))
                        else:
                            pool.wait_ge(pe_s.sem, pe_s.at(u - 1, f"y{STEPS - NQ + n}"))
                        pool.tensor_tensor(hc[:, n % NQ - 1:n % NQ + 1, :], hs[:, n % NH - 1:n % NH + 1, :],
                                           bc[p][:, NS + n % NS - 1:NS + n % NS + 1, :], ALU.mult).then_inc(pool_s.next(f"h{n}"), 1)
                if last:
                    gate(u, p, NC - 1)

            units(pool, body)

        @block.vector
        def _(dve):
            dtx = bank[0][:, 0:W]

            def dbx(n):
                return two[:, (n % 3) * W:(n % 3 + 1) * W]

            def norm_stats(u):
                src = res[:, tiles_of(u), :]
                for t in range(GT):
                    last = dve.bn_stats(stats[:, t, :], src[:, t, :])
                last.then_inc(dve_f.next("stats"), 1)
                dve.wait_ge(dve_f.sem, dve_f.at(u, "stats"))
                dve.memset(spare[:], 0.0)
                for t in range(GT):
                    last = dve.bn_aggr(mv[:, t, :], stats[:, t, :])
                last.then_inc(dve_f.next("aggr"), 1)
                dve.wait_ge(dve_f.sem, dve_f.at(u, "aggr"))
                dve.wait_ge(pool_f.sem, pool_f.at(u - 1, "rstd"))
                dve.tensor_scalar(vare[:], mv[:, :, 1], EPS, None, ALU.add).then_inc(dve_f.next("vare"), 1)

            def norm_apply(u):
                src = res[:, tiles_of(u), :]
                dve.wait_ge(pool_f.sem, pool_f.at(u, "rstd"))
                dve.wait_ge(pe_f.sem, pe_f.at(u - 1, "xt"))
                for t in range(GT):
                    last = dve.tensor_scalar(xn[:, t, :], src[:, t, :], mv[:, t, 0:1], rstd[:, t:t + 1], ALU.subtract, ALU.mult)
                last.then_inc(dve_f.next("xn"), 1)

            def convolve(u, k):
                if k == 1:
                    dve.wait_ge(act_f.sem, act_f.at(u, "c0"))
                else:
                    dve.wait_ge(dve_f.sem, dve_f.at(u, f"c{k - 1}"))
                for c in range(NC - 1):
                    w = pf[:, P_CW + c * TAPS + k:P_CW + c * TAPS + k + 1]
                    dst = batches(conv[:, c, :])
                    last = dve.scalar_tensor_tensor(dst, xpad[:, c, :, k:k + L], w, dst, ALU.mult, ALU.add)
                last.then_inc(dve_f.next(f"c{k}"), 1)

            def split_bc(u):
                dve.wait_ge(act_f.sem, act_f.at(u, "dtr"))
                dve.tensor_tensor(bcr, pair[0][:, 0, 0:W], bcs[:], ALU.subtract).then_inc(dve_f.next("rest"), 1)
                dve.wait_ge(dve_f.sem, dve_f.at(u, "rest"))
                dve.tensor_copy(bcs[64:128, :], bcr[64:128, :]).then_inc(dve_f.next("mid"), 1)
                dve.wait_ge(dve_f.sem, dve_f.at(u, "mid"))
                dve.tensor_tensor(bcs[96:128, :], bcr[96:128, :], bcs[96:128, :], ALU.subtract).then_inc(dve_f.next("lo"), 1)

            def softplus(u, p):
                for c in range(NC):
                    dve.wait_ge(pe_f.sem, pe_f.at(u, "dt01" if c < 2 else "dt2"))
                    dve.wait_ge(act_f.sem, act_f.at(u, "abs1" if c < 2 else "abs2"))
                    src = pair[1][:, c, 0:W] if c < 2 else pair[0][:, 0, 0:W]
                    dve.tensor_scalar(dt[p][:, c, :], src, pf[:, P_DTB + c:P_DTB + c + 1], 0.0, ALU.add, ALU.max).then_inc(dve_f.next(f"sp{c}"), 1)

            def skip(u, p, c):
                dve.wait_ge(pe_s.sem, pe_s.at(u, f"y{NS * (c + 1) - 1}"))
                dve.wait_ge(pe_t.sem, pe_t.at(u - 2, "out"))
                steps = dve_t if c == NC - 1 else dve_s
                dve.scalar_tensor_tensor(y[p][:, c, :], x[p][:, c, :], ps[p][:, P_D + c:P_D + c + 1], bank[3][:, 0:W],
                                         ALU.mult, ALU.add).then_inc(steps.next(f"yd{c}"), 1)

            def scan(u, n):
                dve.wait_ge(act_s.sem, act_s.at(u, f"a{n}"))
                dve.wait_ge(dve_s.sem, dve_s.at(u, f"m{n}"))
                if n % 2 == 0:
                    if n >= NH:
                        dve.wait_ge(pool_s.sem, pool_s.at(u, f"h{n - NH + 1}"))
                    else:
                        dve.wait_ge(pool_s.sem, pool_s.at(u - 1, f"h{STEPS - NH + n + 1}"))
                dve.tensor_tensor_scan(hs[:, n % NH, :], da[:, n % NA, :, :].rearrange("p b l -> p (b l)"),
                                                  dbx(n), 0.0, ALU.mult, ALU.add).then_inc(dve_s.next(f"s{n}"), 1)

            def add_out(u):
                dve.wait_ge(pe_t.sem, pe_t.at(u, "out"))
                t = res[:, tiles_of(u), :].rearrange("p (k t) d -> p k (t d)", k=2)
                dve.tensor_tensor(t, t, pair[1][0:HL, :, 0:2 * D], ALU.add).then_inc(dve_t.next("add"), 1)

            norm_stats(0)
            dve.wait_ge(s_a, 1)
            dve.tensor_scalar(packs[:, :, 0:P_D], packs[:, :, 0:P_D], -1.0, None, ALU.mult).then_inc(s_neg, 1)
            norm_apply(0)
            for k in range(1, TAPS):
                convolve(0, k)
            split_bc(0)
            softplus(0, 0)

            def body(u, p, first, last):
                for n in range(STEPS):
                    if n % NS == 0:
                        c = n // NS
                        if c == 0:
                            dve.wait_ge(pool_f.sem, pool_f.at(u, "dt"))
                            dve.wait_ge(act_f.sem, act_f.at(u, "x"))
                        dve.wait_ge(dve_s.sem, dve_s.at(u if n else u - 1, f"m{(n - 1) % STEPS}"))
                        dve.tensor_tensor(dtx, dt[p][:, c, :], x[p][:, c, :], ALU.mult).then_inc(dve_s.next(f"dtx{c}"), 1)
                        dve.wait_ge(dve_s.sem, dve_s.at(u, f"dtx{c}"))
                    if n < NS and n % 2 == 0:
                        dve.wait_ge(act_f.sem, act_f.at(u, f"bc{n}"))
                    if n >= 3:
                        dve.wait_ge(dve_s.sem, dve_s.at(u, f"s{n - 3}"))
                    else:
                        dve.wait_ge(dve_s.sem, dve_s.at(u - 1, f"s{STEPS - 3 + n}"))
                    dve.tensor_tensor(dbx(n), dtx, bc[p][:, n % NS, :], ALU.mult).then_inc(dve_s.next(f"m{n}"), 1)
                    if n:
                        scan(u, n - 1)
                    if n == DVE_SKIP and not first:
                        skip(u - 1, 1 - p, NC - 1)
                    if n == DVE_ADD and not first:
                        add_out(u - 1)
                    if not last:
                        if n == DVE_STATS:
                            norm_stats(u + 1)
                        if n == DVE_NORM:
                            norm_apply(u + 1)
                        if DVE_CONV <= n < DVE_CONV + TAPS - 1:
                            convolve(u + 1, n - DVE_CONV + 1)
                        if n == DVE_SPLIT:
                            split_bc(u + 1)
                        if n == DVE_SOFT:
                            softplus(u + 1, 1 - p)
                    if n % NS == 4 and n > NS:
                        skip(u, p, n // NS - 1)
                scan(u, STEPS - 1)
                if last:
                    skip(u, p, NC - 1)
                    add_out(u)

            units(dve, body)

        @block.scalar
        def _(act):
            def copy_xt(u):
                act.wait_ge(pool_f.sem, pool_f.at(u, "pf"))
                act.wait_ge(pe_f.sem, pe_f.at(u, "xt"))
                act.wait_ge(pe_f.sem, pe_f.at(u - 1, "in5"))
                for k in range(2):
                    act.activation(xt[:, k, :], pair[0][0:DH2, k, 0:W], ACT.Identity, scale=pf[0:DH2, P_NW + k:P_NW + k + 1],
                                              bias=pf[0:DH2, P_NB + k:P_NB + k + 1]).then_inc(act_f.next(f"xt{k}"), 1)

            def copy_x(u):
                act.wait_ge(pe_f.sem, pe_f.at(u, "in1"))
                act.wait_ge(dve_f.sem, dve_f.at(u - 1, f"c{TAPS - 1}"))
                act.activation(xpad[:, 0:2, :, TAPS - 1:], pair[1][:, :, 0:W].rearrange("p c (b l) -> p c b l", b=GB), ACT.Copy).then_inc(act_f.next("x01"), 1)
                act.wait_ge(pe_f.sem, pe_f.at(u, "in2"))
                act.activation(xpad[:, 2, :, TAPS - 1:], batches(pair[0][:, 0, 0:W]), ACT.Copy).then_inc(act_f.next("x2"), 1)

            def first_tap(u):
                act.wait_ge(pool_f.sem, pool_f.at(u - 1, "dt"))
                act.wait_ge(act_f.sem, act_f.at(u, "x2"))
                for c in range(NC - 1):
                    last = act.activation(batches(conv[:, c, :]), xpad[:, c, :, 0:L], ACT.Identity, scale=pf[:, P_CW + c * TAPS:P_CW + c * TAPS + 1],
                                          bias=pf[:, P_CB + c:P_CB + c + 1])
                last.then_inc(act_f.next("c0"), 1)

            def silus(u, p):
                act.wait_ge(dve_t.sem, dve_t.at(u - 2, "yd2"))
                act.wait_ge(pool_g.sem, pool_g.at(u - 2, "g2"))
                act.wait_ge(pe_f.sem, pe_f.at(u, "in5"))
                act.activation(z[p][:, 0:2, :], pair[1][:, :, 0:W], ACT.Silu).then_inc(act_f.next("z01"), 1)
                act.activation(z[p][:, 2, :], pair[0][:, 1, 0:W], ACT.Silu).then_inc(act_f.next("z2"), 1)
                act.wait_ge(pe_f.sem, pe_f.at(u, "conv"))
                act.activation(x[p][:, NC - 1, :], pair[0][:, 0, 0:W], ACT.Silu, bias=pf[:, P_CB + NC - 1:P_CB + NC]).then_inc(act_f.next("xc"), 1)
                act.wait_ge(dve_f.sem, dve_f.at(u, f"c{TAPS - 1}"))
                act.activation(x[p][:, 0:NC - 1, :], conv[:, 0:NC - 1, :], ACT.Silu).then_inc(act_f.next("x"), 1)

            def high_part(u):
                act.wait_ge(pe_f.sem, pe_f.at(u, "xp"))
                act.wait_ge(pe_f.sem, pe_f.at(u - 1, f"bc{NS - 1}"))
                act.activation(bcs[:], pair[0][:, 0, 0:W], ACT.Copy).then_inc(act_f.next("hi"), 1)
                act.wait_ge(pe_f.sem, pe_f.at(u - 1, "dt2"))
                act.activation(dtr[:], pair[0][0:RANK, 0, 0:W], ACT.Copy).then_inc(act_f.next("dtr"), 1)

            def soft(u):
                act.wait_ge(act_f.sem, act_f.at(u, "x"))
                act.wait_ge(dve_f.sem, dve_f.at(u, "lo"))
                for c in range(NC):
                    act.wait_ge(pe_f.sem, pe_f.at(u, "dt01" if c < 2 else "dt2"))
                    src = pair[1][:, c, 0:W] if c < 2 else pair[0][:, 0, 0:W]
                    act.activation(conv[:, c, :], src, ACT.Abs, bias=pf[:, P_DTB + c:P_DTB + c + 1]).then_inc(act_f.next(f"abs{c}"), 1)
                act.wait_ge(act_f.sem, act_f.at(u, "abs2"))
                act.activation(conv[:], conv[:], ACT.Exp, scale=-1.0).then_inc(act_f.next("exp"), 1)
                act.wait_ge(act_f.sem, act_f.at(u, "exp"))
                act.activation(conv[:], conv[:], ACT.Ln, bias=1.0).then_inc(act_f.next("ln"), 1)

            def copy_bc(u, p, k):
                if k == 0:
                    act.wait_ge(pool_s.sem, pool_s.at(u - 2, f"h{STEPS - 1}"))
                act.wait_ge(pe_f.sem, pe_f.at(u, f"bc{k}"))
                act.activation(bc[p][:, rows_of(k):rows_of(k) + 2, :], pair[(k + 1) % 2][:, :, 0:W], ACT.Copy).then_inc(act_f.next(f"bc{k}"), 1)

            act.wait_ge(s_load, 32)
            act.activation(packs[:, :, 0:P_D], packs[:, :, 0:P_D], ACT.Exp).then_inc(s_a, 1)
            act.wait_ge(s_zero, 1)
            copy_xt(0)
            copy_x(0)
            first_tap(0)
            silus(0, 0)
            high_part(0)
            soft(0)
            for k in range(2):
                copy_bc(0, 0, k)

            def body(u, p, first, last):
                for n in range(STEPS):
                    if n == 0:
                        act.wait_ge(pool_f.sem, pool_f.at(u, "dt"))
                        act.wait_ge(pool_f.sem, pool_f.at(u, "ps"))
                    if first and n < NS - 2:
                        copy_bc(u, p, n + 2)
                    if n in ACT_BC_LATE and not first:
                        copy_bc(u, p, len(ACT_BC) + ACT_BC_LATE.index(n))
                    if n >= NA:
                        act.wait_ge(dve_s.sem, dve_s.at(u, f"s{n - NA}"))
                    else:
                        act.wait_ge(dve_s.sem, dve_s.at(u - 1, f"s{STEPS - NA + n}"))
                    src = batches(dt[p][:, n // NS, :])
                    act.activation(da[:, n % NA, :, 1:L], src[:, :, 1:L], ACT.Exp, scale=ps[p][:, P_A + n:P_A + n + 1]).then_inc(act_s.next(f"a{n}"), 1)
                    if not last:
                        if n == ACT_XT:
                            copy_xt(u + 1)
                        if n == ACT_X:
                            copy_x(u + 1)
                            first_tap(u + 1)
                        if n == ACT_SILU:
                            silus(u + 1, 1 - p)
                        if n == ACT_HI:
                            high_part(u + 1)
                        if n == ACT_SOFT:
                            soft(u + 1)
                        if n in ACT_BC:
                            copy_bc(u + 1, 1 - p, ACT_BC.index(n))

            units(act, body)

        @block.tensor
        def _(pe):
            def transpose_x(u):
                pe.wait_ge(dve_f.sem, dve_f.at(u, "xn"))
                pe.wait_ge(act_f.sem, act_f.at(u - 1, f"bc{NS - 1}"))
                for k in range(2):
                    for t in range(GT):
                        last = pe.transpose(pair[0][0:DH2, k, t * HL:(t + 1) * HL], xn[:, t, k * DH2:(k + 1) * DH2], ident[0:HL, 0:HL])
                last.then_inc(pe_f.next("xt"), 1)

            def project(dst, m):
                for k in range(2):
                    last = pe.matmul(dst, w_in[:, k, m * 128:(m + 1) * 128], xt[:, k, :], start=(k == 0), stop=(k == 1))
                return last

            def project_in(u, step):
                m = (0, 1, 2, NC + 2, NC, NC + 1)[step]
                if step == 0:
                    pe.wait_ge(s_w, (u // 2) * 48 + 48)
                    pe.wait_ge(act_f.sem, act_f.at(u, "xt1"))
                    pe.wait_ge(act_f.sem, act_f.at(u - 1, f"bc{NS - 2}"))
                if step == 4:
                    pe.wait_ge(act_f.sem, act_f.at(u, "x01"))
                last = project(pair[(1, 0, 1)[step // 2]][:, step % 2, 0:W], m)
                last.then_inc(pe_f.next(f"in{step}"), 1)

            def convolve(u):
                pe.wait_ge(act_f.sem, act_f.at(u, "x2"))
                pe.wait_ge(pool_f.sem, pool_f.at(u, "dw"))
                for k in range(TAPS):
                    last = pe.matmul(batches(pair[0][:, 0, 0:W]), diag[:, k, :], xpad[:, NC - 1, :, k:k + L], start=(k == 0), stop=(k == TAPS - 1))
                last.then_inc(pe_f.next("conv"), 1)

            def project_bc(u, p):
                pe.wait_ge(act_f.sem, act_f.at(u, "x"))
                pe.wait_ge(act_f.sem, act_f.at(u, "z2"))
                for c in range(NC):
                    last = pe.matmul(pair[0][:, 0, 0:W], w_x[:, c, :], x[p][:, c, :], start=(c == 0), stop=(c == NC - 1))
                last.then_inc(pe_f.next("xp"), 1)

            def project_dt(u):
                pe.wait_ge(act_f.sem, act_f.at(u, "dtr"))
                pe.wait_ge(dve_t.sem, dve_t.at(u - 2, "add"))
                for c in range(2):
                    last = pe.matmul(pair[1][:, c, 0:W], w_dt[:, c * 128:(c + 1) * 128], dtr[:], start=True, stop=True)
                last.then_inc(pe_f.next("dt01"), 1)
                pe.wait_ge(act_f.sem, act_f.at(u, "hi"))
                pe.wait_ge(dve_f.sem, dve_f.at(u, "rest"))
                pe.matmul(pair[0][:, 0, 0:W], w_dt[:, 2 * 128:3 * 128], dtr[:], start=True, stop=True).then_inc(pe_f.next("dt2"), 1)

            def spread_bc(u, k):
                if k == 0:
                    pe.wait_ge(dve_f.sem, dve_f.at(u, "lo"))
                    pe.wait_ge(dve_f.sem, dve_f.at(u, "sp1"))
                elif k == 1:
                    pe.wait_ge(dve_f.sem, dve_f.at(u, "sp2"))
                else:
                    pe.wait_ge(act_f.sem, act_f.at(u, f"bc{k - 2}"))
                for j in range(2):
                    last = pe.matmul(pair[(k + 1) % 2][:, j, 0:W], spread[:, rows_of(k) + j:rows_of(k) + j + 1].to_broadcast([128, 128]), bcs[:], start=True, stop=True)
                last.then_inc(pe_f.next(f"bc{k}"), 1)

            def sum_states(u, n):
                if n % NS == 0:
                    if n:
                        pe.wait_ge(dve_s.sem, dve_s.at(u, f"yd{n // NS - 1}"))
                    else:
                        pe.wait_ge(dve_t.sem, dve_t.at(u - 1, "yd2"))
                if n % 2 == 0:
                    pe.wait_ge(pool_s.sem, pool_s.at(u, f"h{n + 1}"))
                pe.matmul(bank[3][:, 0:W], ident[:], hc[:, n % NQ, :], start=(n % NS == 0), stop=(n % NS == NS - 1)).then_inc(pe_s.next(f"y{n}"), 1)

            def project_out(u, p, t, last_unit):
                if t == 0:
                    pe.wait_ge(pool_g.sem, pool_g.at(u, f"g{NC - 1}"))
                    pe.wait_ge(s_wo, (u // 2) * 16 + 16)
                    if not last_unit:
                        pe.wait_ge(act_f.sem, act_f.at(u + 2, "z01"))
                for c in range(NC):
                    last = pe.matmul(pair[1][0:HL, t // 2, (t % 2) * D:(t % 2 + 1) * D], y[p][:, c, t * HL:(t + 1) * HL], w_out[:, c, :],
                                     start=(c == 0), stop=(c == NC - 1))
                if t == GT - 1:
                    last.then_inc(pe_t.next("out"), 1)

            pe.wait_ge(s_load, 32)
            transpose_x(0)
            for m in range(2 * NC):
                project_in(0, m)
            convolve(0)
            project_bc(0, 0)
            project_dt(0)
            for k in range(len(PE_BC)):
                spread_bc(0, k)

            def body(u, p, first, last):
                for n in range(STEPS):
                    if n in PE_BC_LATE:
                        spread_bc(u, len(PE_BC) + PE_BC_LATE.index(n))
                    if n in PE_OUT and not first:
                        project_out(u - 1, 1 - p, PE_OUT.index(n), last)
                    if not last:
                        if n == PE_XT:
                            transpose_x(u + 1)
                        if n in PE_IN:
                            project_in(u + 1, PE_IN.index(n))
                        if n == PE_CONV:
                            convolve(u + 1)
                        if n == PE_XP:
                            project_bc(u + 1, 1 - p)
                        if n == PE_DT:
                            project_dt(u + 1)
                        if n in PE_BC:
                            spread_bc(u + 1, PE_BC.index(n))
                    sum_states(u, n)
                if last:
                    for t in range(GT):
                        project_out(u, p, t, True)

            units(pe, body)


def _mamba_arrays(f):
    import numpy as np

    def per_channel(t):
        return t.reshape(NL, NC, 128, -1).transpose(2, 0, 1, 3).reshape(128, NL, -1)

    pack = np.zeros((128, NL, NPACK), np.float32)
    at = 0
    for name in ("A_log", "D_skip", "conv_w", "conv_b", "dt_proj_b"):
        t = per_channel(f["L1_attn_" + name])
        pack[:, :, at:at + t.shape[2]] = t
        at += t.shape[2]
    for name in ("norm_w", "norm_b"):
        pack[:DH2, :, at:at + 2] = f["L1_attn_" + name].reshape(NL, 2, DH2).transpose(2, 0, 1)
        at += 2
    wx = np.zeros((NL, DI, 128), np.float32)
    xp = f["L1_attn_x_proj_w"].transpose(0, 2, 1)
    wx[:, :, :RANK] = xp[:, :, :RANK]
    for k in (32, 64, 96):
        wx[:, :, k:k + 2 * NS] = xp[:, :, RANK:]
    spread = np.zeros((128, 2 * NS), mybir.dt.np(BF16))
    for s in range(2 * NS):
        spread[[32 + s, 64 + s, 96 + s], s] = 1
    return {
        "packs": pack, "spread": spread,
        "w_in": f["L1_attn_in_proj_w"].transpose(0, 2, 1).reshape(NL, 2, DH2, 2 * DI).transpose(0, 2, 1, 3),
        "w_x": wx.reshape(NL, NC, 128, 128).transpose(0, 2, 1, 3),
        "w_dt": f["L1_attn_dt_proj_w"].transpose(0, 2, 1),
        "w_out": f["L1_attn_out_proj_w"].transpose(0, 2, 1).reshape(NL, NC, 128, D).transpose(0, 2, 1, 3),
    }


def _host_arrays(x):
    import numpy as np
    f = {k: np.asarray(v) for k, v in x.items()}
    c = np.ascontiguousarray

    def chunks(w, p):
        return c(w.reshape(-1, p, w.shape[1]).transpose(1, 0, 2))

    img = np.zeros((768, B // 2, PAIR_AT + IMG), np.float32)
    for k in range(2):
        img[:, :, k * PAIR_AT:k * PAIR_AT + IMG] = f["x"].reshape(B, 3, 6, 16, 6, 16).transpose(1, 3, 5, 0, 2, 4).reshape(768, B // 2, 2, IMG)[:, :, k]
    pos = np.arange(L, dtype=np.float32)
    inv = (np.float32(1.0) / np.float32(10000.0) ** (np.arange(0, DH, 2, dtype=np.float32) / np.float32(DH))).astype(np.float32)
    ang = (pos[:, None] * inv[None, :]).astype(np.float32)
    cos = np.concatenate([np.cos(ang), np.cos(ang)], -1)
    sin = np.concatenate([-np.sin(ang), np.sin(ang)], -1)
    scale = np.float32(DH ** -0.5)
    rope = np.stack([np.concatenate([np.tile(t * scale, (1, H)), np.tile(t, (1, H))], 1) for t in (cos, sin)])
    rope = rope.reshape(2, 2, HL, 2 * D).transpose(2, 0, 1, 3).astype(np.float32)
    lat = (np.arange(L) >= CTX).astype(np.float32)
    pad = np.zeros((2, L, H, SW - S_MASK), mybir.dt.np(BF16))
    pad[0, :CTX, :, 0] = -1e30
    pad[1, CTX:, :, 0] = 1
    pad[1, :, :, 1:] = -1
    pad = pad.reshape(2, 2, HL, H, SW - S_MASK).transpose(2, 0, 1, 3, 4)
    widths, ratios = (96, 144, 192), (2, 3, 4)
    rows = np.array([[(np.arange(HID) < r * e) for r in ratios] for e in widths], np.float32)
    cols = np.array([np.arange(D) < e for e in widths], np.float32)
    arrays = {
        "patches": chunks(img.reshape(768, -1), 128).reshape(128, PK, B // 2, PAIR_AT + IMG), "tok_w": chunks(f["L0_tok_W"].T, 128), "tok_b": f["L0_tok_b"][None], "txt": f["txt"],
        "ident": np.eye(128, dtype=np.float32), "ident16": np.eye(HL, dtype=np.float32).astype(mybir.dt.np(BF16)),
        "w_qkv": chunks(np.concatenate([f["L0_attn_Wq"], f["L0_attn_Wkv"]], 1), DH2), "rope": rope, "qk_pad": pad,
        "w_ctx": chunks(f["L0_attn_Wo_ctx"], DH2), "w_lat": chunks(f["L0_attn_Wo_lat"], DH2),
        "b_out": np.stack([f["L0_attn_bo_ctx"], f["L0_attn_bo_lat"]]), "kind": np.stack([1 - lat, lat]),
        "ln_g": f["L0_attn_ln_g"], "ln_b": f["L0_attn_ln_b"],
        "w_up1": chunks(f["L0_ffn_in_weight"].T, DH2), "b_up1": f["L0_ffn_in_bias"].reshape(HM, 128).T,
        "w_down1": chunks(f["L0_ffn_out_weight"], 128),
        "w_up2": chunks(f["L1_ffn_w_fc"].T, DH2), "b_up2": f["L1_ffn_b_fc"].reshape(HM, 128).T,
        "w_down2": chunks(f["L1_ffn_w_proj"].T, 128), "b_down2": f["L1_ffn_b_proj"][None],
        "alpha_e": f["L1_ffn_alpha_e"][:, None], "alpha_r": f["L1_ffn_alpha_r"], "mix_rows": rows, "mix_cols": cols,
        "one3": np.ones((3, 1), np.float32),
        **_mamba_arrays(f),
        "final_w": f["L1_attn_norm_f_w"], "final_b": f["L1_attn_norm_f_b"],
    }
    return {k: c(v) for k, v in arrays.items()}


def kernel(**inputs):
    import concourse.bacc as bacc
    from concourse import mybir
    from concourse.bass_utils import run_bass_kernel_spmd

    arrays = _host_arrays(inputs)
    nc = bacc.Bacc("TRN2", target_bir_lowering=False, num_devices=1)
    aps = {k: nc.dram_tensor("in_" + k, v.shape, mybir.dt.from_np(v.dtype), kind="ExternalInput").ap() for k, v in arrays.items()}
    out = nc.dram_tensor("out", (B, L, D), F32, kind="ExternalOutput").ap()
    build(nc, aps, out)
    r = run_bass_kernel_spmd(nc, [{"in_" + k: v for k, v in arrays.items()}], core_ids=[0])
    return r.results[0]["out"]
```
